# Optimizing a Trainium2 kernel written in Bass

```python
import numpy as np
import jax
import jax.numpy as jnp

def _softmax(x, axis=-1):
    return jax.nn.softmax(x, axis=axis)

def _gelu(x):
    return jax.nn.gelu(x, approximate=True)

def _silu(x):
    return jax.nn.silu(x)

def _sigmoid(x):
    return jax.nn.sigmoid(x)

def _layernorm(x, axis=-1, eps=1e-05):
    m = jnp.mean(x, axis=axis, keepdims=True)
    v = jnp.var(x, axis=axis, keepdims=True)
    return (x - m) / jnp.sqrt(v + eps)

def _scatter_add(tgt, idx, src, axis=0):
    return tgt.at[idx].add(src)

def _segment_sum(src, seg, n):
    return jax.ops.segment_sum(src, seg, n)
kernel_name = 'mk_gnn_resnorm_d4_gnn_r32_d4e048'

def setup_inputs(seed: int=0):
    np.random.seed(seed)
    _w = jnp.asarray

    def _rec_inputs():
        import jax
        import jax.numpy as jnp
        _gk = jax.random.key(seed)
        x = -0.000202 + 1 * jax.random.normal(jax.random.fold_in(_gk, 1), (50000, 64), jnp.float32)
        src = jax.random.randint(jax.random.fold_in(_gk, 2), (50000,), 0, 50000, jnp.int32)
        dst = jnp.minimum((50000 * jax.random.uniform(jax.random.fold_in(_gk, 3), (50000,)) ** 2.0).astype(jnp.int32), 49999)
        _o = jnp.argsort(dst, stable=True)
        src = src[_o]
        dst = dst[_o]
        edge_type_16 = jax.random.randint(jax.random.fold_in(_gk, 13), (50000,), 0, 16, jnp.int32)
        edge_type_200 = jax.random.randint(jax.random.fold_in(_gk, 14), (50000,), 0, 200, jnp.int32)
        return (x, src, dst, edge_type_16, edge_type_200)
    x, src, dst, edge_type_16, edge_type_200 = _rec_inputs()

    def _L0_gnn_setup():
        import jax, jax.numpy as jnp
        import numpy as np
        N_NODES = 3125
        N_EDGES = 31250
        IN_DIM = 64
        OUT_DIM = 64
        key = jax.random.key(seed)
        k1, k2, k3 = jax.random.split(key, 3)
        x = jax.random.normal(k1, (N_NODES, IN_DIM), dtype=jnp.float32)
        edge_index = jax.random.randint(k2, (2, N_EDGES), 0, N_NODES, dtype=jnp.int64)
        W = jax.random.normal(k3, (OUT_DIM, IN_DIM), dtype=jnp.float32) * (1.0 / np.sqrt(IN_DIM))
        b = jnp.zeros((OUT_DIM,), dtype=jnp.float32)
        return {'x': x, 'edge_index': edge_index, 'W': W, 'b': b}
    _L0_gnn_all = _L0_gnn_setup()
    _L0_gnn_in = {k: v for k, v in _L0_gnn_all.items() if k in ('W', 'b')}
    del _L0_gnn_all

    def _L1_gnn_setup():
        import jax, jax.numpy as jnp
        import numpy as np
        N_NODES = 50000
        N_EDGES = 37500
        D_FEAT = 64
        EMBED = 64
        H = 1
        HEAD_DIM = EMBED // H

        def mish(x):
            return x * jnp.tanh(jax.nn.softplus(x))
        key = jax.random.key(seed)
        ks = jax.random.split(key, 12)
        nodes = jax.random.normal(ks[0], (N_NODES, D_FEAT), dtype=jnp.float32)
        senders = jax.random.randint(ks[1], (N_EDGES,), 0, N_NODES, dtype=jnp.int32)
        receivers = jax.random.randint(ks[2], (N_EDGES,), 0, N_NODES, dtype=jnp.int32)
        s = 0.05
        We_k = jax.random.normal(ks[3], (D_FEAT, H, HEAD_DIM), dtype=jnp.float32) * s
        We_b = jnp.zeros((H, HEAD_DIM), dtype=jnp.float32)
        Ws_k = jax.random.normal(ks[4], (HEAD_DIM, EMBED), dtype=jnp.float32) * s
        Ws_b = jnp.zeros((EMBED,), dtype=jnp.float32)
        Wr_k = jax.random.normal(ks[5], (D_FEAT, H, HEAD_DIM), dtype=jnp.float32) * s
        Wr_b = jnp.zeros((H, HEAD_DIM), dtype=jnp.float32)
        Wa_k = jax.random.normal(ks[6], (EMBED, 1), dtype=jnp.float32) * s
        Wa_b = jnp.zeros((1,), dtype=jnp.float32)
        return {'nodes': nodes, 'senders': senders, 'receivers': receivers, 'We_k': We_k, 'We_b': We_b, 'Ws_k': Ws_k, 'Ws_b': Ws_b, 'Wr_k': Wr_k, 'Wr_b': Wr_b, 'Wa_k': Wa_k, 'Wa_b': Wa_b}
    _L1_gnn_all = _L1_gnn_setup()
    _L1_gnn_in = {k: v for k, v in _L1_gnn_all.items() if k in ('We_k', 'We_b', 'Ws_k', 'Ws_b', 'Wr_k', 'Wr_b', 'Wa_k', 'Wa_b')}
    del _L1_gnn_all

    def _L2_gnn_setup():
        import jax, jax.numpy as jnp
        import numpy as np
        N_NODES = 3125
        N_EDGES = 31250
        D_IN = 64
        D_OUT = 64
        N_RELS = 16
        key = jax.random.key(seed)
        k1, k2, k3, k4, k5 = jax.random.split(key, 5)
        feat = jax.random.normal(k1, (N_NODES, D_IN), dtype=jnp.float32)
        weight = jax.random.normal(k2, (N_RELS, D_IN, D_OUT), dtype=jnp.float32) * 0.05
        src = jax.random.randint(k3, (N_EDGES,), 0, N_NODES)
        dst = jax.random.randint(k4, (N_EDGES,), 0, N_NODES)
        etypes = jax.random.randint(k5, (N_EDGES,), 0, N_RELS)
        return {'feat': feat, 'weight': weight, 'src': src, 'dst': dst, 'etypes': etypes}
    _L2_gnn_all = _L2_gnn_setup()
    _L2_gnn_in = {k: v for k, v in _L2_gnn_all.items() if k in ('weight',)}
    del _L2_gnn_all

    def _L3_gnn_setup():
        import jax, jax.numpy as jnp
        import numpy as np
        N, E, D, RD, NUM_RELS = (3125, 31250, 64, 64, 200)
        NEG_SLOPE = 0.2
        key = jax.random.key(seed)
        ks = jax.random.split(key, 8)
        H = jax.random.normal(ks[0], (N, D), dtype=jnp.float32)
        src = jax.random.randint(ks[1], (E,), 0, N, dtype=jnp.int32)
        dst = jax.random.randint(ks[2], (E,), 0, N, dtype=jnp.int32)
        rel = jax.random.randint(ks[3], (E,), 0, NUM_RELS, dtype=jnp.int32)

        def xavier(k, shape):
            fan_in, fan_out = (shape[1], shape[0])
            lim = float(np.sqrt(6.0 / (fan_in + fan_out)))
            return jax.random.uniform(k, shape, jnp.float32, -lim, lim)
        W_node = xavier(ks[4], (D, D))
        W_rel = xavier(ks[5], (D, RD))
        attvec = xavier(ks[6], (1, 3 * D))
        rel_emb = xavier(ks[7], (NUM_RELS, RD))
        return {'H': H, 'W_node': W_node, 'W_rel': W_rel, 'attvec': attvec, 'rel_emb': rel_emb, 'src': src, 'dst': dst, 'rel': rel, 'num_nodes': N}
    _L3_gnn_all = _L3_gnn_setup()
    _L3_gnn_in = {k: v for k, v in _L3_gnn_all.items() if k in ('W_node', 'W_rel', 'attvec', 'rel_emb')}
    del _L3_gnn_all
    return {'x': x, 'src': src, 'dst': dst, 'edge_type_16': edge_type_16, 'edge_type_200': edge_type_200, 'L0_gnn_W': _L0_gnn_in['W'], 'L0_gnn_b': _L0_gnn_in['b'], 'L1_gnn_We_k': _L1_gnn_in['We_k'], 'L1_gnn_We_b': _L1_gnn_in['We_b'], 'L1_gnn_Ws_k': _L1_gnn_in['Ws_k'], 'L1_gnn_Ws_b': _L1_gnn_in['Ws_b'], 'L1_gnn_Wr_k': _L1_gnn_in['Wr_k'], 'L1_gnn_Wr_b': _L1_gnn_in['Wr_b'], 'L1_gnn_Wa_k': _L1_gnn_in['Wa_k'], 'L1_gnn_Wa_b': _L1_gnn_in['Wa_b'], 'L2_gnn_weight': _L2_gnn_in['weight'], 'L3_gnn_W_node': _L3_gnn_in['W_node'], 'L3_gnn_W_rel': _L3_gnn_in['W_rel'], 'L3_gnn_attvec': _L3_gnn_in['attvec'], 'L3_gnn_rel_emb': _L3_gnn_in['rel_emb']}

def reference(x, src, dst, edge_type_16, edge_type_200, L0_gnn_W, L0_gnn_b, L1_gnn_We_k, L1_gnn_We_b, L1_gnn_Ws_k, L1_gnn_Ws_b, L1_gnn_Wr_k, L1_gnn_Wr_b, L1_gnn_Wa_k, L1_gnn_Wa_b, L2_gnn_weight, L3_gnn_W_node, L3_gnn_W_rel, L3_gnn_attvec, L3_gnn_rel_emb):
    import jax
    import jax.numpy as jnp

    def _L0_gnn_ref(x, edge_index, W, b):
        import jax, jax.numpy as jnp
        import numpy as np
        N_NODES = 3125
        N_EDGES = 31250
        IN_DIM = 64
        OUT_DIM = 64
        N = x.shape[0]
        loop = jnp.arange(N, dtype=edge_index.dtype)
        src = jnp.concatenate([edge_index[0], loop])
        dst = jnp.concatenate([edge_index[1], loop])
        deg = jax.ops.segment_sum(jnp.ones_like(dst, dtype=x.dtype), dst, num_segments=N)
        dinv = jnp.where(deg > 0, jax.lax.rsqrt(deg), 0.0)
        norm = dinv[src] * dinv[dst]
        h = x @ W.T
        msg = h[src] * norm[:, None]
        out = jax.ops.segment_sum(msg, dst, num_segments=N)
        return out + b

    def _L1_gnn_ref(nodes, senders, receivers, We_k, We_b, Ws_k, Ws_b, Wr_k, Wr_b, Wa_k, Wa_b):
        import jax, jax.numpy as jnp
        import numpy as np
        N_NODES = 50000
        N_EDGES = 37500
        D_FEAT = 64
        EMBED = 64
        H = 1
        HEAD_DIM = EMBED // H

        def mish(x):
            return x * jnp.tanh(jax.nn.softplus(x))
        n = nodes.shape[0]
        sent = nodes[senders]
        edges = jnp.einsum('ef,fhd->ehd', sent, We_k) + We_b
        recv = nodes[receivers]
        s_att = jnp.einsum('ehd,dm->ehm', edges, Ws_k) + Ws_b
        r_att = jnp.einsum('ef,fhd->ehd', recv, Wr_k) + Wr_b
        x = mish(s_att + r_att)
        logits = jnp.einsum('ehm,mo->eho', x, Wa_k) + Wa_b
        seg_max = jax.ops.segment_max(logits, receivers, num_segments=n)
        seg_max = jnp.where(jnp.isfinite(seg_max), seg_max, 0.0)
        unnorm = jnp.exp(logits - seg_max[receivers])
        denom = jax.ops.segment_sum(unnorm, receivers, num_segments=n)
        weights = unnorm / denom[receivers]
        msg = (weights * edges).reshape(edges.shape[0], H * HEAD_DIM)
        out_nodes = jax.ops.segment_sum(msg, receivers, num_segments=n)
        return out_nodes

    def _L2_gnn_ref(feat, weight, src, dst, etypes):
        import jax, jax.numpy as jnp
        import numpy as np
        N_NODES = 3125
        N_EDGES = 31250
        D_IN = 64
        D_OUT = 64
        N_RELS = 16
        h = feat[src]
        n_rels = weight.shape[0]
        e, d_out = (h.shape[0], weight.shape[2])

        def step(m, rw):
            r, w_r = rw
            mask = jnp.where(etypes == r, 1.0, 0.0).astype(h.dtype)
            m = m + mask[:, None] * (h @ w_r)
            return (m, None)
        m0 = jnp.zeros((e, d_out), dtype=h.dtype)
        m, _ = jax.lax.scan(step, m0, (jnp.arange(n_rels), weight))
        out = jax.ops.segment_sum(m, dst, num_segments=feat.shape[0])
        return out

    def _L3_gnn_ref(H, W_node, W_rel, attvec, rel_emb, src, dst, rel, num_nodes):
        import jax, jax.numpy as jnp
        import numpy as np
        N, E, D, RD, NUM_RELS = (3125, 31250, 64, 64, 200)
        NEG_SLOPE = 0.2
        Wh = H @ W_node.T
        Wr = rel_emb[rel] @ W_rel.T
        h_i = Wh[src]
        h_j = Wh[dst]
        a = attvec[0]
        e_ij = h_i @ a[:D] + h_j @ a[D:2 * D] + Wr @ a[2 * D:]
        e_ij = jax.nn.leaky_relu(e_ij, NEG_SLOPE)
        e_max = jax.ops.segment_max(e_ij, src, num_segments=num_nodes)
        alpha_num = jnp.exp(e_ij - e_max[src])
        denom = jax.ops.segment_sum(alpha_num, src, num_segments=num_nodes) + 1e-12
        alpha = alpha_num / denom[src]
        msg = h_j + Wr
        H_out = jax.ops.segment_sum(alpha[:, None] * msg, src, num_segments=num_nodes)
        return H_out
    edge_index = jnp.stack([src, dst])
    x = _layernorm(x + _L0_gnn_ref(x, edge_index, L0_gnn_W, L0_gnn_b), axis=-1)
    x = _layernorm(x + _L1_gnn_ref(x, src, dst, L1_gnn_We_k, L1_gnn_We_b, L1_gnn_Ws_k, L1_gnn_Ws_b, L1_gnn_Wr_k, L1_gnn_Wr_b, L1_gnn_Wa_k, L1_gnn_Wa_b), axis=-1)
    x = _layernorm(x + _L2_gnn_ref(x, L2_gnn_weight, src, dst, edge_type_16), axis=-1)
    x = _layernorm(x + _L3_gnn_ref(x, L3_gnn_W_node, L3_gnn_W_rel, L3_gnn_attvec, L3_gnn_rel_emb, src, dst, edge_type_200, 50000), axis=-1)
    return x

_drawn_inputs = setup_inputs


def setup_inputs(seed=0):
    import zlib

    import numpy as np

    out = dict(_drawn_inputs(seed))
    spreads = {'L0_gnn_b': (0.0, 0.1),
     'L1_gnn_We_b': (0.0, 0.1),
     'L1_gnn_Ws_b': (0.0, 0.8),
     'L1_gnn_Wr_b': (0.0, 0.8)}
    factors = {'L1_gnn_Ws_k': 8.0, 'L1_gnn_Wr_k': 8.0, 'L1_gnn_Wa_k': 8.0}
    for name, (base, spread) in spreads.items():
        noise = np.random.default_rng([zlib.crc32(name.encode()), seed]).standard_normal(out[name].shape)
        drawn = base * np.exp(spread * noise) if base else spread * noise
        out[name] = jnp.asarray(drawn.astype(out[name].dtype))
    for name, factor in factors.items():
        out[name] = (out[name] * factor).astype(out[name].dtype)
    return out
```

```python
from contextlib import ExitStack

import numpy as np

import concourse.bass as bass
from concourse import mybir

ALU = mybir.AluOpType
ACT = mybir.ActivationFunctionType
AX_X = mybir.AxisListType.X
F32 = mybir.dt.float32
BF16 = mybir.dt.bfloat16
I32 = mybir.dt.int32

P = 128
D = 64
N_NODES = 50000
N_EDGES = 50000
TILES = 392
PAD = TILES * P
PAD_KEY = PAD - 1
G = 4
NG = TILES // G
PAIRS = NG // 2
E = G * P
LO = 256
HI = PAD // LO
HH = HI // 2
QA = TILES // 4
N_REL = 16
RELS = 200
RH = RELS // 2
NEG = -1.0e30
SKIP = 65536
EPS = 1e-5
SRC, DST, T16, T200 = range(4)
J = 28
NCH = TILES // J

assert PAD == HI * LO and TILES % (2 * G) == 0 and NCH % 2 == 0


class Net:
    pass


def phase(nc, name):
    ctx = ExitStack()
    sems = []

    def clear():
        nc.clear_and_free_semaphores(sems)
        nc.all_engine_barrier()

    ctx.callback(clear)

    def sb(n, shape, dt=F32):
        return ctx.enter_context(nc.sbuf_tensor(f"{name}_{n}", shape, dt))

    def ps(n, shape, dt=F32):
        return ctx.enter_context(nc.psum_tensor(f"{name}_{n}", shape, dt))

    def sem(n):
        sems.append(nc.alloc_semaphore(f"{name}_{n}"))
        return sems[-1]

    return ctx, sb, ps, sem


def linker(eng, sem, base):
    count = [0]

    def link(ins):
        count[0] += 1
        ins.then_inc(sem, 1)
        eng.wait_ge(sem, base + count[0])

    return link


def pipelined(eng, stages):
    def pair(i, begun):
        for s in range(2):
            for stage, lag in stages:
                turn = i + (s - lag) // 2
                if begun or 0 <= turn < PAIRS:
                    stage((s - lag) % 2, turn)

    peeled = 1 - min((0 - lag) // 2 for _, lag in stages)
    for i in range(peeled):
        pair(i, False)
    with eng.Fori(peeled, PAIRS) as i:
        pair(i, True)
    for i in range(PAIRS, PAIRS + peeled - 1):
        pair(i, False)


def again(turn):
    return not (isinstance(turn, int) and turn == 0)


def tiles_on_partitions(ap):
    return ap.rearrange("(q a c) -> a q c", q=4, c=P)


def load_phase(nc, n, x, edge_fields):
    ctx, sb, ps, sem = phase(nc, "load")
    with ctx:
        iota_i = sb("iota_i", [P, LO], I32)
        part_i = sb("part_i", [P, 1], I32)
        half = sb("half", [P, 1])
        raw = sb("raw", [QA, 4, 4, P], I32)
        rawf = sb("rawf", [QA, 4, 4, P])
        digit_i = sb("digit_i", [P, 2, 2, TILES], I32)
        zeros = sb("zeros", [P, 14 * D * 4])
        minus = sb("minus", [1, 4], I32)
        turned = ps("turned", [P, 4, 512])

        pads_set = sem("pads_set")
        pool_step = sem("pool_step")
        consts_made = sem("consts_made")
        edges_in = sem("edges_in")
        floats_made = sem("floats_made")
        fields_turned = sem("fields_turned")
        payload_made = sem("payload_made")
        dve_step = sem("dve_step")
        zeros_set = sem("zeros_set")
        filled = sem("filled")

        block = ctx.enter_context(nc.Block())

        @block.gpsimd
        def _(pool):
            nc.gpsimd.memset(minus[:], -1).then_inc(zeros_set, 1)
            nc.gpsimd.memset(n.ident[:], 0.0).then_inc(pool_step, 1)
            nc.gpsimd.memset(n.before[:], 1.0).then_inc(pool_step, 1)
            nc.gpsimd.memset(n.lower[:], 1.0).then_inc(pool_step, 1)
            nc.gpsimd.memset(n.ones[:], 1.0).then_inc(consts_made, 1)
            pool.wait_ge(pool_step, 3)
            nc.gpsimd.affine_select(out=n.ident[:], in_=n.ident[:], compare_op=ALU.not_equal, fill=1.0,
                                    base=0, pattern=[[-1, P]], channel_multiplier=1).then_inc(consts_made, 1)
            nc.gpsimd.affine_select(out=n.before[:, E - P:E], in_=n.before[:, E - P:E], compare_op=ALU.is_gt,
                                    fill=0.0, base=0, pattern=[[-1, P]], channel_multiplier=1).then_inc(consts_made, 1)
            nc.gpsimd.affine_select(out=n.lower[:], in_=n.lower[:], compare_op=ALU.is_gt,
                                    fill=0.0, base=0, pattern=[[1, HH]], channel_multiplier=-1).then_inc(consts_made, 1)
            nc.gpsimd.iota(iota_i[:], pattern=[[1, LO]], base=0, channel_multiplier=0).then_inc(consts_made, 1)
            nc.gpsimd.iota(part_i[:], pattern=[[1, 1]], base=0, channel_multiplier=1).then_inc(consts_made, 1)

        @block.sync
        def _(sp):
            sp.wait_ge(pads_set, 2)
            whole = 3 * QA * P
            for f, a in enumerate(edge_fields):
                sp.dma_start(raw[:, f, 0:3, :], a[0:whole].rearrange("(q a c) -> a q c", q=3, c=P)).then_inc(edges_in, 16)
                rows = (N_EDGES - whole) // P
                rest = whole + rows * P
                sp.dma_start(raw[0:rows, f, 3, :], a[whole:rest].rearrange("(a c) -> a c", c=P)).then_inc(edges_in, 16)
                sp.dma_start(raw[rows:rows + 1, f, 3, 0:N_EDGES - rest],
                             a[rest:N_EDGES].rearrange("(a c) -> a c", a=1)).then_inc(edges_in, 16)
            split = lambda t: t.rearrange("(p r) d -> p (r d)", p=400)
            sp.dma_start(split(n.xpad[0:N_NODES, :]), split(x)).then_inc(filled, 16)
            sp.wait_ge(zeros_set, 2)
            pad_rows = PAD - N_NODES
            sp.dma_start(n.xpad[N_NODES:PAD, :].rearrange("(p r) d -> p (r d)", r=2),
                         zeros[0:pad_rows // 2, 0:2 * D]).then_inc(filled, 16)
            for table in (n.agg_dst, n.agg_src):
                view = table.rearrange("(p c r) d -> c p (r d)", p=P, c=7)
                for c in range(7):
                    sp.dma_start(view[c], zeros[:]).then_inc(filled, 16)
            for table in (n.sorted_dst, n.sorted_src):
                sp.dma_start(table[0:1, :], minus[:]).then_inc(filled, 16)
                sp.dma_start(table[PAD + 1:PAD + 2, :], minus[:]).then_inc(filled, 16)
            sp.wait_ge(filled, 16 * (2 + 14 + 4))

        @block.tensor
        def _(pe):
            pe.wait_ge(floats_made, 1)
            pe.wait_ge(consts_made, 6)
            for f in range(4):
                for q in range(4):
                    mm = pe.transpose(turned[:, f, q * QA:(q + 1) * QA], rawf[:, f, q, :], n.ident[0:QA, 0:QA])
                mm.then_inc(fields_turned, 1)

        @block.scalar
        def _(act):
            for f in range(4):
                act.wait_ge(fields_turned, f + 1)
                nc.scalar.copy(n.payload[:, :, f], turned[:, f, 0:TILES]).then_inc(payload_made, 1)

        @block.vector
        def _(dve):
            link = linker(dve, dve_step, 0)
            nc.vector.memset(raw[96:QA, SRC:DST + 1, 3, :], PAD_KEY).then_inc(pads_set, 1)
            nc.vector.memset(raw[96:QA, T16:T200 + 1, 3, :], 0).then_inc(pads_set, 1)
            nc.vector.memset(zeros[:], 0.0).then_inc(zeros_set, 1)
            dve.wait_ge(edges_in, 16 * 12)
            nc.vector.tensor_copy(rawf[:], raw[:]).then_inc(floats_made, 1)
            dve.wait_ge(consts_made, 6)
            link(nc.vector.tensor_copy(n.ident_b[:], n.ident[:]))
            link(nc.vector.tensor_copy(n.iota_lo[:], iota_i[:]))
            link(nc.vector.tensor_copy(n.part[:, 0:1], part_i[:]))
            link(nc.vector.tensor_scalar(n.part[:, 1:2], n.part[:, 0:1], float(RH), None, ALU.add))
            link(nc.vector.tensor_scalar(half[:], n.part[:, 0:1], float(D), None, ALU.is_ge))
            for j in range(N_REL // 2):
                link(nc.vector.tensor_scalar(n.relid[:, j:j + 1], half[:], float(2 * j), None, ALU.add))
            dve.wait_ge(payload_made, 4)
            for k in (SRC, DST):
                link(nc.vector.tensor_scalar(digit_i[:, k, 0, :], n.payload[:, :, k], 8, None, ALU.logical_shift_right))
                link(nc.vector.tensor_scalar(digit_i[:, k, 1, :], n.payload[:, :, k], LO - 1, None, ALU.bitwise_and))
                link(nc.vector.tensor_copy(n.hi[:, k, :], digit_i[:, k, 0, :]))
                link(nc.vector.tensor_copy(n.lo[:, k, :], digit_i[:, k, 1, :]))
                link(nc.vector.tensor_scalar(n.hi256[:, k, :], n.hi[:, k, :], float(LO), None, ALU.mult))
                link(nc.vector.tensor_copy(n.keyf[:, k, :], n.payload[:, :, k]))


def one_hots(nc, n, k, g, lo_hot, hi_hot):
    nc.vector.tensor_tensor(lo_hot, n.iota_lo[:].unsqueeze(1).broadcast_to([P, G, LO]),
                            n.lo[:, k, bass.ds(g * G, G)].unsqueeze(2).broadcast_to([P, G, LO]), ALU.is_equal)
    return nc.vector.tensor_tensor(hi_hot, n.iota_lo[:, 0:HI].unsqueeze(1).broadcast_to([P, G, HI]),
                                   n.hi[:, k, bass.ds(g * G, G)].unsqueeze(2).broadcast_to([P, G, HI]), ALU.is_equal)


def histogram_phase(nc, n):
    ctx, sb, ps, sem = phase(nc, "hist")
    with ctx:
        lo_hot = sb("lo_hot", [P, 2, G, LO], BF16)
        hi_hot = sb("hi_hot", [P, 2, G, HI], BF16)
        counts = sb("counts", [HH, 2, 2, LO])
        upto = sb("upto", [HH, 2, 2, LO])
        total = sb("total", [HH, 2, 2])
        excl = sb("excl", [HH, 2, 2, LO])
        hist = [ps(f"hist{k}", [HH, 2, LO]) for k in range(2)]
        offset = ps("offset", [HH, 2, 2])

        hots_made = sem("hots_made")
        hots_used = sem("hots_used")
        counts_made = sem("counts_made")
        totals_made = sem("totals_made")
        offsets_made = sem("offsets_made")
        dve_step = sem("dve_step")
        stored = sem("stored")

        block = ctx.enter_context(nc.Block())

        @block.vector
        def _(dve):
            def group(g, first):
                for k in (SRC, DST):
                    if not first:
                        dve.wait_ge(hots_used, 2 * g + k - 1)
                    one_hots(nc, n, k, g, lo_hot[:, k], hi_hot[:, k]).then_inc(hots_made, 1)

            group(0, True)
            with dve.Fori(1, NG) as g:
                group(g, False)
            dve.wait_ge(hots_used, 2 * NG)
            link = linker(dve, dve_step, 0)
            for k in (SRC, DST):
                nc.vector.tensor_copy(counts[:, k], hist[k][:]).then_inc(counts_made, 1)
            dve.wait_ge(counts_made, 2)
            for k in (SRC, DST):
                for h in range(2):
                    link(nc.vector.tensor_tensor_scan(upto[:, k, h], n.ones[0:HH, 0:LO], counts[:, k, h], 0.0,
                                                      ALU.mult, ALU.add))
                link(nc.vector.tensor_copy(total[:, k, :], upto[:, k, :, LO - 1]))
                link(nc.vector.tensor_tensor(excl[:, k], upto[:, k], counts[:, k], ALU.subtract))
            nc.vector.tensor_copy(total[:, 0, :], total[:, 0, :]).then_inc(totals_made, 1)
            dve.wait_ge(offsets_made, 1)
            for k in (SRC, DST):
                for h in range(2):
                    link(nc.vector.tensor_scalar(n.start[:, k, h], excl[:, k, h], offset[:, k, h:h + 1], None, ALU.add))

        @block.tensor
        def _(pe):
            def group(g, first):
                for k in (SRC, DST):
                    pe.wait_ge(hots_made, 2 * g + k + 1)
                    for t in range(G):
                        for h in range(2):
                            mm = pe.matmul(hist[k][:, h, :], lhsT=hi_hot[:, k, t, h * HH:(h + 1) * HH],
                                           rhs=lo_hot[:, k, t, :], start=first and t == 0 and h == 0,
                                           stop=False, skip_group_check=True)
                    mm.then_inc(hots_used, 1)

            group(0, True)
            with pe.Fori(1, NG) as g:
                group(g, False)
            pe.wait_ge(totals_made, 1)
            for k in (SRC, DST):
                pe.matmul(offset[:, k, 0:1], lhsT=n.lower[0:HH, :], rhs=total[:, k, 0:1], start=True, stop=True)
                pe.matmul(offset[:, k, 1:2], lhsT=n.lower[0:HH, :], rhs=total[:, k, 1:2], start=True, stop=False)
                mm = pe.matmul(offset[:, k, 1:2], lhsT=n.ones[0:HH, 0:HH], rhs=total[:, k, 0:1], start=False, stop=True)
            mm.then_inc(offsets_made, 1)

        @block.sync
        def _(sp):
            sp.wait_ge(counts_made, 2)
            sp.dma_start(n.degree.rearrange("(h p l) -> p h l", h=2, l=LO), counts[:, DST]).then_inc(stored, 16)
            sp.wait_ge(stored, 16)


def sort_phase(nc, n, k, table, name):
    ctx, sb, ps, sem = phase(nc, name)
    with ctx:
        lo_hot = sb("lo_hot", [P, 2, G, LO], BF16)
        hi_hot = sb("hi_hot", [P, 2, G, HI], BF16)
        hi_turned = sb("hi_turned", [HH, 2, 2 * G, P])
        next_free = sb("next_free", [HH, 2, 2, LO])
        picked = sb("picked", [P, G, LO])
        matched = sb("matched", [P, G, E])
        base = sb("base", [P, 2, G])
        rank = sb("rank", [P, 2, G])
        place = sb("place", [P, 2, G], I32)
        moved = sb("moved", [P, 2, G, 4], I32)
        running = ps("running", [HH, 2, LO])
        turned = [ps(f"turned{s}", [HH, 2 * G, P], BF16) for s in range(2)]
        keys = [ps(f"keys{s}", [P, G, P]) for s in range(2)]
        found = ps("found", [P, G, LO])

        hots_made = sem("hots_made")
        turns_made = sem("turns_made")
        turns_copied = sem("turns_copied")
        free_copied = sem("free_copied")
        found_made = sem("found_made")
        updated = sem("updated")
        picks_made = sem("picks_made")
        places_made = sem("places_made")
        payload_staged = sem("payload_staged")
        scatter_begun = sem("scatter_begun")
        scattered = [sem(f"scattered{s}") for s in range(2)]

        block = ctx.enter_context(nc.Block())

        @block.vector
        def _(dve):
            def hots(s, t):
                g = 2 * t + s
                if again(t):
                    dve.wait_ge(updated, g)
                one_hots(nc, n, k, g, lo_hot[:, s], hi_hot[:, s]).then_inc(hots_made, 1)

            def places(s, t):
                g = 2 * t + s
                dve.wait_ge(found_made, g + 1)
                if again(t):
                    dve.wait_ge(scattered[s], 64 * t)
                for c in range(G):
                    nc.vector.tensor_tensor_reduce(picked[:, c], found[:, c], lo_hot[:, s, c], 1.0, 0.0,
                                                   ALU.mult, ALU.add, base[:, s, c:c + 1])
                    last = nc.vector.scalar_tensor_tensor(
                        matched[:, c, 0:(c + 1) * P], keys[s][:, 0:c + 1, :].rearrange("p c e -> p (c e)"),
                        n.keyf[:, k, bass.ds(g * G + c, 1)], n.before[:, (G - 1 - c) * P:E],
                        ALU.is_equal, ALU.mult, accum_out=rank[:, s, c:c + 1])
                last.then_inc(picks_made, 1)
                dve.wait_ge(picks_made, g + 1)
                nc.vector.scalar_tensor_tensor(place[:, s], base[:, s], 1.0, rank[:, s],
                                               ALU.add, ALU.add).then_inc(places_made, 1)

            pipelined(dve, [(hots, 0), (places, 1)])

        @block.tensor
        def _(pe):
            def turns(s, t):
                g = 2 * t + s
                pe.wait_ge(hots_made, g + 1)
                if again(t):
                    pe.wait_ge(turns_copied, g - 1)
                    pe.wait_ge(places_made, g - 1)
                for c in range(G):
                    for h in range(2):
                        mm = pe.transpose(turned[s][:, 2 * c + h, :], hi_hot[:, s, c, h * HH:(h + 1) * HH], n.ident_b[:])
                mm.then_inc(turns_made, 1)
                for c in range(G):
                    col = bass.ds(g * G + c, 1)
                    pe.matmul(keys[s][:, c, :], lhsT=n.hi256[:, k, col].broadcast_to([P, P]), rhs=n.ident_b[:],
                              start=True, stop=False)
                    pe.matmul(keys[s][:, c, :], lhsT=n.lo[:, k, col].broadcast_to([P, P]), rhs=n.ident_b[:],
                              start=False, stop=True)

            def lookups(s, t):
                g = 2 * t + s
                pe.wait_ge(turns_copied, g + 1)
                pe.wait_ge(free_copied, g + 1)
                if not (again(t) is False and s == 0):
                    pe.wait_ge(places_made, g)
                for c in range(G):
                    for h in range(2):
                        mm = pe.matmul(found[:, c, :], lhsT=hi_turned[:, s, 2 * c + h, :], rhs=next_free[:, s, h, :],
                                       start=(h == 0), stop=(h == 1))
                mm.then_inc(found_made, 1)
                for c in range(G):
                    for h in range(2):
                        mm = pe.matmul(running[:, h, :], lhsT=hi_hot[:, s, c, h * HH:(h + 1) * HH],
                                       rhs=lo_hot[:, s, c, :], start=False, stop=False, skip_group_check=True)
                mm.then_inc(updated, 1)

            for h in range(2):
                mm = pe.matmul(running[:, h, :], lhsT=n.ident[0:HH, 0:HH], rhs=n.start[:, k, h, :],
                               start=(h == 0), stop=False, skip_group_check=True)
            mm.then_inc(updated, 1)
            pipelined(pe, [(turns, 0), (lookups, 1)])

        @block.scalar
        def _(act):
            def copies(s, t):
                g = 2 * t + s
                act.wait_ge(turns_made, g + 1)
                if again(t):
                    act.wait_ge(found_made, g - 1)
                nc.scalar.copy(hi_turned[:, s], turned[s][:]).then_inc(turns_copied, 1)

            def free(s, t):
                g = 2 * t + s
                act.wait_ge(updated, g + 1)
                nc.scalar.copy(next_free[:, s], running[:]).then_inc(free_copied, 1)
                if again(t):
                    act.wait_ge(scattered[s], 64 * t)
                nc.scalar.copy(moved[:, s], n.payload[:, bass.ds(g * G, G), :]).then_inc(payload_staged, 1)

            pipelined(act, [(copies, 0), (free, 1)])

        @block.gpsimd
        def _(pool):
            last_row = pool.to_reg(PAD + 1)

            def scatter(s, t):
                g = 2 * t + s
                pool.wait_ge(places_made, g + 1)
                pool.wait_ge(payload_staged, g + 1)
                pool.sem_inc(scatter_begun, 1)
                for c in range(G):
                    pool.indirect_dma_start(out=table, out_offset=bass.IndirectOffsetOnAxis(ap=place[:, s, c:c + 1], axis=0),
                                            in_=moved[:, s, c, :], in_offset=None,
                                            bounds_check=last_row, oob_is_err=False).then_inc(scattered[s], 16)

            pipelined(pool, [(scatter, 0)])
            for s in range(2):
                pool.wait_ge(scattered[s], 64 * PAIRS)


def edge_phase(nc, n, kind, rows, agg, name):
    A = D + 1
    soft = kind in ("gat", "att")
    ends = 2 if soft else 1
    wide = P if kind != "sum" else D
    order, marks = (n.cols_src, n.marks_src) if kind == "att" else (n.cols_dst, n.marks_dst)
    SRC_COL, KEY_COL = 0, 1
    F = A if soft else D
    LATE = 3 if kind == "rel" else 2

    ctx, sb, ps, sem = phase(nc, name)
    with ctx:
        gcol = sb("gcol", [P, 2, 2, G], I32)
        scol = sb("scol", [P, 2, G], I32)
        mark = sb("mark", [P, 2, 3, G], BF16)
        got = sb("got", [P, 2, G, ends * D])
        feat = sb("feat", [wide, 2, E])
        state = sb("state", [F, 2, E])
        outs = sb("outs", [P, 2, G, D])
        turned = [ps(f"turned{s}", [ends * D, G, P]) for s in range(2)]
        keep = ps("keep", [F, G, P])
        back = ps("back", [P, G, A if soft else D])
        if kind != "sum":
            keep_s = sb("keep_s", [F, 2, E])
        if kind in ("rel", "att"):
            types = ps("types", [P, G, P])
            msg = [ps(f"msg{s}", [D, E]) for s in range(2)]
        if kind == "rel":
            masked = sb("masked", [P, 2, N_REL // 2, E])
        if kind == "att":
            hot = sb("hot", [RH, 2, 2, E])
            raw_score = sb("raw_score", [A, E])
            score = sb("score", [A, 2, E])
        if kind == "gat":
            pre = ps("pre", [P, G, D])
            z = sb("z", [P, 2, G, D])
            clamped = sb("clamped", [P, 2, G, D])
            u = sb("u", [P, 2, G, D])
            t2 = sb("t2", [P, G, D])
            den = sb("den", [P, G, D])
            mish = sb("mish", [P, 2, G, D])
            logit = sb("logit", [P, 2, G])
        if soft:
            score_p = ps("score_p", [A, G, P])
            top = sb("top", [A, 2, E + 1])
            drop = sb("drop", [A, 2, E])
            below = sb("below", [A, 2, E])
            decay = sb("decay", [A, 2, E])
            weight = sb("weight", [A, 2, E])
            inv_den = sb("inv_den", [P, 2, G])

        gcol_in = [sem(f"gcol_in{s}") for s in range(2)]
        mark_in = [sem(f"mark_in{s}") for s in range(2)]
        scol_in = [sem(f"scol_in{s}") for s in range(2)]
        gathered = [sem(f"gathered{s}") for s in range(2)]
        scattered = [sem(f"scattered{s}") for s in range(2)]
        pool_begun = sem("pool_begun")
        turns_made = sem("turns_made")
        feat_made = sem("feat_made")
        keep_copied = sem("keep_copied")
        start_set = sem("start_set")
        scanned = sem("scanned")
        back_begun = sem("back_begun")
        back_made = sem("back_made")
        outs_made = sem("outs_made")
        if kind in ("rel", "att"):
            picked = sem("picked")
            msg_made = sem("msg_made")
        if kind == "att":
            score_in = sem("score_in")
            score_made = sem("score_made")
            raw_copied = sem("raw_copied")
        if kind == "gat":
            pre_made = sem("pre_made")
            z_made = sem("z_made")
            clamp_made = sem("clamp_made")
            u_made = sem("u_made")
            mish_step = sem("mish_step")
            logits_made = sem("logits_made")
            score_in = sem("score_in")
        if soft:
            top_step = sem("top_step")
            drop_made = sem("drop_made")
            below_made = sem("below_made")
            decay_made = sem("decay_made")
            weight_made = sem("weight_made")
            weighted = sem("weighted")
            den_made = sem("den_made")

        flat = lambda a: a.rearrange("p c e -> p (c e)")
        block = ctx.enter_context(nc.Block())

        @block.sync
        def _(sp):
            def gather_cols(s, t):
                g = 2 * t + s
                if again(t):
                    sp.wait_ge(gathered[s], 64 * ends * t)
                sp.dma_start(gcol[:, s], order[:, bass.ds(g, 1), 0:2, :].rearrange("p o f c -> p (o f c)")
                             .rearrange("p (f c) -> p f c", f=2)).then_inc(gcol_in[s], 16)
                if again(t):
                    sp.wait_ge(turns_made, g - 1)
                sp.dma_start(mark[:, s], marks[:, bass.ds(g, 1), :, :].rearrange("p o f c -> p (o f c)")
                             .rearrange("p (f c) -> p f c", f=3)).then_inc(mark_in[s], 16)

            def scatter_cols(s, t):
                g = 2 * t + s
                if again(t):
                    sp.wait_ge(scattered[s], 64 * t)
                sp.dma_start(scol[:, s], order[:, bass.ds(g, 1), 2, :].rearrange("p o c -> p (o c)")).then_inc(scol_in[s], 16)

            pipelined(sp, [(gather_cols, 0), (scatter_cols, 1)])

        @block.gpsimd
        def _(pool):
            last_row = pool.to_reg(PAD - 1)

            def gather(s, t):
                g = 2 * t + s
                pool.wait_ge(gcol_in[s], 16 * t + 16)
                if again(t):
                    pool.wait_ge(turns_made, g - 1)
                pool.sem_inc(pool_begun, 1)
                for m, col in enumerate((SRC_COL, KEY_COL)[:ends]):
                    for c in range(G):
                        pool.indirect_dma_start(
                            out=got[:, s, c, m * D:(m + 1) * D], out_offset=None, in_=rows,
                            in_offset=bass.IndirectOffsetOnAxis(ap=gcol[:, s, col, c:c + 1], axis=0),
                            bounds_check=last_row, oob_is_err=False).then_inc(gathered[s], 16)

            def scatter(s, t):
                g = 2 * t + s
                pool.wait_ge(scol_in[s], 16 * t + 16)
                pool.wait_ge(outs_made, g + 1)
                pool.sem_inc(pool_begun, 1)
                for c in range(G):
                    pool.indirect_dma_start(
                        out=agg, out_offset=bass.IndirectOffsetOnAxis(ap=scol[:, s, c:c + 1], axis=0),
                        in_=outs[:, s, c, :], in_offset=None,
                        bounds_check=last_row, oob_is_err=False).then_inc(scattered[s], 16)

            pipelined(pool, [(gather, 0), (scatter, LATE)])
            for s in range(2):
                pool.wait_ge(scattered[s], 64 * PAIRS)

        @block.tensor
        def _(pe):
            def turn(s, t):
                g = 2 * t + s
                pe.wait_ge(gathered[s], 64 * ends * (t + 1))
                pe.wait_ge(mark_in[s], 16 * t + 16)
                if again(t):
                    pe.wait_ge(feat_made, g - 1)
                if again(t) or s == 1:
                    if kind == "sum":
                        pe.wait_ge(scanned, g)
                    else:
                        pe.wait_ge(keep_copied, g)
                m = 1 if soft else 0
                for c in range(G):
                    pe.matmul(keep[:, c, :], lhsT=mark[:, s, m, c:c + 1].broadcast_to([P, F]), rhs=n.ident_b[:],
                              start=True, stop=True)
                if kind in ("rel", "att"):
                    if again(t) or s == 1:
                        pe.wait_ge(picked, g)
                    for c in range(G):
                        pe.matmul(types[:, c, :], lhsT=mark[:, s, 2, c:c + 1].broadcast_to([P, P]),
                                  rhs=n.ident_b[:], start=True, stop=True)
                for c in range(G):
                    mm = pe.transpose(turned[s][:, c, :], got[:, s, c, :], n.ident[:])
                mm.then_inc(turns_made, 1)

            def relate(s, t):
                g = 2 * t + s
                pe.wait_ge(picked, g + 1)
                if again(t):
                    pe.wait_ge(scanned, g - 1)
                for j in range(N_REL // 2):
                    mm = pe.matmul(msg[s][:], lhsT=n.rel_w[:, j, :], rhs=masked[:, s, j, :],
                                   start=(j == 0), stop=(j == N_REL // 2 - 1))
                mm.then_inc(msg_made, 1)

            def attend(s, t):
                g = 2 * t + s
                pe.wait_ge(feat_made, g + 1)
                pe.wait_ge(picked, g + 1)
                if again(t) or s == 1:
                    pe.wait_ge(score_made, g)
                if again(t):
                    pe.wait_ge(weighted, g - 1)
                sp_flat = flat(score_p[:])
                pe.matmul(sp_flat, lhsT=n.att_w[:], rhs=feat[:, s], start=True, stop=False)
                for h in range(2):
                    mm = pe.matmul(sp_flat, lhsT=n.att_rel[:, h, :], rhs=hot[:, s, h, :], start=False, stop=(h == 1))
                mm.then_inc(score_in, 1)
                pe.matmul(msg[s][:], lhsT=n.node_w[:], rhs=feat[:, s], start=True, stop=False)
                for h in range(2):
                    mm = pe.matmul(msg[s][:], lhsT=n.rel_rows[:, h, :], rhs=hot[:, s, h, :], start=False, stop=(h == 1))
                mm.then_inc(msg_made, 1)

            def preact(s, t):
                g = 2 * t + s
                pe.wait_ge(feat_made, g + 1)
                if again(t) or s == 1:
                    pe.wait_ge(clamp_made, g)
                for c in range(G):
                    mm = pe.matmul(pre[:, c, :], lhsT=feat[:, s, c * P:(c + 1) * P], rhs=n.score_w[:],
                                   start=True, stop=True)
                mm.then_inc(pre_made, 1)

            def spread(s, t):
                g = 2 * t + s
                pe.wait_ge(logits_made, g + 1)
                if again(t) or s == 1:
                    pe.wait_ge(below_made, g)
                for c in range(G):
                    mm = pe.matmul(score_p[:, c, :], lhsT=logit[:, s, c:c + 1].broadcast_to([P, A]), rhs=n.ident[:],
                                   start=True, stop=True)
                mm.then_inc(score_in, 1)

            def turn_back(s, t):
                g = 2 * t + s
                pe.wait_ge(scanned, g + 1)
                if again(t) or s == 1:
                    pe.wait_ge(outs_made, g)
                pe.sem_inc(back_begun, 1)
                for c in range(G):
                    part = state[:, s, c * P:(c + 1) * P]
                    if kind in ("sum", "gat"):
                        mm = pe.matmul(back[:, c, :], lhsT=part, rhs=n.w0[:] if kind == "sum" else n.edge_w[:],
                                       start=True, stop=True)
                    else:
                        mm = pe.transpose(back[:, c, :], part, n.ident[0:F, 0:F])
                mm.then_inc(back_made, 1)

            pipelined(pe, {
                "sum": [(turn, 0), (turn_back, 1)],
                "gat": [(turn, 0), (spread, 1), (preact, 0), (turn_back, 1)],
                "rel": [(turn, 0), (relate, 1), (turn_back, 2)],
                "att": [(turn, 0), (attend, 0), (turn_back, 1)],
            }[kind])

        @block.scalar
        def _(act):
            def copies(s, t):
                g = 2 * t + s
                act.wait_ge(turns_made, g + 1)
                if again(t):
                    act.wait_ge(scanned if kind == "sum" else picked if kind == "rel" else weighted, g - 1)
                    if kind == "gat":
                        act.wait_ge(pre_made, g - 1)
                    if kind == "att":
                        act.wait_ge(msg_made, g - 1)
                if kind == "rel":
                    nc.scalar.copy(feat[D:P, s], flat(turned[s][:]))
                nc.scalar.copy(feat[0:ends * D, s], flat(turned[s][:])).then_inc(feat_made, 1)
                if kind != "sum":
                    if again(t):
                        act.wait_ge(scanned, g - 1)
                    nc.scalar.copy(keep_s[:, s], flat(keep[:])).then_inc(keep_copied, 1)

            def raw_scores(s, t):
                g = 2 * t + s
                act.wait_ge(score_in, g + 1)
                if again(t) or s == 1:
                    act.wait_ge(score_made, g)
                nc.scalar.copy(raw_score[:], flat(score_p[:])).then_inc(raw_copied, 1)

            def exps(s, t):
                g = 2 * t + s
                act.wait_ge(drop_made, g + 1)
                act.wait_ge(below_made, g + 1)
                if again(t):
                    act.wait_ge(scanned, g - 1)
                nc.scalar.activation(weight[:, s], below[:, s], ACT.Exp).then_inc(weight_made, 1)
                nc.scalar.activation(decay[:, s], drop[:, s], ACT.Exp).then_inc(decay_made, 1)

            def exp_z(s, t):
                g = 2 * t + s
                act.wait_ge(clamp_made, g + 1)
                if again(t):
                    act.wait_ge(logits_made, g - 1)
                nc.scalar.activation(u[:, s], clamped[:, s], ACT.Exp).then_inc(u_made, 1)

            if kind in ("sum", "rel"):
                pipelined(act, [(copies, 0)])
            elif kind == "gat":
                pipelined(act, [(copies, 0), (exps, 1), (exp_z, 0)])
            else:
                pipelined(act, [(copies, 0), (raw_scores, 0), (exps, 1)])

        @block.vector
        def _(dve):
            nc.vector.memset(state[:, 1, E - 1:E], 0.0).then_inc(start_set, 1)
            if soft:
                nc.vector.memset(top[:, 1, E:E + 1], 0.0).then_inc(start_set, 1)
            dve.wait_ge(start_set, 2 if soft else 1)

            def scan(s, t):
                g = 2 * t + s
                if again(t):
                    dve.wait_ge(back_made, g - 1)
                if again(t) or s == 1:
                    dve.wait_ge(scanned, g)
                first = state[:, 1 - s, E - 1:E]
                if kind == "sum":
                    dve.wait_ge(feat_made, g + 1)
                    ins = nc.vector.tensor_tensor_scan(state[:, s], flat(keep[:]), feat[:, s], first, ALU.mult, ALU.add)
                elif kind == "rel":
                    dve.wait_ge(keep_copied, g + 1)
                    dve.wait_ge(msg_made, g + 1)
                    ins = nc.vector.tensor_tensor_scan(state[:, s], keep_s[:, s], msg[s][:], first, ALU.mult, ALU.add)
                else:
                    dve.wait_ge(decay_made, g + 1)
                    dve.wait_ge(weighted, g + 1)
                    ins = nc.vector.tensor_tensor_scan(state[:, s], decay[:, s], weight[:, s], first, ALU.mult, ALU.add)
                ins.then_inc(scanned, 1)

            def finish(s, t):
                g = 2 * t + s
                dve.wait_ge(back_made, g + 1)
                if again(t):
                    dve.wait_ge(scattered[s], 64 * t)
                if not soft:
                    nc.vector.tensor_copy(outs[:, s], back[:]).then_inc(outs_made, 1)
                    return
                link = linker(dve, den_made, (2 if kind == "att" else 1) * g)
                if kind == "att":
                    link(nc.vector.tensor_scalar(inv_den[:, s], back[:, :, D], 1e-12, None, ALU.add))
                    link(nc.vector.reciprocal(inv_den[:, s], inv_den[:, s]))
                else:
                    link(nc.vector.reciprocal(inv_den[:, s], back[:, :, D]))
                nc.vector.tensor_tensor(outs[:, s], back[:, :, 0:D], inv_den[:, s].unsqueeze(2).broadcast_to([P, G, D]),
                                        ALU.mult).then_inc(outs_made, 1)

            def mask(s, t):
                g = 2 * t + s
                dve.wait_ge(feat_made, g + 1)
                if again(t):
                    dve.wait_ge(msg_made, g - 1)
                for j in range(N_REL // 2):
                    ins = nc.vector.scalar_tensor_tensor(masked[:, s, j, :], flat(types[:]), n.relid[:, j:j + 1],
                                                         feat[:, s], ALU.is_equal, ALU.mult)
                ins.then_inc(picked, 1)

            def hots(s, t):
                g = 2 * t + s
                dve.wait_ge(turns_made, g + 1)
                if again(t):
                    dve.wait_ge(msg_made, g - 1)
                for h in range(2):
                    ins = nc.vector.tensor_scalar(hot[:, s, h, :], flat(types[0:RH]), n.part[0:RH, h:h + 1], None, ALU.is_equal)
                ins.then_inc(picked, 1)

            def leaky(s, t):
                g = 2 * t + s
                dve.wait_ge(raw_copied, g + 1)
                if again(t):
                    dve.wait_ge(below_made, g - 1)
                nc.vector.scalar_tensor_tensor(score[:, s], flat(score_p[:]), 0.2, raw_score[:], ALU.mult,
                                               ALU.max).then_inc(score_made, 1)

            def tops(s, t):
                g = 2 * t + s
                link = linker(dve, top_step, 3 * g)
                if again(t):
                    dve.wait_ge(decay_made, g - 1)
                if kind == "gat":
                    dve.wait_ge(score_in, g + 1)
                    sc = flat(score_p[:])
                else:
                    dve.wait_ge(score_made, g + 1)
                    sc = score[:, s]
                dve.wait_ge(keep_copied, g + 1)
                link(nc.vector.tensor_copy(top[:, s, 0:1], top[:, 1 - s, E:E + 1]))
                link(nc.vector.tensor_tensor_scan(top[:, s, 1:E + 1], keep_s[:, s], sc, top[:, s, 0:1], ALU.add, ALU.max))
                link(nc.vector.tensor_tensor(drop[:, s], top[:, s, 0:E], keep_s[:, s], ALU.add))
                nc.vector.tensor_tensor(drop[:, s], drop[:, s], top[:, s, 1:E + 1], ALU.subtract).then_inc(drop_made, 1)
                nc.vector.tensor_tensor(below[:, s], sc, top[:, s, 1:E + 1], ALU.subtract).then_inc(below_made, 1)

            def weigh(s, t):
                g = 2 * t + s
                dve.wait_ge(weight_made, g + 1)
                other = feat[0:D, s] if kind == "gat" else msg[s][:]
                nc.vector.tensor_tensor(weight[0:D, s], weight[0:D, s], other, ALU.mult).then_inc(weighted, 1)

            def clamp(s, t):
                g = 2 * t + s
                dve.wait_ge(pre_made, g + 1)
                if again(t):
                    dve.wait_ge(u_made, g - 1)
                nc.vector.tensor_tensor(z[:, s], pre[:], n.score_b[:].unsqueeze(1).broadcast_to([P, G, D]),
                                        ALU.add).then_inc(z_made, 1)
                dve.wait_ge(z_made, g + 1)
                nc.vector.tensor_scalar(clamped[:, s], z[:, s], 20.0, None, ALU.min).then_inc(clamp_made, 1)

            def logits(s, t):
                g = 2 * t + s
                dve.wait_ge(u_made, g + 1)
                if again(t):
                    dve.wait_ge(score_in, g - 1)
                link = linker(dve, mish_step, 7 * g)
                link(nc.vector.scalar_tensor_tensor(t2[:], u[:, s], 2.0, u[:, s], ALU.add, ALU.mult))
                link(nc.vector.tensor_scalar(den[:], t2[:], 2.0, None, ALU.add))
                link(nc.vector.reciprocal(den[:], den[:]))
                link(nc.vector.tensor_tensor(t2[:], t2[:], z[:, s], ALU.mult))
                link(nc.vector.tensor_tensor(mish[:, s], t2[:], den[:], ALU.mult))
                link(nc.vector.tensor_tensor(mish[:, s], mish[:, s], n.wa[:].unsqueeze(1).broadcast_to([P, G, D]), ALU.mult))
                link(nc.vector.tensor_reduce(logit[:, s], mish[:, s], AX_X, ALU.add))
                nc.vector.tensor_scalar(logit[:, s], logit[:, s], n.wa_b[:, 0:1], None, ALU.add).then_inc(logits_made, 1)

            if kind == "sum":
                pipelined(dve, [(scan, 0), (finish, 1)])
            elif kind == "rel":
                pipelined(dve, [(mask, 0), (scan, 1), (finish, 2)])
            elif kind == "gat":
                pipelined(dve, [(tops, 1), (clamp, 0), (weigh, 1), (scan, 1), (logits, 0), (finish, 1)])
            else:
                pipelined(dve, [(tops, 1), (hots, 0), (leaky, 0), (weigh, 1), (scan, 1), (finish, 1)])



def order_phase(nc, n, k, table, cols, marks, name):
    ctx, sb, ps, sem = phase(nc, name)
    other, kind = (SRC, T16) if k == DST else (DST, T200)
    with ctx:
        edges = [sb(f"edges{m}", [QA, 4, P, 4], I32) for m in range(3)]
        f = sb("fields", [QA, 6, 4, P])
        near = sb("near", [QA, 3, 4, P])
        turned = ps("turned", [P, 6, 512])

        loaded = sem("loaded")
        dve_step = sem("dve_step")
        fields_made = sem("fields_made")
        turns_made = sem("turns_made")

        block = ctx.enter_context(nc.Block())

        @block.sync
        def _(sp):
            for m in range(3):
                view = table[m:m + PAD, :].rearrange("(q a c) f -> a q (c f)", q=4, c=P)
                sp.dma_start(edges[m][:].rearrange("a q c f -> a q (c f)"), view).then_inc(loaded, 16)

        @block.vector
        def _(dve):
            link = linker(dve, dve_step, 0)
            dve.wait_ge(loaded, 48)
            for m in range(3):
                link(nc.vector.tensor_copy(near[:, m], edges[m][:, :, :, k]))
            link(nc.vector.tensor_copy(f[:, 0], edges[1][:, :, :, other]))
            link(nc.vector.tensor_copy(f[:, 1], near[:, 1]))
            link(nc.vector.tensor_tensor(f[:, 2], near[:, 1], near[:, 2], ALU.is_equal))
            link(nc.vector.scalar_tensor_tensor(f[:, 2], f[:, 2], float(SKIP), near[:, 1], ALU.mult, ALU.add))
            link(nc.vector.tensor_tensor(f[:, 3], near[:, 1], near[:, 0], ALU.is_equal))
            link(nc.vector.tensor_scalar(f[:, 4], f[:, 3], -NEG, NEG, ALU.mult, ALU.add))
            nc.vector.tensor_copy(f[:, 5], edges[1][:, :, :, kind]).then_inc(fields_made, 1)

        @block.tensor
        def _(pe):
            pe.wait_ge(fields_made, 1)
            for m in range(6):
                for q in range(4):
                    mm = pe.transpose(turned[:, m, q * QA:(q + 1) * QA], f[:, m, q, :], n.ident[0:QA, 0:QA])
                mm.then_inc(turns_made, 1)

        @block.scalar
        def _(act):
            for m in range(6):
                act.wait_ge(turns_made, m + 1)
                to = cols[:, :, m, :] if m < 3 else marks[:, :, m - 3, :]
                nc.scalar.copy(to, turned[:, m, 0:TILES].rearrange("p (g c) -> p g c", c=G))


def weights_phase(nc, n, w):
    ctx, sb, ps, sem = phase(nc, "weights")
    A = D + 1
    with ctx:
        raw = sb("raw", [D, 8, D])
        row = sb("row", [1, 2, D])
        col = sb("col", [D, 4])
        emb = sb("emb", [RH, 2, D])
        turned_s = sb("turned_s", [D, 4, D])
        emb_t = sb("emb_t", [D, 2, RH])
        v3 = sb("v3", [D, 1])
        vcat = sb("vcat", [P, 1])
        ra = sb("ra", [RH, 2])
        turned = ps("turned", [D, 4, D])
        emb_p = ps("emb_p", [D, 2, RH])
        prod = ps("prod", [P, D])
        bias = ps("bias", [P, D])
        rel = ps("rel", [RH, 2, D])
        vec = ps("vec", [P, 8])

        loaded = sem("loaded")
        dve_step = sem("dve_step")
        turns_made = sem("turns_made")
        turns_copied = sem("turns_copied")
        products_made = sem("products_made")
        v3_made = sem("v3_made")
        v3_copied = sem("v3_copied")
        last_made = sem("last_made")

        block = ctx.enter_context(nc.Block())
        loads = [
            (raw[:, 0, :], w["L0_gnn_W"]), (raw[:, 1, :], w["L1_gnn_We_k"].rearrange("f h d -> f (h d)")),
            (raw[:, 2, :], w["L1_gnn_Ws_k"]), (raw[:, 3, :], w["L3_gnn_W_node"]),
            (raw[:, 4, :], w["L3_gnn_W_node"]), (raw[:, 5, :], w["L3_gnn_W_rel"]),
            (row[:, 0, :], w["L1_gnn_Ws_b"].unsqueeze(0)), (row[:, 1, :], w["L1_gnn_Wr_b"]),
            (emb[:], w["L3_gnn_rel_emb"].rearrange("(h p) d -> p h d", h=2)),
            (col[:, 0:1], w["L1_gnn_We_b"].rearrange("h d -> d h")),
            (n.score_w[D:P, :], w["L1_gnn_Wr_k"].rearrange("f h d -> f (h d)")),
            (n.edge_w[0:D, 0:D], w["L1_gnn_We_k"].rearrange("f h d -> f (h d)")),
            (n.edge_w[D:A, 0:D], w["L1_gnn_We_b"]),
            (n.wa[:], w["L1_gnn_Wa_k"].rearrange("d o -> o d").broadcast_to([P, D])),
            (n.wa_b[:], w["L1_gnn_Wa_b"].unsqueeze(0).broadcast_to([P, 1])),
            (n.bias0[:], w["L0_gnn_b"].unsqueeze(0).broadcast_to([P, D])),
        ]
        loads += [(col[:, 1 + c:2 + c], w["L3_gnn_attvec"][:, c * D:(c + 1) * D].rearrange("o d -> d o")) for c in range(3)]
        loads += [(n.rel_w[h * D:(h + 1) * D], w["L2_gnn_weight"].rearrange("(j h) k n -> h k j n", h=2)[h])
                  for h in range(2)]

        @block.sync
        def _(sp):
            with nc.allow_non_contiguous_dma(reason="a few short vectors"):
                for to, of in loads:
                    sp.dma_start(to, of).then_inc(loaded, 16)
            sp.wait_ge(loaded, 16 * len(loads))

        @block.tensor
        def _(pe):
            pe.wait_ge(loaded, 16 * len(loads))
            for m, r in enumerate((0, 1, 3, 5)):
                pe.transpose(turned[:, m, :], raw[:, r, :], n.ident[0:D, 0:D])
            for h in range(2):
                mm = pe.transpose(emb_p[:, h, :], emb[:, h, :], n.ident[0:RH, 0:RH])
            mm.then_inc(turns_made, 1)
            pe.matmul(vec[0:D, 0:1], lhsT=raw[:, 5, :], rhs=col[:, 3:4], start=True, stop=True).then_inc(v3_made, 1)
            pe.wait_ge(turns_copied, 1)
            pe.matmul(prod[0:D, :], lhsT=turned_s[:, 1, :], rhs=raw[:, 2, :], start=True, stop=True)
            pe.matmul(bias[:], lhsT=col[:, 0:1].broadcast_to([D, P]), rhs=raw[:, 2, :], start=True, stop=False)
            for r in range(2):
                pe.matmul(bias[:], lhsT=n.ones[0:1, 0:P], rhs=row[:, r, :], start=False, stop=(r == 1))
            for h in range(2):
                mm = pe.matmul(rel[:, h, :], lhsT=emb_t[:, h, :], rhs=turned_s[:, 3, :], start=True, stop=True)
            mm.then_inc(products_made, 1)
            pe.wait_ge(v3_copied, 1)
            pe.matmul(vec[:, 1:2], lhsT=raw[:, 3:5, :].rearrange("o c i -> o (c i)"), rhs=col[:, 2:3], start=True, stop=True)
            pe.matmul(vec[:, 2:3], lhsT=raw[:, 3:5, :].rearrange("o c i -> o (c i)"), rhs=col[:, 1:2], start=True, stop=True)
            for h in range(2):
                mm = pe.matmul(vec[0:RH, 3 + h:4 + h], lhsT=emb_t[:, h, :], rhs=v3[:], start=True, stop=True)
            mm.then_inc(last_made, 1)

        @block.vector
        def _(dve):
            link = linker(dve, dve_step, 0)
            dve.wait_ge(loaded, 16 * len(loads))
            link(nc.vector.memset(n.edge_w[:, D:A], 0.0))
            link(nc.vector.memset(n.edge_w[D:A, D:A], 1.0))
            link(nc.vector.memset(n.node_w[:], 0.0))
            dve.wait_ge(turns_made, 1)
            link(nc.vector.tensor_copy(emb_t[:], emb_p[:]))
            link(nc.vector.tensor_copy(n.w0[:], turned[:, 0, :]))
            link(nc.vector.tensor_copy(n.node_w[0:D, :], turned[:, 2, :]))
            nc.vector.tensor_copy(turned_s[:], turned[:]).then_inc(turns_copied, 1)
            dve.wait_ge(v3_made, 1)
            nc.vector.tensor_copy(v3[:], vec[0:D, 0:1]).then_inc(v3_copied, 1)
            dve.wait_ge(products_made, 1)
            link(nc.vector.tensor_copy(n.score_w[0:D, :], prod[0:D, :]))
            link(nc.vector.tensor_copy(n.score_b[:], bias[:]))
            link(nc.vector.tensor_copy(n.rel_rows[:], rel[:]))
            dve.wait_ge(last_made, 1)
            link(nc.vector.tensor_copy(vcat[0:D, :], vec[0:D, 1:2]))
            link(nc.vector.tensor_copy(vcat[D:P, :], vec[D:P, 2:3]))
            link(nc.vector.tensor_copy(ra[:], vec[0:RH, 3:5]))
            link(nc.vector.tensor_copy(n.att_w[:], vcat[:].broadcast_to([P, A])))
            link(nc.vector.tensor_copy(n.att_rel[:], ra[:].unsqueeze(2).broadcast_to([RH, 2, A])))


def prepare_phase(nc, n):
    ctx, sb, ps, sem = phase(nc, "prep")
    with ctx:
        root = sb("root", [P, TILES])
        xin = sb("xin", [P, 2, G, D])
        y = sb("y", [P, 2, G, D])
        yt = sb("yt", [D, 2, G, P])
        own = sb("own", [P, 2, G, D])
        base = sb("base", [P, 2, G, D])
        turned = [ps(f"turned{s}", [D, G, P]) for s in range(2)]
        prod = [ps(f"prod{s}", [P, G, D]) for s in range(2)]

        degree_in = sem("degree_in")
        root_made = sem("root_made")
        inv_made = sem("inv_made")
        x_in = [sem(f"x_in{s}") for s in range(2)]
        y_made = sem("y_made")
        turns_begun = sem("turns_begun")
        turns_made = sem("turns_made")
        turns_copied = sem("turns_copied")
        products_made = sem("products_made")
        dve_step = sem("dve_step")
        base_made = sem("base_made")
        y_out = [sem(f"y_out{s}") for s in range(2)]
        base_out = [sem(f"base_out{s}") for s in range(2)]

        block = ctx.enter_context(nc.Block())
        by_part = lambda t: t.rearrange("(p g c) d -> p g (c d)", p=P, c=G)
        flat = lambda a: a.rearrange("p c d -> p (c d)")
        per_node = lambda a, g: a[:, bass.ds(g * G, G)].unsqueeze(2).broadcast_to([P, G, D])

        @block.sync
        def _(sp):
            sp.dma_start(n.inv[:], n.degree.rearrange("(p t) -> p t", p=P)).then_inc(degree_in, 16)

            def load(s, t):
                g = 2 * t + s
                if again(t):
                    sp.wait_ge(base_made, g - 1)
                sp.dma_start(flat(xin[:, s]), by_part(n.xpad)[:, bass.ds(g, 1), :].rearrange("p o f -> p (o f)")).then_inc(x_in[s], 16)

            pipelined(sp, [(load, 0)])

        @block.scalar
        def _(act):
            act.wait_ge(degree_in, 16)
            nc.scalar.activation(root[:], n.inv[:], ACT.Sqrt, bias=n.ones[:, 0:1]).then_inc(root_made, 1)

            def copy(s, t):
                g = 2 * t + s
                act.wait_ge(turns_made, g + 1)
                if again(t):
                    act.wait_ge(products_made, g - 1)
                nc.scalar.copy(yt[:, s], turned[s][:]).then_inc(turns_copied, 1)

            def store(s, t):
                g = 2 * t + s
                act.wait_ge(y_made, g + 1)
                act.dma_start(by_part(n.y)[:, bass.ds(g, 1), :].rearrange("p o f -> p (o f)"), flat(y[:, s])).then_inc(y_out[s], 16)
                act.wait_ge(base_made, g + 1)
                act.dma_start(by_part(n.base0)[:, bass.ds(g, 1), :].rearrange("p o f -> p (o f)"), flat(base[:, s])).then_inc(base_out[s], 16)

            pipelined(act, [(copy, 0), (store, 1)])
            for s in range(2):
                act.wait_ge(y_out[s], 16 * PAIRS)
                act.wait_ge(base_out[s], 16 * PAIRS)

        @block.vector
        def _(dve):
            dve.wait_ge(root_made, 1)
            nc.vector.reciprocal(n.inv[:], root[:]).then_inc(inv_made, 1)
            dve.wait_ge(inv_made, 1)

            def scale(s, t):
                g = 2 * t + s
                dve.wait_ge(x_in[s], 16 * t + 16)
                if again(t):
                    dve.wait_ge(y_out[s], 16 * t)
                    dve.wait_ge(turns_made, g - 1)
                nc.vector.tensor_tensor(y[:, s], xin[:, s], per_node(n.inv, g), ALU.mult).then_inc(y_made, 1)

            def combine(s, t):
                g = 2 * t + s
                dve.wait_ge(products_made, g + 1)
                link = linker(dve, dve_step, 2 * g)
                link(nc.vector.tensor_tensor(own[:, s], prod[s][:], per_node(n.inv, g), ALU.mult))
                link(nc.vector.tensor_tensor(own[:, s], own[:, s], xin[:, s], ALU.add))
                if again(t):
                    dve.wait_ge(base_out[s], 16 * t)
                nc.vector.tensor_tensor(base[:, s], own[:, s], n.bias0[:].unsqueeze(1).broadcast_to([P, G, D]),
                                        ALU.add).then_inc(base_made, 1)

            pipelined(dve, [(scale, 0), (combine, 1)])

        @block.tensor
        def _(pe):
            def turn(s, t):
                g = 2 * t + s
                pe.wait_ge(y_made, g + 1)
                if again(t):
                    pe.wait_ge(turns_copied, g - 1)
                pe.sem_inc(turns_begun, 1)
                for c in range(G):
                    mm = pe.transpose(turned[s][:, c, :], y[:, s, c, :], n.ident[:])
                mm.then_inc(turns_made, 1)

            def multiply(s, t):
                g = 2 * t + s
                pe.wait_ge(turns_copied, g + 1)
                if again(t):
                    pe.wait_ge(base_made, g - 1)
                for c in range(G):
                    mm = pe.matmul(prod[s][:, c, :], lhsT=yt[:, s, c, :], rhs=n.w0[:], start=True, stop=True)
                mm.then_inc(products_made, 1)

            pipelined(pe, [(turn, 0), (multiply, 1)])


def norm_phase(nc, n, base, sums, to, scale, rows, name):
    ctx, sb, ps, sem = phase(nc, name)
    with ctx:
        a = sb("a", [P, 2, J, D])
        b = sb("b", [P, 2, J, D])
        sq = sb("sq", [P, 2, J, D])
        o = sb("o", [P, 2, J, D])
        mean = sb("mean", [P, 2, J])
        var = sb("var", [P, 2, J])
        dev = sb("dev", [P, 2, J])
        eps = sb("eps", [P, 1])

        rows_in = [sem(f"rows_in{s}") for s in range(2)]
        eps_set = sem("eps_set")
        dve_step = sem("dve_step")
        centred = sem("centred")
        squared = sem("squared")
        var_made = sem("var_made")
        dev_made = sem("dev_made")
        inv_made = sem("inv_made")
        rows_made = sem("rows_made")
        rows_out = [sem(f"rows_out{s}") for s in range(2)]

        block = ctx.enter_context(nc.Block())
        by_part = lambda t: t.rearrange("(p g c) d -> p g (c d)", p=P, c=J)
        flat = lambda t: t.rearrange("p c d -> p (c d)")
        per_node = lambda t: t.unsqueeze(2).broadcast_to([P, J, D])
        STEPS = 3 + (scale is not None)
        full = (N_NODES - (P - 1) * TILES) // J
        part = N_NODES - (P - 1) * TILES - full * J

        def chunks(eng, stages):
            for i in range(NCH // 2 + 1):
                for s in range(2):
                    for stage, lag in stages:
                        c = 2 * i + s - lag
                        if 0 <= c < NCH:
                            stage(c % 2, c // 2)

        @block.sync
        def _(sp):
            def load(s, t):
                c = 2 * t + s
                if again(t):
                    sp.wait_ge(rows_made, c - 1)
                sp.dma_start(flat(a[:, s]), by_part(base)[:, c, :]).then_inc(rows_in[s], 16)
                sp.dma_start(flat(b[:, s]), by_part(sums)[:, c, :]).then_inc(rows_in[s], 16)

            chunks(sp, [(load, 0)])

        @block.vector
        def _(dve):
            nc.vector.memset(eps[:], EPS).then_inc(eps_set, 1)

            def centre(s, t):
                c = 2 * t + s
                dve.wait_ge(rows_in[s], 32 * t + 32)
                link = linker(dve, dve_step, STEPS * c)
                if scale is not None:
                    link(nc.vector.tensor_tensor(b[:, s], b[:, s], per_node(scale[:, c * J:(c + 1) * J]), ALU.mult))
                link(nc.vector.tensor_tensor(a[:, s], a[:, s], b[:, s], ALU.add))
                link(nc.vector.tensor_reduce(mean[:, s], a[:, s], AX_X, ALU.add))
                link(nc.vector.tensor_scalar(mean[:, s], mean[:, s], 1.0 / D, None, ALU.mult))
                nc.vector.tensor_tensor(a[:, s], a[:, s], per_node(mean[:, s]), ALU.subtract).then_inc(centred, 1)

            def spread(s, t):
                c = 2 * t + s
                dve.wait_ge(squared, c + 1)
                if again(t):
                    dve.wait_ge(dev_made, c - 1)
                nc.vector.tensor_reduce(var[:, s], sq[:, s], AX_X, ALU.add).then_inc(var_made, 1)
                dve.wait_ge(dev_made, c + 1)
                if again(t):
                    dve.wait_ge(rows_made, c - 1)
                nc.vector.reciprocal(mean[:, s], dev[:, s]).then_inc(inv_made, 1)

            chunks(dve, [(centre, 0), (spread, 1)])

        @block.scalar
        def _(act):
            act.wait_ge(eps_set, 1)

            def square(s, t):
                c = 2 * t + s
                act.wait_ge(centred, c + 1)
                if again(t):
                    act.wait_ge(var_made, c - 1)
                nc.scalar.activation(sq[:, s], a[:, s], ACT.Square).then_inc(squared, 1)

            def root(s, t):
                c = 2 * t + s
                act.wait_ge(var_made, c + 1)
                if again(t):
                    act.wait_ge(inv_made, c - 1)
                nc.scalar.activation(dev[:, s], var[:, s], ACT.Sqrt, bias=eps[:, 0:1], scale=1.0 / D).then_inc(dev_made, 1)

            def store(s, t):
                c = 2 * t + s
                act.wait_ge(rows_made, c + 1)
                if rows == PAD:
                    act.dma_start(by_part(to)[:, c, :], flat(o[:, s])).then_inc(rows_out[s], 16)
                else:
                    view = to[0:(P - 1) * TILES, :].rearrange("(p g c) d -> p g (c d)", p=P - 1, c=J)
                    act.dma_start(view[:, c, :], flat(o[0:P - 1, s])).then_inc(rows_out[s], 16)
                    left = J if c < full else part if c == full else 0
                    if left:
                        first = (P - 1) * TILES + c * J
                        act.dma_start(to[first:first + left, :].rearrange("(o r) d -> o (r d)", o=1),
                                      flat(o[P - 1:P, s, 0:left])).then_inc(rows_out[s], 16)

            chunks(act, [(square, 0), (root, 1), (store, 1)])
            for s in range(2):
                extra = sum(1 for c in range(s, NCH, 2) if c < full or (c == full and part)) if rows != PAD else 0
                act.wait_ge(rows_out[s], 16 * (NCH // 2 + extra))

        @block.gpsimd
        def _(pool):
            def scaled(s, t):
                c = 2 * t + s
                pool.wait_ge(inv_made, c + 1)
                if again(t):
                    if rows == PAD:
                        pool.wait_ge(rows_out[s], 16 * t)
                    else:
                        extra = sum(1 for d in range(s, c, 2) if d < full or (d == full and part))
                        pool.wait_ge(rows_out[s], 16 * (t + extra))
                nc.gpsimd.tensor_tensor(o[:, s], a[:, s], per_node(mean[:, s]), ALU.mult).then_inc(rows_made, 1)

            chunks(pool, [(scaled, 0)])


def build(nc, x, edge_fields, w, out, upto=99):
    n = Net()
    ctx = ExitStack()

    def dram(name, shape, dt=F32):
        return nc.dram_tensor(name, shape, dt, kind="Internal").ap()

    def sb(name, shape, dt=F32):
        return ctx.enter_context(nc.sbuf_tensor(name, shape, dt))

    with ctx:
        n.xpad = dram("xpad", [PAD, D])
        n.y = dram("y", [PAD, D])
        n.base0 = dram("base0", [PAD, D])
        n.x1 = dram("x1", [PAD, D])
        n.x2 = dram("x2", [PAD, D])
        n.x3 = dram("x3", [PAD, D])
        n.agg_dst = dram("agg_dst", [PAD, D])
        n.agg_src = dram("agg_src", [PAD, D])
        n.sorted_dst = dram("sorted_dst", [PAD + 2, 4], I32)
        n.sorted_src = dram("sorted_src", [PAD + 2, 4], I32)
        n.degree = dram("degree", [PAD])
        n.ident = sb("ident", [P, P])
        n.ident_b = sb("ident_b", [P, P], BF16)
        n.ones = sb("ones", [P, LO])
        n.part = sb("part", [P, 2])
        n.relid = sb("relid", [P, N_REL // 2])
        n.cols_dst = sb("cols_dst", [P, NG, 3, G], I32)
        n.cols_src = sb("cols_src", [P, NG, 3, G], I32)
        n.marks_dst = sb("marks_dst", [P, NG, 3, G], BF16)
        n.marks_src = sb("marks_src", [P, NG, 3, G], BF16)
        n.inv = sb("inv", [P, TILES])
        n.w0 = sb("w0", [D, D])
        n.bias0 = sb("bias0", [P, D])
        n.score_w = sb("score_w", [P, D])
        n.score_b = sb("score_b", [P, D])
        n.edge_w = sb("edge_w", [D + 1, D + 1])
        n.wa = sb("wa", [P, D])
        n.wa_b = sb("wa_b", [P, 1])
        n.rel_w = sb("rel_w", [P, N_REL // 2, D])
        n.node_w = sb("node_w", [P, D])
        n.att_w = sb("att_w", [P, D + 1])
        n.rel_rows = sb("rel_rows", [RH, 2, D])
        n.att_rel = sb("att_rel", [RH, 2, D + 1])
        with ExitStack() as sorting:
            def sb2(name, shape, dt=F32):
                return sorting.enter_context(nc.sbuf_tensor(name, shape, dt))
            n.payload = sb2("payload", [P, TILES, 4], I32)
            n.before = sb2("before", [P, E])
            n.lower = sb2("lower", [P, HH])
            n.iota_lo = sb2("iota_lo", [P, LO], BF16)
            n.hi = sb2("hi", [P, 2, TILES], BF16)
            n.lo = sb2("lo", [P, 2, TILES], BF16)
            n.hi256 = sb2("hi256", [P, 2, TILES], BF16)
            n.keyf = sb2("keyf", [P, 2, TILES])
            n.start = sb2("start", [HH, 2, 2, LO])
            load_phase(nc, n, x, edge_fields)
            histogram_phase(nc, n)
            sort_phase(nc, n, DST, n.sorted_dst, "by_dst")
            sort_phase(nc, n, SRC, n.sorted_src, "by_src")
        order_phase(nc, n, DST, n.sorted_dst, n.cols_dst, n.marks_dst, "order_dst")
        order_phase(nc, n, SRC, n.sorted_src, n.cols_src, n.marks_src, "order_src")
        weights_phase(nc, n, w)
        prepare_phase(nc, n)
        if upto >= 4:
            edge_phase(nc, n, "sum", n.y, n.agg_dst, "edges0")
            norm_phase(nc, n, n.base0, n.agg_dst, n.x1, n.inv, PAD, "norm0")
        if upto >= 5:
            edge_phase(nc, n, "gat", n.x1, n.agg_dst, "edges1")
            norm_phase(nc, n, n.x1, n.agg_dst, n.x2, None, PAD, "norm1")
        if upto >= 6:
            edge_phase(nc, n, "rel", n.x2, n.agg_dst, "edges2")
            norm_phase(nc, n, n.x2, n.agg_dst, n.x3, None, PAD, "norm2")
        if upto >= 7:
            edge_phase(nc, n, "att", n.x3, n.agg_src, "edges3")
            norm_phase(nc, n, n.x3, n.agg_src, out, None, N_NODES, "norm3")


EDGE_INS = ["src", "dst", "edge_type_16", "edge_type_200"]
WEIGHT_INS = ["L0_gnn_W", "L0_gnn_b", "L1_gnn_We_k", "L1_gnn_We_b", "L1_gnn_Ws_k", "L1_gnn_Ws_b", "L1_gnn_Wr_k",
              "L1_gnn_Wr_b", "L1_gnn_Wa_k", "L1_gnn_Wa_b", "L2_gnn_weight", "L3_gnn_W_node", "L3_gnn_W_rel",
              "L3_gnn_attvec", "L3_gnn_rel_emb"]


def kernel(**inputs):
    import concourse.bacc as bacc
    from concourse.bass_utils import run_bass_kernel_spmd

    nc = bacc.Bacc("TRN2", target_bir_lowering=False, num_devices=1)
    arrays, aps = {}, {}
    for name in ["x"] + EDGE_INS + WEIGHT_INS:
        a = np.ascontiguousarray(inputs[name])
        arrays[f"in_{name}"] = a
        aps[name] = nc.dram_tensor(f"in_{name}", a.shape, mybir.dt.from_np(a.dtype), kind="ExternalInput").ap()
    out = nc.dram_tensor("out_x", [N_NODES, D], F32, kind="ExternalOutput").ap()
    build(nc, aps["x"], [aps[name] for name in EDGE_INS], {name: aps[name] for name in WEIGHT_INS}, out)
    ran = run_bass_kernel_spmd(nc, [arrays], core_ids=[0])
    return ran.results[0]["out_x"]
```

```python
from contextlib import ExitStack

import numpy as np

import concourse.bass as bass
from concourse import mybir

ALU = mybir.AluOpType
ACT = mybir.ActivationFunctionType
AX_X = mybir.AxisListType.X
F32 = mybir.dt.float32
BF16 = mybir.dt.bfloat16
I32 = mybir.dt.int32

P = 128
D = 64
N_NODES = 50000
N_EDGES = 50000
TILES = 392
PAD = TILES * P
PAD_KEY = PAD - 1
G = 4
NG = TILES // G
PAIRS = NG // 2
E = G * P
LO = 256
HI = PAD // LO
HH = HI // 2
QA = TILES // 4
N_REL = 16
RELS = 200
RH = RELS // 2
NEG = -1.0e30
SKIP = 65536
EPS = 1e-5
SRC, DST, T16, T200 = range(4)
J = 14
NCH = TILES // J

assert PAD == HI * LO and TILES % (2 * G) == 0 and NCH % 2 == 0


class Net:
    pass


def phase(nc, name):
    ctx = ExitStack()
    sems = []

    def clear():
        nc.clear_and_free_semaphores(sems)
        nc.all_engine_barrier()

    ctx.callback(clear)

    def sb(n, shape, dt=F32):
        return ctx.enter_context(nc.sbuf_tensor(f"{name}_{n}", shape, dt))

    def ps(n, shape, dt=F32):
        return ctx.enter_context(nc.psum_tensor(f"{name}_{n}", shape, dt))

    def sem(n):
        sems.append(nc.alloc_semaphore(f"{name}_{n}"))
        return sems[-1]

    return ctx, sb, ps, sem


def linker(eng, sem, base):
    count = [0]

    def link(ins):
        count[0] += 1
        ins.then_inc(sem, 1)
        eng.wait_ge(sem, base + count[0])

    return link


def pipelined(eng, stages):
    def pair(i, begun):
        for s in range(2):
            for stage, lag in stages:
                turn = i + (s - lag) // 2
                if begun or 0 <= turn < PAIRS:
                    stage((s - lag) % 2, turn)

    peeled = 1 - min((0 - lag) // 2 for _, lag in stages)
    for i in range(peeled):
        pair(i, False)
    with eng.Fori(peeled, PAIRS) as i:
        pair(i, True)
    for i in range(PAIRS, PAIRS + peeled - 1):
        pair(i, False)


def again(turn):
    return not (isinstance(turn, int) and turn == 0)


def node_group(table, g):
    return table.rearrange("(p g c) d -> p g (c d)", p=P, c=G)[:, bass.ds(g, 1), :].rearrange("p o f -> p (o f)")


def rows_of(tile):
    return tile.rearrange("p c d -> p (c d)")


def per_node(column, g):
    return column[:, bass.ds(g * G, G)].unsqueeze(2).broadcast_to([P, G, D])


def load_phase(nc, n, edge_fields):
    ctx, sb, ps, sem = phase(nc, "load")
    with ctx:
        iota_i = sb("iota_i", [P, LO], I32)
        part_i = sb("part_i", [P, 1], I32)
        half = sb("half", [P, 1])
        raw = sb("raw", [QA, 4, 4, P], I32)
        rawf = sb("rawf", [QA, 4, 4, P])
        after = sb("after", [QA, 4, P], I32)
        afterf = sb("afterf", [QA, 4, P])
        falls = sb("falls", [QA, 4, P])
        fall = sb("fall", [QA, 1])
        falls_p = ps("falls_p", [1, 1])
        as_given = sb("as_given", [QA, 4, P, 4], I32)
        digit_i = sb("digit_i", [P, 2, 2, TILES], I32)
        turned = ps("turned", [P, 4, 512])

        pads_set = sem("pads_set")
        pool_step = sem("pool_step")
        consts_made = sem("consts_made")
        edges_in = sem("edges_in")
        floats_made = sem("floats_made")
        fields_turned = sem("fields_turned")
        payload_made = sem("payload_made")
        after_in = sem("after_in")
        falls_made = sem("falls_made")
        falls_summed = sem("falls_summed")
        given_made = sem("given_made")
        given_out = sem("given_out")
        dve_step = sem("dve_step")

        block = ctx.enter_context(nc.Block())

        @block.gpsimd
        def _(pool):
            nc.gpsimd.memset(n.ident[:], 0.0).then_inc(pool_step, 1)
            nc.gpsimd.memset(n.before[:], 1.0).then_inc(pool_step, 1)
            nc.gpsimd.memset(n.lower[:], 1.0).then_inc(pool_step, 1)
            nc.gpsimd.memset(n.ones[:], 1.0).then_inc(consts_made, 1)
            pool.wait_ge(pool_step, 3)
            nc.gpsimd.affine_select(out=n.ident[:], in_=n.ident[:], compare_op=ALU.not_equal, fill=1.0,
                                    base=0, pattern=[[-1, P]], channel_multiplier=1).then_inc(consts_made, 1)
            nc.gpsimd.affine_select(out=n.before[:, E - P:E], in_=n.before[:, E - P:E], compare_op=ALU.is_gt,
                                    fill=0.0, base=0, pattern=[[-1, P]], channel_multiplier=1).then_inc(consts_made, 1)
            nc.gpsimd.affine_select(out=n.lower[:], in_=n.lower[:], compare_op=ALU.is_gt,
                                    fill=0.0, base=0, pattern=[[1, HH]], channel_multiplier=-1).then_inc(consts_made, 1)
            nc.gpsimd.iota(iota_i[:], pattern=[[1, LO]], base=0, channel_multiplier=0).then_inc(consts_made, 1)
            nc.gpsimd.iota(part_i[:], pattern=[[1, 1]], base=0, channel_multiplier=1).then_inc(consts_made, 1)
            pool.wait_ge(edges_in, 16 * 12)
            for f in range(4):
                nc.gpsimd.tensor_copy(as_given[:, :, :, f], raw[:, f]).then_inc(given_made, 1)

        @block.sync
        def _(sp):
            sp.wait_ge(pads_set, 3)
            whole = 3 * QA * P
            for f, a in enumerate(edge_fields):
                sp.dma_start(raw[:, f, 0:3, :], a[0:whole].rearrange("(q a c) -> a q c", q=3, c=P)).then_inc(edges_in, 16)
                rows = (N_EDGES - whole) // P
                rest = whole + rows * P
                sp.dma_start(raw[0:rows, f, 3, :], a[whole:rest].rearrange("(a c) -> a c", c=P)).then_inc(edges_in, 16)
                sp.dma_start(raw[rows:rows + 1, f, 3, 0:N_EDGES - rest],
                             a[rest:N_EDGES].rearrange("(a c) -> a c", a=1)).then_inc(edges_in, 16)
            a = edge_fields[DST]
            sp.dma_start(after[:, 0:3, :], a[1:1 + whole].rearrange("(q a c) -> a q c", q=3, c=P)).then_inc(after_in, 16)
            sp.dma_start(after[0:rows, 3, :], a[1 + whole:1 + rest].rearrange("(a c) -> a c", c=P)).then_inc(after_in, 16)
            sp.dma_start(after[rows:rows + 1, 3, 0:N_EDGES - rest - 1],
                         a[rest + 1:N_EDGES].rearrange("(a c) -> a c", a=1)).then_inc(after_in, 16)
            sp.wait_ge(given_made, 4)
            sp.dma_start(n.sorted_dst[1:PAD + 1, :].rearrange("(q a c) f -> a q (c f)", q=4, c=P),
                         as_given[:].rearrange("a q c f -> a q (c f)")).then_inc(given_out, 16)
            sp.wait_ge(given_out, 16)

        @block.tensor
        def _(pe):
            pe.wait_ge(floats_made, 1)
            pe.wait_ge(consts_made, 6)
            for f in range(4):
                for q in range(4):
                    mm = pe.transpose(turned[:, f, q * QA:(q + 1) * QA], rawf[:, f, q, :], n.ident[0:QA, 0:QA])
                mm.then_inc(fields_turned, 1)
            pe.wait_ge(falls_made, 1)
            pe.matmul(falls_p[:], lhsT=fall[:], rhs=n.ones[0:QA, 0:1], start=True, stop=True).then_inc(falls_summed, 1)

        @block.scalar
        def _(act):
            for f in range(4):
                act.wait_ge(fields_turned, f + 1)
                nc.scalar.copy(n.payload[:, :, f], turned[:, f, 0:TILES]).then_inc(payload_made, 1)

        @block.vector
        def _(dve):
            link = linker(dve, dve_step, 0)
            nc.vector.memset(raw[96:QA, SRC:DST + 1, 3, :], PAD_KEY).then_inc(pads_set, 1)
            nc.vector.memset(raw[96:QA, T16:T200 + 1, 3, :], 0).then_inc(pads_set, 1)
            nc.vector.memset(after[96:QA, 3, :], PAD_KEY).then_inc(pads_set, 1)
            dve.wait_ge(edges_in, 16 * 12)
            nc.vector.tensor_copy(rawf[:], raw[:]).then_inc(floats_made, 1)
            dve.wait_ge(consts_made, 6)
            link(nc.vector.tensor_copy(n.ident_b[:], n.ident[:]))
            link(nc.vector.tensor_copy(n.iota_lo[:], iota_i[:]))
            link(nc.vector.tensor_copy(n.part[:, 0:1], part_i[:]))
            link(nc.vector.tensor_scalar(n.part[:, 1:2], n.part[:, 0:1], float(RH), None, ALU.add))
            link(nc.vector.tensor_scalar(half[:], n.part[:, 0:1], float(D), None, ALU.is_ge))
            for j in range(N_REL // 2):
                link(nc.vector.tensor_scalar(n.relid[:, j:j + 1], half[:], float(2 * j), None, ALU.add))
            dve.wait_ge(after_in, 16 * 3)
            link(nc.vector.tensor_copy(afterf[:], after[:]))
            link(nc.vector.tensor_tensor(falls[:], rawf[:, DST], afterf[:], ALU.is_gt))
            nc.vector.tensor_reduce(fall[:], falls[:].rearrange("a q c -> a (q c)"), AX_X, ALU.add).then_inc(falls_made, 1)
            dve.wait_ge(falls_summed, 1)
            link(nc.vector.tensor_copy(n.falls[:], falls_p[:]))
            dve.wait_ge(payload_made, 4)
            for k in (SRC, DST):
                link(nc.vector.tensor_scalar(digit_i[:, k, 0, :], n.payload[:, :, k], 8, None, ALU.logical_shift_right))
                link(nc.vector.tensor_scalar(digit_i[:, k, 1, :], n.payload[:, :, k], LO - 1, None, ALU.bitwise_and))
                for d in range(2):
                    link(nc.vector.tensor_copy(n.digit[:, k, d, :], digit_i[:, k, d, :]))
                link(nc.vector.tensor_scalar(n.hi256[:, k, :], n.digit[:, k, 0, :], float(LO), None, ALU.mult))
                link(nc.vector.tensor_copy(n.lo[:, k, :], n.digit[:, k, 1, :]))
                link(nc.vector.tensor_copy(n.keyf[:, k, :], n.payload[:, :, k]))


def one_hots(eng, n, k, g, hot, digit):
    width = HI if digit == 0 else LO
    for c in range(G):
        last = eng.tensor_scalar(hot[:, c, :], n.iota_lo[:, 0:width], n.digit[:, k, digit, bass.ds(g * G + c, 1)],
                                 None, ALU.is_equal)
    return last


def histogram_phase(nc, n, x):
    ctx, sb, ps, sem = phase(nc, "hist")
    with ctx:
        lo_hot = sb("lo_hot", [P, 2, 2, G, LO], BF16)
        hi_hot = sb("hi_hot", [P, 2, 2, G, HI], BF16)
        counts = sb("counts", [HH, 2, 2, LO])
        upto = sb("upto", [HH, 2, 2, LO])
        total = sb("total", [HH, 2, 2])
        excl = sb("excl", [HH, 2, 2, LO])
        hist = [ps(f"hist{k}", [HH, 2, LO]) for k in range(2)]
        offset = ps("offset", [HH, 2, 2])
        apart = sb("apart", [P, 2, G, HI], BF16)
        zeros = sb("zeros", [P, TILES // 7 * D])
        minus = sb("minus", [1, 4], I32)

        zeros_set = sem("zeros_set")
        filled = sem("filled")
        hots_made = sem("hots_made")
        apart_made = sem("apart_made")
        act_hots_made = sem("act_hots_made")
        hots_used = sem("hots_used")
        counts_made = sem("counts_made")
        totals_made = sem("totals_made")
        offsets_made = sem("offsets_made")
        dve_step = sem("dve_step")
        stored = sem("stored")

        block = ctx.enter_context(nc.Block())

        @block.vector
        def _(dve):
            nc.vector.memset(zeros[:], 0.0).then_inc(zeros_set, 1)
            nc.vector.memset(minus[:], -1).then_inc(zeros_set, 1)

            def hots(s, t):
                g = 2 * t + s
                for k in (SRC, DST):
                    if again(t):
                        dve.wait_ge(hots_used, 2 * g + k - 3)
                    if k == SRC:
                        one_hots(nc.vector, n, k, g, hi_hot[:, s, k], 0)
                    one_hots(nc.vector, n, k, g, lo_hot[:, s, k], 1).then_inc(hots_made, 1)

            pipelined(dve, [(hots, 0)])
            dve.wait_ge(hots_used, 2 * NG)
            link = linker(dve, dve_step, 0)
            for k in (SRC, DST):
                nc.vector.tensor_copy(counts[:, k], hist[k][:]).then_inc(counts_made, 1)
            dve.wait_ge(counts_made, 2)
            for k in (SRC, DST):
                for h in range(2):
                    link(nc.vector.tensor_tensor_scan(upto[:, k, h], n.ones[0:HH, 0:LO], counts[:, k, h], 0.0,
                                                      ALU.mult, ALU.add))
                link(nc.vector.tensor_copy(total[:, k, :], upto[:, k, :, LO - 1]))
                link(nc.vector.tensor_tensor(excl[:, k], upto[:, k], counts[:, k], ALU.subtract))
            nc.vector.tensor_copy(total[:, 0, :], total[:, 0, :]).then_inc(totals_made, 1)
            dve.wait_ge(offsets_made, 1)
            for k in (SRC, DST):
                for h in range(2):
                    link(nc.vector.tensor_scalar(n.start[:, k, h], excl[:, k, h], offset[:, k, h:h + 1], None, ALU.add))

        @block.tensor
        def _(pe):
            def count(s, t):
                g = 2 * t + s
                for k in (SRC, DST):
                    pe.wait_ge(hots_made, 2 * g + k + 1)
                    if k == DST:
                        pe.wait_ge(act_hots_made, g + 1)
                    for c in range(G):
                        for h in range(2):
                            mm = pe.matmul(hist[k][:, h, :], lhsT=hi_hot[:, s, k, c, h * HH:(h + 1) * HH],
                                           rhs=lo_hot[:, s, k, c, :],
                                           start=not again(t) and s == 0 and c == 0 and h == 0,
                                           stop=False, skip_group_check=True)
                    mm.then_inc(hots_used, 1)

            pipelined(pe, [(count, 0)])
            pe.wait_ge(totals_made, 1)
            for k in (SRC, DST):
                pe.matmul(offset[:, k, 0:1], lhsT=n.lower[0:HH, :], rhs=total[:, k, 0:1], start=True, stop=True)
                pe.matmul(offset[:, k, 1:2], lhsT=n.lower[0:HH, :], rhs=total[:, k, 1:2], start=True, stop=False)
                mm = pe.matmul(offset[:, k, 1:2], lhsT=n.ones[0:HH, 0:HH], rhs=total[:, k, 0:1], start=False, stop=True)
            mm.then_inc(offsets_made, 1)

        @block.scalar
        def _(act):
            def distances(s, t):
                g = 2 * t + s
                if again(t):
                    act.wait_ge(act_hots_made, g - 1)
                for c in range(G):
                    last = nc.scalar.activation(apart[:, s, c, :], n.iota_lo[:, 0:HI], ACT.Abs, scale=-1.0,
                                                bias=n.digit[:, DST, 0, bass.ds(g * G + c, 1)])
                last.then_inc(apart_made, 1)

            def hots(s, t):
                g = 2 * t + s
                act.wait_ge(apart_made, g + 1)
                if again(t):
                    act.wait_ge(hots_used, 2 * g - 2)
                nc.scalar.activation(hi_hot[:, s, DST], apart[:, s], ACT.Relu, scale=-1.0,
                                     bias=n.ones[:, 0:1]).then_inc(act_hots_made, 1)

            pipelined(act, [(distances, 0), (hots, 1)])

        @block.sync
        def _(sp):
            split = lambda t: t.rearrange("(p r) d -> p (r d)", p=400)
            sp.dma_start(split(n.xpad[0:N_NODES, :]), split(x)).then_inc(filled, 16)
            sp.wait_ge(zeros_set, 2)
            pad_rows = PAD - N_NODES
            sp.dma_start(n.xpad[N_NODES:PAD, :].rearrange("(p r) d -> p (r d)", r=2),
                         zeros[0:pad_rows // 2, 0:2 * D]).then_inc(filled, 16)
            for table in (n.agg_dst, n.agg_src):
                view = table.rearrange("(p c r) d -> c p (r d)", p=P, c=7)
                for c in range(7):
                    sp.dma_start(view[c], zeros[:]).then_inc(filled, 16)
            for table in (n.sorted_dst, n.sorted_src):
                sp.dma_start(table[0:1, :], minus[:]).then_inc(filled, 16)
                sp.dma_start(table[PAD + 1:PAD + 2, :], minus[:]).then_inc(filled, 16)
            sp.wait_ge(counts_made, 2)
            sp.dma_start(n.degree.rearrange("(h p l) -> p h l", h=2, l=LO), counts[:, DST]).then_inc(stored, 16)
            sp.wait_ge(stored, 16)
            sp.wait_ge(filled, 16 * (2 + 14 + 4))


def sort_parts(nc, n, k, table, sb, ps, sem, deep):
    r = Net()
    slots = 2 if deep else 1
    lo_hot = sb("lo_hot", [P, 2, G, LO], BF16)
    hi_hot = sb("hi_hot", [P, 2, G, HI], BF16)
    hi_turned = sb("hi_turned", [HH, 2, 2 * G, P], BF16)
    free_hi = sb("free_hi", [HH, 2, 2, LO], BF16)
    free_lo = sb("free_lo", [HH, 2, 2, LO], BF16)
    picked = sb("picked", [P, G, LO])
    matched = sb("matched", [P, G, E])
    base = sb("base", [P, 2, G])
    rank = sb("rank", [P, 2, G])
    place = sb("place", [P, 2, G], I32)
    moved = sb("moved", [P, 2, G, 4], I32)
    running = ps("running", [HH, 2, LO])
    turned = ps("hi_turns", [HH, 2 * G, P], BF16)
    keys = [ps(f"keys{s}", [P, G, P]) for s in range(slots)]
    found = [ps(f"found{s}", [P, G, LO]) for s in range(slots)]

    hi_hots_made = sem("hi_hots_made")
    lo_hots_made = sem("lo_hots_made")
    turns_made = sem("hi_turns_made")
    turns_copied = sem("hi_turns_copied")
    free_hi_made = sem("free_hi_made")
    free_made = sem("free_made")
    found_made = sem("found_made")
    updated = sem("updated")
    picks_made = sem("picks_made")
    places_made = sem("places_made")
    payload_staged = sem("payload_staged")
    scatter_begun = sem("sort_begun")
    scattered = [sem(f"sort_scattered{s}") for s in range(2)]

    def vector(dve):
        def hi_hots(s, t):
            g = 2 * t + s
            if again(t):
                dve.wait_ge(updated, g)
            one_hots(nc.vector, n, k, g, hi_hot[:, s], 0).then_inc(hi_hots_made, 1)

        def lo_hots(s, t):
            g = 2 * t + s
            if again(t):
                dve.wait_ge(updated, g)
            one_hots(nc.vector, n, k, g, lo_hot[:, s], 1).then_inc(lo_hots_made, 1)

        def split(s, t):
            g = 2 * t + s
            dve.wait_ge(free_hi_made, g + 1)
            if again(t):
                dve.wait_ge(found_made, g - 1)
            nc.vector.tensor_tensor(free_lo[:, s], running[:], free_hi[:, s], ALU.subtract).then_inc(free_made, 1)

        def places(s, t):
            g = 2 * t + s
            dve.wait_ge(found_made, g + 1)
            if again(t):
                dve.wait_ge(scattered[s], 64 * t)
            for c in range(G):
                nc.vector.tensor_tensor_reduce(picked[:, c], found[s % slots][:, c], lo_hot[:, s, c], 1.0, 0.0,
                                               ALU.mult, ALU.add, base[:, s, c:c + 1])
                last = nc.vector.scalar_tensor_tensor(
                    matched[:, c, 0:(c + 1) * P], keys[s % slots][:, 0:c + 1, :].rearrange("p c e -> p (c e)"),
                    n.keyf[:, k, bass.ds(g * G + c, 1)], n.before[:, (G - 1 - c) * P:E],
                    ALU.is_equal, ALU.mult, accum_out=rank[:, s, c:c + 1])
            last.then_inc(picks_made, 1)
            dve.wait_ge(picks_made, g + 1)
            nc.vector.scalar_tensor_tensor(place[:, s], base[:, s], 1.0, rank[:, s],
                                           ALU.add, ALU.add).then_inc(places_made, 1)

        if deep:
            return [(split, 1), (hi_hots, 0), (places, 2), (lo_hots, 0)]
        return [(places, 2), (lo_hots, 0), (split, 1), (hi_hots, 0)]

    def tensor(pe):
        def turns(s, t):
            g = 2 * t + s
            pe.wait_ge(hi_hots_made, g + 1)
            if again(t) or s == 1:
                pe.wait_ge(turns_copied, g)
            for c in range(G):
                for h in range(2):
                    mm = pe.transpose(turned[:, 2 * c + h, :], hi_hot[:, s, c, h * HH:(h + 1) * HH], n.ident_b[:])
            mm.then_inc(turns_made, 1)

        def lookups(s, t):
            g = 2 * t + s
            if deep:
                if again(t):
                    pe.wait_ge(places_made, g - 1)
            elif again(t) or s == 1:
                pe.wait_ge(places_made, g)
            for c in range(G):
                col = bass.ds(g * G + c, 1)
                pe.matmul(keys[s % slots][:, c, :], lhsT=n.hi256[:, k, col].broadcast_to([P, P]), rhs=n.ident_b[:],
                          start=True, stop=False)
                pe.matmul(keys[s % slots][:, c, :], lhsT=n.lo[:, k, col].broadcast_to([P, P]), rhs=n.ident_b[:],
                          start=False, stop=True)
            pe.wait_ge(turns_copied, g + 1)
            pe.wait_ge(free_made, g + 1)
            for c in range(G):
                for h in range(2):
                    for part in (free_hi, free_lo):
                        mm = pe.matmul(found[s % slots][:, c, :], lhsT=hi_turned[:, s, 2 * c + h, :],
                                       rhs=part[:, s, h, :], start=(h == 0 and part is free_hi),
                                       stop=(h == 1 and part is free_lo))
            mm.then_inc(found_made, 1)
            pe.wait_ge(lo_hots_made, g + 1)
            for c in range(G):
                for h in range(2):
                    mm = pe.matmul(running[:, h, :], lhsT=hi_hot[:, s, c, h * HH:(h + 1) * HH],
                                   rhs=lo_hot[:, s, c, :], start=False, stop=False, skip_group_check=True)
            mm.then_inc(updated, 1)

        for h in range(2):
            mm = pe.matmul(running[:, h, :], lhsT=n.ident[0:HH, 0:HH], rhs=n.start[:, k, h, :],
                           start=(h == 0), stop=False, skip_group_check=True)
        mm.then_inc(updated, 1)
        return [(lookups, 1), (turns, 0)]

    def scalar(act):
        def copies(s, t):
            g = 2 * t + s
            act.wait_ge(turns_made, g + 1)
            if again(t):
                act.wait_ge(found_made, g - 1)
            nc.scalar.copy(hi_turned[:, s], turned[:]).then_inc(turns_copied, 1)

        def free(s, t):
            g = 2 * t + s
            act.wait_ge(updated, g + 1)
            nc.scalar.copy(free_hi[:, s], running[:]).then_inc(free_hi_made, 1)

        def stage(s, t):
            g = 2 * t + s
            if again(t):
                act.wait_ge(scattered[s], 64 * t)
            nc.scalar.copy(moved[:, s], n.payload[:, bass.ds(g * G, G), :]).then_inc(payload_staged, 1)

        return [(free, 0), (copies, 0), (stage, 2)]

    def gpsimd(pool, last_row):
        def scatter(s, t):
            g = 2 * t + s
            pool.wait_ge(places_made, g + 1)
            pool.wait_ge(payload_staged, g + 1)
            pool.sem_inc(scatter_begun, 1)
            for c in range(G):
                pool.indirect_dma_start(out=table, out_offset=bass.IndirectOffsetOnAxis(ap=place[:, s, c:c + 1], axis=0),
                                        in_=moved[:, s, c, :], in_offset=None,
                                        bounds_check=last_row, oob_is_err=False).then_inc(scattered[s], 16)

        return [(scatter, 3)]

    def finish(pool):
        for s in range(2):
            pool.wait_ge(scattered[s], 64 * PAIRS)

    r.vector, r.tensor, r.scalar, r.gpsimd, r.finish = vector, tensor, scalar, gpsimd, finish
    return r


def sort_phase(nc, n):
    SLOTS = 6
    ctx, sb, ps, sem = phase(nc, "sort")
    with ctx:
        sort = sort_parts(nc, n, DST, n.sorted_dst, sb, ps, sem, True)
        root = sb("root", [P, TILES])
        y = sb("y", [P, SLOTS, J, D])

        degree_in = sem("degree_in")
        root_made = sem("root_made")
        inv_made = sem("inv_made")
        x_in = [sem(f"x_in{s}") for s in range(SLOTS)]
        y_made = sem("y_made")
        y_out = [sem(f"y_out{s}") for s in range(SLOTS)]

        block = ctx.enter_context(nc.Block())
        by_part = lambda t: t.rearrange("(p g c) d -> p g (c d)", p=P, c=J)

        def if_unsorted(eng, name):
            falls = eng.alloc_register(f"falls_{name}")
            eng.load(falls, n.falls[0:1, 0:1])
            return eng.If_ne(falls, 0)

        @block.sync
        def _(sp):
            sp.dma_start(n.inv[:], n.degree.rearrange("(p t) -> p t", p=P)).then_inc(degree_in, 16)
            for c in range(NCH):
                s = c % SLOTS
                if c >= SLOTS:
                    sp.wait_ge(y_out[s], 16 * (c // SLOTS))
                sp.dma_start(rows_of(y[:, s]), by_part(n.xpad)[:, c, :]).then_inc(x_in[s], 16)

        @block.vector
        def _(dve):
            dve.wait_ge(root_made, 1)
            nc.vector.reciprocal(n.inv[:], root[:]).then_inc(inv_made, 1)
            with if_unsorted(dve, "dve"):
                pipelined(dve, sort.vector(dve))

        @block.scalar
        def _(act):
            act.wait_ge(degree_in, 16)
            nc.scalar.activation(root[:], n.inv[:], ACT.Sqrt, bias=n.ones[:, 0:1]).then_inc(root_made, 1)
            for c in range(NCH):
                act.wait_ge(y_made, c + 1)
                act.dma_start(by_part(n.y)[:, c, :], rows_of(y[:, c % SLOTS])).then_inc(y_out[c % SLOTS], 16)
            with if_unsorted(act, "act"):
                pipelined(act, sort.scalar(act))
            for s in range(SLOTS):
                act.wait_ge(y_out[s], 16 * len(range(s, NCH, SLOTS)))

        @block.tensor
        def _(pe):
            with if_unsorted(pe, "pe"):
                pipelined(pe, sort.tensor(pe))

        @block.gpsimd
        def _(pool):
            pool.wait_ge(inv_made, 1)
            for c in range(NCH):
                s = c % SLOTS
                pool.wait_ge(x_in[s], 16 * (c // SLOTS + 1))
                nc.gpsimd.tensor_tensor(y[:, s], y[:, s], n.inv[:, c * J:(c + 1) * J].unsqueeze(2).broadcast_to([P, J, D]),
                                        ALU.mult).then_inc(y_made, 1)
            with if_unsorted(pool, "pool"):
                last_row = pool.to_reg(PAD + 1)
                pipelined(pool, sort.gpsimd(pool, last_row))
                sort.finish(pool)


def edge_phase(nc, n, kind, rows, agg, name):
    A = D + 1
    soft = kind in ("gat", "att")
    ends = 2 if soft else 1
    wide = D if kind == "sum" else P
    order, marks = (n.cols_src, n.marks_src) if kind == "att" else (n.cols_dst, n.marks_dst)
    SRC_COL, KEY_COL = 0, 1
    F = A if soft else D
    LATE = 4 if kind == "rel" else 3

    ctx, sb, ps, sem = phase(nc, name)
    with ctx:
        gcol = sb("gcol", [P, 2, 2, G], I32)
        scol = sb("scol", [P, 2, G], I32)
        mark = sb("mark", [P, 2, 3, G], BF16)
        got = sb("got", [P, 2, G, P if kind in ("sum",) else ends * D])
        feat = sb("feat", [wide, 2, E])
        state = sb("state", [P if kind == "sum" else F, 2, E])
        outs = sb("outs", [P, 2, G, D])
        turned = [ps(f"turned{s}", [P if kind == "sum" else ends * D, G, P]) for s in range(1 if kind == "sum" else 2)]
        turned = turned * (3 - len(turned))
        keep = ps("keep", [F, G, P])
        back = ps("back", [P, G, P if kind == "sum" else A if soft else D])
        if kind == "sum":
            sort = sort_parts(nc, n, SRC, n.sorted_src, sb, ps, sem, False)
            xin = sb("xin", [P, 2, G, D])
            base = sb("own_base", [P, 2, G, D])
            own_in = [sem(f"own_in{s}") for s in range(2)]
            x_in = [sem(f"x_in{s}") for s in range(2)]
            base_step = sem("base_step")
            base_made = sem("base_made")
            base_out = [sem(f"base_out{s}") for s in range(2)]
        if kind != "sum":
            keep_s = sb("keep_s", [F, 2, E])
        if kind in ("rel", "att"):
            types = ps("types", [P, G, P])
            msg = [ps(f"msg{s}", [D, E]) for s in range(2)]
        if kind == "rel":
            masked = sb("masked", [P, 2, N_REL // 2, E])
        if kind == "att":
            hot = sb("hot", [RH, 2, 2, E])
            raw_score = sb("raw_score", [A, E])
            score = sb("score", [A, 2, E])
        if kind == "gat":
            pre = ps("pre", [P, G, D])
            z = sb("z", [P, 2, G, D])
            clamped = sb("clamped", [P, 2, G, D])
            u = sb("u", [P, 2, G, D])
            t2 = sb("t2", [P, G, D])
            den = sb("den", [P, G, D])
            mish = sb("mish", [P, 2, G, D])
            logit = sb("logit", [P, 2, G])
        if soft:
            score_p = ps("score_p", [A, G, P])
            top = sb("top", [A, 2, E + 1])
            drop = sb("drop", [A, 2, E])
            below = sb("below", [A, 2, E])
            decay = sb("decay", [A, 2, E])
            weight = sb("weight", [A, 2, E])
            inv_den = sb("inv_den", [P, 2, G])

        gcol_in = [sem(f"gcol_in{s}") for s in range(2)]
        mark_in = [sem(f"mark_in{s}") for s in range(2)]
        scol_in = [sem(f"scol_in{s}") for s in range(2)]
        gathered = [sem(f"gathered{s}") for s in range(2)]
        scattered = [sem(f"scattered{s}") for s in range(2)]
        pool_begun = sem("pool_begun")
        turns_made = sem("turns_made")
        feat_made = sem("feat_made")
        keep_copied = sem("keep_copied")
        start_set = sem("start_set")
        scanned = sem("scanned")
        back_begun = sem("back_begun")
        back_made = sem("back_made")
        outs_made = sem("outs_made")
        if kind in ("rel", "att"):
            picked = sem("picked")
            msg_made = sem("msg_made")
        if kind == "att":
            score_in = sem("score_in")
            score_made = sem("score_made")
            raw_copied = sem("raw_copied")
        if kind == "gat":
            pre_made = sem("pre_made")
            z_made = sem("z_made")
            clamp_made = sem("clamp_made")
            u_made = sem("u_made")
            mish_step = sem("mish_step")
            logits_made = sem("logits_made")
            score_in = sem("score_in")
        if soft:
            top_step = sem("top_step")
            drop_made = sem("drop_made")
            below_made = sem("below_made")
            decay_made = sem("decay_made")
            weight_made = sem("weight_made")
            weighted = sem("weighted")
            den_made = sem("den_made")

        flat = lambda a: a.rearrange("p c e -> p (c e)")
        block = ctx.enter_context(nc.Block())

        @block.sync
        def _(sp):
            def gather_cols(s, t):
                g = 2 * t + s
                if again(t):
                    sp.wait_ge(gathered[s], 64 * ends * t)
                sp.dma_start(gcol[:, s], order[:, bass.ds(g, 1), 0:2, :].rearrange("p o f c -> p (o f c)")
                             .rearrange("p (f c) -> p f c", f=2)).then_inc(gcol_in[s], 16)
                if again(t):
                    sp.wait_ge(turns_made, g - 1)
                sp.dma_start(mark[:, s], marks[:, bass.ds(g, 1), :, :].rearrange("p o f c -> p (o f c)")
                             .rearrange("p (f c) -> p f c", f=3)).then_inc(mark_in[s], 16)

            def scatter_cols(s, t):
                g = 2 * t + s
                if again(t):
                    sp.wait_ge(scattered[s], 64 * t)
                sp.dma_start(scol[:, s], order[:, bass.ds(g, 1), 2, :].rearrange("p o c -> p (o c)")).then_inc(scol_in[s], 16)

            def own_rows(s, t):
                g = 2 * t + s
                sp.dma_start(got[:, s, :, D:P], n.y.rearrange("(p g c) d -> p g c d", p=P, c=G)[:, bass.ds(g, 1)]
                             .rearrange("p o c d -> p (o c) d")).then_inc(own_in[s], 16)

            def x_rows(s, t):
                g = 2 * t + s
                if again(t):
                    sp.wait_ge(base_made, g - 1)
                sp.dma_start(rows_of(xin[:, s]), node_group(n.xpad, g)).then_inc(x_in[s], 16)

            def base_rows(s, t):
                g = 2 * t + s
                sp.wait_ge(base_made, g + 1)
                sp.dma_start(node_group(n.base0, g), rows_of(base[:, s])).then_inc(base_out[s], 16)

            stages = [(scatter_cols, LATE), (gather_cols, 0)]
            if kind == "sum":
                stages = [(scatter_cols, LATE), (gather_cols, 0), (own_rows, 0), (x_rows, 1), (base_rows, 3)]
            pipelined(sp, stages)
            if kind == "sum":
                for s in range(2):
                    sp.wait_ge(base_out[s], 16 * PAIRS)

        @block.gpsimd
        def _(pool):
            last_row = pool.to_reg(PAD - 1)

            def gather(s, t):
                g = 2 * t + s
                pool.wait_ge(gcol_in[s], 16 * t + 16)
                if again(t):
                    pool.wait_ge(turns_made, g - 1)
                pool.sem_inc(pool_begun, 1)
                for m, col in enumerate((SRC_COL, KEY_COL)[:ends]):
                    for c in range(G):
                        pool.indirect_dma_start(
                            out=got[:, s, c, m * D:(m + 1) * D], out_offset=None, in_=rows,
                            in_offset=bass.IndirectOffsetOnAxis(ap=gcol[:, s, col, c:c + 1], axis=0),
                            bounds_check=last_row, oob_is_err=False).then_inc(gathered[s], 16)

            def scatter(s, t):
                g = 2 * t + s
                pool.wait_ge(scol_in[s], 16 * t + 16)
                pool.wait_ge(outs_made, g + 1)
                pool.sem_inc(pool_begun, 1)
                for c in range(G):
                    pool.indirect_dma_start(
                        out=agg, out_offset=bass.IndirectOffsetOnAxis(ap=scol[:, s, c:c + 1], axis=0),
                        in_=outs[:, s, c, :], in_offset=None,
                        bounds_check=last_row, oob_is_err=False).then_inc(scattered[s], 16)

            if kind == "sum":
                pipelined(pool, [(gather, 0), (scatter, LATE)] + sort.gpsimd(pool, pool.to_reg(PAD + 1)))
                sort.finish(pool)
            else:
                pipelined(pool, [(gather, 0), (scatter, LATE)])
            for s in range(2):
                pool.wait_ge(scattered[s], 64 * PAIRS)

        @block.tensor
        def _(pe):
            def turn(s, t):
                g = 2 * t + s
                pe.wait_ge(gathered[s], 64 * ends * (t + 1))
                pe.wait_ge(mark_in[s], 16 * t + 16)
                if kind == "sum":
                    pe.wait_ge(own_in[s], 16 * (t + 1))
                    if again(t) or s == 1:
                        pe.wait_ge(feat_made, g)
                elif again(t):
                    pe.wait_ge(feat_made, g - 1)
                if again(t) or s == 1:
                    if kind == "sum":
                        pe.wait_ge(scanned, g)
                    else:
                        pe.wait_ge(keep_copied, g)
                m = 1 if soft else 0
                for c in range(G):
                    pe.matmul(keep[:, c, :], lhsT=mark[:, s, m, c:c + 1].broadcast_to([P, F]), rhs=n.ident_b[:],
                              start=True, stop=True)
                if kind in ("rel", "att"):
                    if again(t) or s == 1:
                        pe.wait_ge(picked, g)
                    for c in range(G):
                        pe.matmul(types[:, c, :], lhsT=mark[:, s, 2, c:c + 1].broadcast_to([P, P]),
                                  rhs=n.ident_b[:], start=True, stop=True)
                for c in range(G):
                    mm = pe.transpose(turned[s][:, c, :], got[:, s, c, :], n.ident[:])
                mm.then_inc(turns_made, 1)

            def relate(s, t):
                g = 2 * t + s
                pe.wait_ge(picked, g + 1)
                if again(t):
                    pe.wait_ge(scanned, g - 1)
                for j in range(N_REL // 2):
                    mm = pe.matmul(msg[s][:], lhsT=n.rel_w[:, j, :], rhs=masked[:, s, j, :],
                                   start=(j == 0), stop=(j == N_REL // 2 - 1))
                mm.then_inc(msg_made, 1)

            def attend(s, t):
                g = 2 * t + s
                pe.wait_ge(feat_made, g + 1)
                pe.wait_ge(picked, g + 1)
                if again(t) or s == 1:
                    pe.wait_ge(score_made, g)
                if again(t):
                    pe.wait_ge(weighted, g - 1)
                sp_flat = flat(score_p[:])
                pe.matmul(sp_flat, lhsT=n.att_w[:], rhs=feat[:, s], start=True, stop=False)
                for h in range(2):
                    mm = pe.matmul(sp_flat, lhsT=n.att_rel[:, h, :], rhs=hot[:, s, h, :], start=False, stop=(h == 1))
                mm.then_inc(score_in, 1)
                pe.matmul(msg[s][:], lhsT=n.node_w[:], rhs=feat[:, s], start=True, stop=False)
                for h in range(2):
                    mm = pe.matmul(msg[s][:], lhsT=n.rel_rows[:, h, :], rhs=hot[:, s, h, :], start=False, stop=(h == 1))
                mm.then_inc(msg_made, 1)

            def preact(s, t):
                g = 2 * t + s
                pe.wait_ge(feat_made, g + 1)
                if again(t) or s == 1:
                    pe.wait_ge(clamp_made, g)
                for c in range(G):
                    mm = pe.matmul(pre[:, c, :], lhsT=feat[:, s, c * P:(c + 1) * P], rhs=n.score_w[:],
                                   start=True, stop=True)
                mm.then_inc(pre_made, 1)

            def spread(s, t):
                g = 2 * t + s
                pe.wait_ge(logits_made, g + 1)
                if again(t) or s == 1:
                    pe.wait_ge(below_made, g)
                for c in range(G):
                    mm = pe.matmul(score_p[:, c, :], lhsT=logit[:, s, c:c + 1].broadcast_to([P, A]), rhs=n.ident[:],
                                   start=True, stop=True)
                mm.then_inc(score_in, 1)

            def turn_back(s, t):
                g = 2 * t + s
                pe.wait_ge(scanned, g + 1)
                if again(t) or s == 1:
                    pe.wait_ge(outs_made, g)
                pe.sem_inc(back_begun, 1)
                for c in range(G):
                    part = state[:, s, c * P:(c + 1) * P]
                    if kind in ("sum", "gat"):
                        mm = pe.matmul(back[:, c, :], lhsT=part, rhs=n.w0[:] if kind == "sum" else n.edge_w[:],
                                       start=True, stop=True)
                    else:
                        mm = pe.transpose(back[:, c, :], part, n.ident[0:F, 0:F])
                mm.then_inc(back_made, 1)

            pipelined(pe, {
                "sum": [(turn, 0), (turn_back, 1)] + (sort.tensor(pe) if kind == "sum" else []),
                "gat": [(turn, 0), (spread, 1), (preact, 0), (turn_back, 1)],
                "rel": [(turn, 0), (relate, 1), (turn_back, 2)],
                "att": [(turn, 0), (attend, 0), (turn_back, 1)],
            }[kind])

        @block.scalar
        def _(act):
            def copies(s, t):
                g = 2 * t + s
                act.wait_ge(turns_made, g + 1)
                if again(t):
                    act.wait_ge(scanned if kind == "sum" else picked if kind == "rel" else weighted, g - 1)
                    if kind == "gat":
                        act.wait_ge(pre_made, g - 1)
                    if kind == "att":
                        act.wait_ge(msg_made, g - 1)
                if kind == "sum":
                    if again(t):
                        act.wait_ge(back_made, g - 1)
                    nc.scalar.copy(state[D:P, s], flat(turned[s][D:P]))
                if kind == "rel":
                    nc.scalar.copy(feat[D:P, s], flat(turned[s][:]))
                nc.scalar.copy(feat[0:ends * D, s], flat(turned[s][0:ends * D])).then_inc(feat_made, 1)
                if kind != "sum":
                    if again(t):
                        act.wait_ge(scanned, g - 1)
                    nc.scalar.copy(keep_s[:, s], flat(keep[:])).then_inc(keep_copied, 1)

            def raw_scores(s, t):
                g = 2 * t + s
                act.wait_ge(score_in, g + 1)
                if again(t) or s == 1:
                    act.wait_ge(score_made, g)
                nc.scalar.copy(raw_score[:], flat(score_p[:])).then_inc(raw_copied, 1)

            def exps(s, t):
                g = 2 * t + s
                act.wait_ge(drop_made, g + 1)
                act.wait_ge(below_made, g + 1)
                if again(t):
                    act.wait_ge(scanned, g - 1)
                nc.scalar.activation(weight[:, s], below[:, s], ACT.Exp).then_inc(weight_made, 1)
                nc.scalar.activation(decay[:, s], drop[:, s], ACT.Exp).then_inc(decay_made, 1)

            def exp_z(s, t):
                g = 2 * t + s
                act.wait_ge(clamp_made, g + 1)
                if again(t):
                    act.wait_ge(logits_made, g - 1)
                nc.scalar.activation(u[:, s], clamped[:, s], ACT.Exp).then_inc(u_made, 1)

            if kind == "sum":
                pipelined(act, [(copies, 0)] + sort.scalar(act))
            elif kind == "rel":
                pipelined(act, [(copies, 0)])
            elif kind == "gat":
                pipelined(act, [(copies, 0), (exps, 1), (exp_z, 0)])
            else:
                pipelined(act, [(copies, 0), (exps, 1), (raw_scores, 0)])

        @block.vector
        def _(dve):
            nc.vector.memset(state[0:F, 1, E - 1:E], 0.0).then_inc(start_set, 1)
            if soft:
                nc.vector.memset(top[:, 1, E:E + 1], 0.0).then_inc(start_set, 1)
            dve.wait_ge(start_set, 2 if soft else 1)

            def scan(s, t):
                g = 2 * t + s
                if again(t):
                    dve.wait_ge(back_made, g - 1)
                if again(t) or s == 1:
                    dve.wait_ge(scanned, g)
                first = state[0:F, 1 - s, E - 1:E]
                if kind == "sum":
                    dve.wait_ge(feat_made, g + 1)
                    ins = nc.vector.tensor_tensor_scan(state[0:F, s], flat(keep[:]), feat[:, s], first, ALU.mult, ALU.add)
                elif kind == "rel":
                    dve.wait_ge(keep_copied, g + 1)
                    dve.wait_ge(msg_made, g + 1)
                    ins = nc.vector.tensor_tensor_scan(state[:, s], keep_s[:, s], msg[s][:], first, ALU.mult, ALU.add)
                else:
                    dve.wait_ge(decay_made, g + 1)
                    dve.wait_ge(weighted, g + 1)
                    ins = nc.vector.tensor_tensor_scan(state[:, s], decay[:, s], weight[:, s], first, ALU.mult, ALU.add)
                ins.then_inc(scanned, 1)

            def finish(s, t):
                g = 2 * t + s
                dve.wait_ge(back_made, g + 1)
                if again(t):
                    dve.wait_ge(scattered[s], 64 * t)
                if kind == "sum":
                    link = linker(dve, base_step, 2 * g)
                    dve.wait_ge(x_in[s], 16 * t + 16)
                    if again(t):
                        dve.wait_ge(base_out[s], 16 * t)
                    link(nc.vector.tensor_tensor(base[:, s], back[:, :, D:P], per_node(n.inv, g), ALU.mult))
                    link(nc.vector.tensor_tensor(base[:, s], base[:, s], xin[:, s], ALU.add))
                    nc.vector.tensor_tensor(base[:, s], base[:, s], n.bias0[:].unsqueeze(1).broadcast_to([P, G, D]),
                                            ALU.add).then_inc(base_made, 1)
                if not soft:
                    nc.vector.tensor_copy(outs[:, s], back[:, :, 0:D]).then_inc(outs_made, 1)
                    return
                link = linker(dve, den_made, (2 if kind == "att" else 1) * g)
                if kind == "att":
                    link(nc.vector.tensor_scalar(inv_den[:, s], back[:, :, D], 1e-12, None, ALU.add))
                    link(nc.vector.reciprocal(inv_den[:, s], inv_den[:, s]))
                else:
                    link(nc.vector.reciprocal(inv_den[:, s], back[:, :, D]))
                nc.vector.tensor_tensor(outs[:, s], back[:, :, 0:D], inv_den[:, s].unsqueeze(2).broadcast_to([P, G, D]),
                                        ALU.mult).then_inc(outs_made, 1)

            def mask(s, t):
                g = 2 * t + s
                dve.wait_ge(feat_made, g + 1)
                if again(t):
                    dve.wait_ge(msg_made, g - 1)
                for j in range(N_REL // 2):
                    ins = nc.vector.scalar_tensor_tensor(masked[:, s, j, :], flat(types[:]), n.relid[:, j:j + 1],
                                                         feat[:, s], ALU.is_equal, ALU.mult)
                ins.then_inc(picked, 1)

            def hots(s, t):
                g = 2 * t + s
                dve.wait_ge(turns_made, g + 1)
                if again(t):
                    dve.wait_ge(msg_made, g - 1)
                for h in range(2):
                    ins = nc.vector.tensor_scalar(hot[:, s, h, :], flat(types[0:RH]), n.part[0:RH, h:h + 1], None, ALU.is_equal)
                ins.then_inc(picked, 1)

            def leaky(s, t):
                g = 2 * t + s
                dve.wait_ge(raw_copied, g + 1)
                if again(t):
                    dve.wait_ge(below_made, g - 1)
                nc.vector.scalar_tensor_tensor(score[:, s], flat(score_p[:]), 0.2, raw_score[:], ALU.mult,
                                               ALU.max).then_inc(score_made, 1)

            def tops(s, t):
                g = 2 * t + s
                link = linker(dve, top_step, 3 * g)
                if again(t):
                    dve.wait_ge(decay_made, g - 1)
                if kind == "gat":
                    dve.wait_ge(score_in, g + 1)
                    sc = flat(score_p[:])
                else:
                    dve.wait_ge(score_made, g + 1)
                    sc = score[:, s]
                dve.wait_ge(keep_copied, g + 1)
                link(nc.vector.tensor_copy(top[:, s, 0:1], top[:, 1 - s, E:E + 1]))
                link(nc.vector.tensor_tensor_scan(top[:, s, 1:E + 1], keep_s[:, s], sc, top[:, s, 0:1], ALU.add, ALU.max))
                link(nc.vector.tensor_tensor(drop[:, s], top[:, s, 0:E], keep_s[:, s], ALU.add))
                nc.vector.tensor_tensor(drop[:, s], drop[:, s], top[:, s, 1:E + 1], ALU.subtract).then_inc(drop_made, 1)
                nc.vector.tensor_tensor(below[:, s], sc, top[:, s, 1:E + 1], ALU.subtract).then_inc(below_made, 1)

            def weigh(s, t):
                g = 2 * t + s
                dve.wait_ge(weight_made, g + 1)
                other = feat[0:D, s] if kind == "gat" else msg[s][:]
                nc.vector.tensor_tensor(weight[0:D, s], weight[0:D, s], other, ALU.mult).then_inc(weighted, 1)

            def clamp(s, t):
                g = 2 * t + s
                dve.wait_ge(pre_made, g + 1)
                if again(t):
                    dve.wait_ge(u_made, g - 1)
                nc.vector.tensor_tensor(z[:, s], pre[:], n.score_b[:].unsqueeze(1).broadcast_to([P, G, D]),
                                        ALU.add).then_inc(z_made, 1)
                dve.wait_ge(z_made, g + 1)
                nc.vector.tensor_scalar(clamped[:, s], z[:, s], 20.0, None, ALU.min).then_inc(clamp_made, 1)

            def logits(s, t):
                g = 2 * t + s
                dve.wait_ge(u_made, g + 1)
                if again(t):
                    dve.wait_ge(score_in, g - 1)
                link = linker(dve, mish_step, 7 * g)
                link(nc.vector.scalar_tensor_tensor(t2[:], u[:, s], 2.0, u[:, s], ALU.add, ALU.mult))
                link(nc.vector.tensor_scalar(den[:], t2[:], 2.0, None, ALU.add))
                link(nc.vector.reciprocal(den[:], den[:]))
                link(nc.vector.tensor_tensor(t2[:], t2[:], z[:, s], ALU.mult))
                link(nc.vector.tensor_tensor(mish[:, s], t2[:], den[:], ALU.mult))
                link(nc.vector.tensor_tensor(mish[:, s], mish[:, s], n.wa[:].unsqueeze(1).broadcast_to([P, G, D]), ALU.mult))
                link(nc.vector.tensor_reduce(logit[:, s], mish[:, s], AX_X, ALU.add))
                nc.vector.tensor_scalar(logit[:, s], logit[:, s], n.wa_b[:, 0:1], None, ALU.add).then_inc(logits_made, 1)

            if kind == "sum":
                pipelined(dve, sort.vector(dve) + [(scan, 0), (finish, 1)])
            elif kind == "rel":
                pipelined(dve, [(mask, 0), (scan, 1), (finish, 2)])
            elif kind == "gat":
                pipelined(dve, [(tops, 1), (clamp, 0), (weigh, 1), (scan, 1), (logits, 0), (finish, 1)])
            else:
                pipelined(dve, [(hots, 0), (tops, 1), (weigh, 1), (scan, 1), (leaky, 0), (finish, 1)])



def order_phase(nc, n, k, table, cols, marks, name):
    ctx, sb, ps, sem = phase(nc, name)
    other, kind = (SRC, T16) if k == DST else (DST, T200)
    with ctx:
        edges = [sb(f"edges{m}", [QA, 4, P, 4], I32) for m in range(3)]
        f = sb("fields", [QA, 6, 4, P])
        near = sb("near", [QA, 3, 4, P])
        turned = ps("turned", [P, 6, 512])

        loaded = sem("loaded")
        dve_step = sem("dve_step")
        fields_made = sem("fields_made")
        turns_made = sem("turns_made")

        block = ctx.enter_context(nc.Block())

        @block.sync
        def _(sp):
            for m in range(3):
                view = table[m:m + PAD, :].rearrange("(q a c) f -> a q (c f)", q=4, c=P)
                sp.dma_start(edges[m][:].rearrange("a q c f -> a q (c f)"), view).then_inc(loaded, 16)

        @block.vector
        def _(dve):
            link = linker(dve, dve_step, 0)
            dve.wait_ge(loaded, 48)
            for m in range(3):
                link(nc.vector.tensor_copy(near[:, m], edges[m][:, :, :, k]))
            link(nc.vector.tensor_copy(f[:, 0], edges[1][:, :, :, other]))
            link(nc.vector.tensor_copy(f[:, 1], near[:, 1]))
            link(nc.vector.tensor_tensor(f[:, 2], near[:, 1], near[:, 2], ALU.is_equal))
            link(nc.vector.scalar_tensor_tensor(f[:, 2], f[:, 2], float(SKIP), near[:, 1], ALU.mult, ALU.add))
            link(nc.vector.tensor_tensor(f[:, 3], near[:, 1], near[:, 0], ALU.is_equal))
            link(nc.vector.tensor_scalar(f[:, 4], f[:, 3], -NEG, NEG, ALU.mult, ALU.add))
            nc.vector.tensor_copy(f[:, 5], edges[1][:, :, :, kind]).then_inc(fields_made, 1)

        @block.tensor
        def _(pe):
            pe.wait_ge(fields_made, 1)
            for m in range(6):
                for q in range(4):
                    mm = pe.transpose(turned[:, m, q * QA:(q + 1) * QA], f[:, m, q, :], n.ident[0:QA, 0:QA])
                mm.then_inc(turns_made, 1)

        @block.scalar
        def _(act):
            for m in range(6):
                act.wait_ge(turns_made, m + 1)
                to = cols[:, :, m, :] if m < 3 else marks[:, :, m - 3, :]
                nc.scalar.copy(to, turned[:, m, 0:TILES].rearrange("p (g c) -> p g c", c=G))


def weights_phase(nc, n, w):
    ctx, sb, ps, sem = phase(nc, "weights")
    A = D + 1
    with ctx:
        raw = sb("raw", [D, 8, D])
        row = sb("row", [1, 2, D])
        col = sb("col", [D, 4])
        emb = sb("emb", [RH, 2, D])
        turned_s = sb("turned_s", [D, 4, D])
        emb_t = sb("emb_t", [D, 2, RH])
        v3 = sb("v3", [D, 1])
        vcat = sb("vcat", [P, 1])
        ra = sb("ra", [RH, 2])
        turned = ps("turned", [D, 4, D])
        emb_p = ps("emb_p", [D, 2, RH])
        prod = ps("prod", [P, D])
        bias = ps("bias", [P, D])
        rel = ps("rel", [RH, 2, D])
        vec = ps("vec", [P, 8])

        loaded = sem("loaded")
        dve_step = sem("dve_step")
        turns_made = sem("turns_made")
        turns_copied = sem("turns_copied")
        products_made = sem("products_made")
        v3_made = sem("v3_made")
        v3_copied = sem("v3_copied")
        last_made = sem("last_made")

        block = ctx.enter_context(nc.Block())
        loads = [
            (raw[:, 0, :], w["L0_gnn_W"]), (raw[:, 1, :], w["L1_gnn_We_k"].rearrange("f h d -> f (h d)")),
            (raw[:, 2, :], w["L1_gnn_Ws_k"]), (raw[:, 3, :], w["L3_gnn_W_node"]),
            (raw[:, 4, :], w["L3_gnn_W_node"]), (raw[:, 5, :], w["L3_gnn_W_rel"]),
            (row[:, 0, :], w["L1_gnn_Ws_b"].unsqueeze(0)), (row[:, 1, :], w["L1_gnn_Wr_b"]),
            (emb[:], w["L3_gnn_rel_emb"].rearrange("(h p) d -> p h d", h=2)),
            (col[:, 0:1], w["L1_gnn_We_b"].rearrange("h d -> d h")),
            (n.score_w[D:P, :], w["L1_gnn_Wr_k"].rearrange("f h d -> f (h d)")),
            (n.edge_w[0:D, 0:D], w["L1_gnn_We_k"].rearrange("f h d -> f (h d)")),
            (n.edge_w[D:A, 0:D], w["L1_gnn_We_b"]),
            (n.wa[:], w["L1_gnn_Wa_k"].rearrange("d o -> o d").broadcast_to([P, D])),
            (n.wa_b[:], w["L1_gnn_Wa_b"].unsqueeze(0).broadcast_to([P, 1])),
            (n.bias0[:], w["L0_gnn_b"].unsqueeze(0).broadcast_to([P, D])),
        ]
        loads += [(col[:, 1 + c:2 + c], w["L3_gnn_attvec"][:, c * D:(c + 1) * D].rearrange("o d -> d o")) for c in range(3)]
        loads += [(n.rel_w[h * D:(h + 1) * D], w["L2_gnn_weight"].rearrange("(j h) k n -> h k j n", h=2)[h])
                  for h in range(2)]

        @block.sync
        def _(sp):
            with nc.allow_non_contiguous_dma(reason="a few short vectors"):
                for to, of in loads:
                    sp.dma_start(to, of).then_inc(loaded, 16)
            sp.wait_ge(loaded, 16 * len(loads))

        @block.tensor
        def _(pe):
            pe.wait_ge(loaded, 16 * len(loads))
            for m, r in enumerate((0, 1, 3, 5)):
                pe.transpose(turned[:, m, :], raw[:, r, :], n.ident[0:D, 0:D])
            for h in range(2):
                mm = pe.transpose(emb_p[:, h, :], emb[:, h, :], n.ident[0:RH, 0:RH])
            mm.then_inc(turns_made, 1)
            pe.matmul(vec[0:D, 0:1], lhsT=raw[:, 5, :], rhs=col[:, 3:4], start=True, stop=True).then_inc(v3_made, 1)
            pe.wait_ge(turns_copied, 1)
            pe.matmul(prod[0:D, :], lhsT=turned_s[:, 1, :], rhs=raw[:, 2, :], start=True, stop=True)
            pe.matmul(bias[:], lhsT=col[:, 0:1].broadcast_to([D, P]), rhs=raw[:, 2, :], start=True, stop=False)
            for r in range(2):
                pe.matmul(bias[:], lhsT=n.ones[0:1, 0:P], rhs=row[:, r, :], start=False, stop=(r == 1))
            for h in range(2):
                mm = pe.matmul(rel[:, h, :], lhsT=emb_t[:, h, :], rhs=turned_s[:, 3, :], start=True, stop=True)
            mm.then_inc(products_made, 1)
            pe.wait_ge(v3_copied, 1)
            pe.matmul(vec[:, 1:2], lhsT=raw[:, 3:5, :].rearrange("o c i -> o (c i)"), rhs=col[:, 2:3], start=True, stop=True)
            pe.matmul(vec[:, 2:3], lhsT=raw[:, 3:5, :].rearrange("o c i -> o (c i)"), rhs=col[:, 1:2], start=True, stop=True)
            for h in range(2):
                mm = pe.matmul(vec[0:RH, 3 + h:4 + h], lhsT=emb_t[:, h, :], rhs=v3[:], start=True, stop=True)
            mm.then_inc(last_made, 1)

        @block.vector
        def _(dve):
            link = linker(dve, dve_step, 0)
            dve.wait_ge(loaded, 16 * len(loads))
            link(nc.vector.memset(n.edge_w[:, D:A], 0.0))
            link(nc.vector.memset(n.edge_w[D:A, D:A], 1.0))
            link(nc.vector.memset(n.node_w[:], 0.0))
            link(nc.vector.memset(n.w0[:], 0.0))
            dve.wait_ge(turns_made, 1)
            link(nc.vector.tensor_copy(emb_t[:], emb_p[:]))
            link(nc.vector.tensor_copy(n.w0[0:D, 0:D], turned[:, 0, :]))
            link(nc.vector.tensor_copy(n.w0[D:P, D:P], turned[:, 0, :]))
            link(nc.vector.tensor_copy(n.node_w[0:D, :], turned[:, 2, :]))
            nc.vector.tensor_copy(turned_s[:], turned[:]).then_inc(turns_copied, 1)
            dve.wait_ge(v3_made, 1)
            nc.vector.tensor_copy(v3[:], vec[0:D, 0:1]).then_inc(v3_copied, 1)
            dve.wait_ge(products_made, 1)
            link(nc.vector.tensor_copy(n.score_w[0:D, :], prod[0:D, :]))
            link(nc.vector.tensor_copy(n.score_b[:], bias[:]))
            link(nc.vector.tensor_copy(n.rel_rows[:], rel[:]))
            dve.wait_ge(last_made, 1)
            link(nc.vector.tensor_copy(vcat[0:D, :], vec[0:D, 1:2]))
            link(nc.vector.tensor_copy(vcat[D:P, :], vec[D:P, 2:3]))
            link(nc.vector.tensor_copy(ra[:], vec[0:RH, 3:5]))
            link(nc.vector.tensor_copy(n.att_w[:], vcat[:].broadcast_to([P, A])))
            link(nc.vector.tensor_copy(n.att_rel[:], ra[:].unsqueeze(2).broadcast_to([RH, 2, A])))


def norm_phase(nc, n, base, sums, to, scale, rows, name):
    SLOTS = 6
    ctx, sb, ps, sem = phase(nc, name)
    with ctx:
        a = sb("a", [P, SLOTS, J, D])
        b = sb("b", [P, SLOTS, J, D])
        sq = sb("sq", [P, SLOTS, J, D])
        o = sb("o", [P, SLOTS, J, D])
        total = sb("total", [P, SLOTS, J])
        mean = sb("mean", [P, SLOTS, J])
        var = sb("var", [P, SLOTS, J])
        dev = sb("dev", [P, SLOTS, J])
        inv = sb("inv", [P, SLOTS, J])
        eps = sb("eps", [P, 1])

        rows_in = [sem(f"rows_in{s}") for s in range(SLOTS)]
        eps_set = sem("eps_set")
        pooled = sem("pooled")
        dve_step = sem("dve_step")
        centred = sem("centred")
        squared = sem("squared")
        var_made = sem("var_made")
        dev_made = sem("dev_made")
        inv_made = sem("inv_made")
        rows_made = sem("rows_made")
        rows_out = [sem(f"rows_out{s}") for s in range(SLOTS)]

        block = ctx.enter_context(nc.Block())
        by_part = lambda t: t.rearrange("(p g c) d -> p g (c d)", p=P, c=J)
        flat = lambda t: t.rearrange("p c d -> p (c d)")
        spread = lambda t: t.unsqueeze(2).broadcast_to([P, J, D])
        full = (N_NODES - (P - 1) * TILES) // J
        part = N_NODES - (P - 1) * TILES - full * J

        def chunks(stages):
            for step in range(NCH + max(lag for _, lag in stages)):
                for stage, lag in stages:
                    if 0 <= step - lag < NCH:
                        stage(step - lag, (step - lag) % SLOTS)

        def stores(c):
            each = [1 if rows == PAD or d > full or (d == full and not part) else 2 for d in range(c % SLOTS, c, SLOTS)]
            return sum(each)

        @block.sync
        def _(sp):
            def load(c, s):
                if c >= SLOTS:
                    sp.wait_ge(rows_made, c - SLOTS + 1)
                sp.dma_start(flat(a[:, s]), by_part(base)[:, c, :]).then_inc(rows_in[s], 16)
                sp.dma_start(flat(b[:, s]), by_part(sums)[:, c, :]).then_inc(rows_in[s], 16)

            chunks([(load, 0)])

        @block.vector
        def _(dve):
            nc.vector.memset(eps[:], EPS).then_inc(eps_set, 1)

            def centre(c, s):
                dve.wait_ge(pooled, c + 1)
                if c >= SLOTS:
                    dve.wait_ge(var_made, c - SLOTS + 1)
                link = linker(dve, dve_step, (2 if scale is None else 3) * c)
                if scale is not None:
                    link(nc.vector.tensor_tensor(a[:, s], a[:, s], b[:, s], ALU.add))
                link(nc.vector.tensor_reduce(total[:, s], a[:, s], AX_X, ALU.add))
                link(nc.vector.tensor_scalar(mean[:, s], total[:, s], 1.0 / D, None, ALU.mult))
                nc.vector.tensor_tensor(a[:, s], a[:, s], spread(mean[:, s]), ALU.subtract).then_inc(centred, 1)

            def variance(c, s):
                dve.wait_ge(squared, c + 1)
                if c >= SLOTS:
                    dve.wait_ge(dev_made, c - SLOTS + 1)
                nc.vector.tensor_reduce(var[:, s], sq[:, s], AX_X, ALU.add).then_inc(var_made, 1)

            def invert(c, s):
                dve.wait_ge(dev_made, c + 1)
                if c >= SLOTS:
                    dve.wait_ge(rows_made, c - SLOTS + 1)
                nc.vector.reciprocal(inv[:, s], dev[:, s]).then_inc(inv_made, 1)

            chunks([(centre, 1), (variance, 2), (invert, 3)])

        @block.scalar
        def _(act):
            act.wait_ge(eps_set, 1)

            def square(c, s):
                act.wait_ge(centred, c + 1)
                if c >= SLOTS:
                    act.wait_ge(var_made, c - SLOTS + 1)
                nc.scalar.activation(sq[:, s], a[:, s], ACT.Square).then_inc(squared, 1)

            def root(c, s):
                act.wait_ge(var_made, c + 1)
                if c >= SLOTS:
                    act.wait_ge(inv_made, c - SLOTS + 1)
                nc.scalar.activation(dev[:, s], var[:, s], ACT.Sqrt, bias=eps[:, 0:1], scale=1.0 / D).then_inc(dev_made, 1)

            def store(c, s):
                act.wait_ge(rows_made, c + 1)
                if rows == PAD:
                    act.dma_start(by_part(to)[:, c, :], flat(o[:, s])).then_inc(rows_out[s], 16)
                    return
                view = to[0:(P - 1) * TILES, :].rearrange("(p g c) d -> p g (c d)", p=P - 1, c=J)
                act.dma_start(view[:, c, :], flat(o[0:P - 1, s])).then_inc(rows_out[s], 16)
                left = J if c < full else part if c == full else 0
                if left:
                    first = (P - 1) * TILES + c * J
                    act.dma_start(to[first:first + left, :].rearrange("(o r) d -> o (r d)", o=1),
                                  flat(o[P - 1:P, s, 0:left])).then_inc(rows_out[s], 16)

            chunks([(square, 1), (root, 2), (store, 4)])
            for c in range(NCH, NCH + SLOTS):
                act.wait_ge(rows_out[c % SLOTS], 16 * stores(c))

        @block.gpsimd
        def _(pool):
            def rescale(c, s):
                pool.wait_ge(rows_in[s], 32 * (c // SLOTS + 1))
                nc.gpsimd.tensor_tensor(b[:, s], b[:, s], spread(scale[:, c * J:(c + 1) * J]), ALU.mult).then_inc(pooled, 1)

            def add(c, s):
                pool.wait_ge(rows_in[s], 32 * (c // SLOTS + 1))
                nc.gpsimd.tensor_tensor(a[:, s], a[:, s], b[:, s], ALU.add).then_inc(pooled, 1)

            def normalise(c, s):
                pool.wait_ge(inv_made, c + 1)
                if c >= SLOTS:
                    pool.wait_ge(rows_out[s], 16 * stores(c))
                nc.gpsimd.tensor_tensor(o[:, s], a[:, s], spread(inv[:, s]), ALU.mult).then_inc(rows_made, 1)

            chunks([(add if scale is None else rescale, 0), (normalise, 3)])


def build(nc, x, edge_fields, w, out):
    n = Net()
    ctx = ExitStack()

    def dram(name, shape, dt=F32):
        return nc.dram_tensor(name, shape, dt, kind="Internal").ap()

    def sb(name, shape, dt=F32):
        return ctx.enter_context(nc.sbuf_tensor(name, shape, dt))

    with ctx:
        n.xpad = dram("xpad", [PAD, D])
        n.y = dram("y", [PAD, D])
        n.base0 = dram("base0", [PAD, D])
        n.x1 = dram("x1", [PAD, D])
        n.x2 = dram("x2", [PAD, D])
        n.x3 = dram("x3", [PAD, D])
        n.agg_dst = dram("agg_dst", [PAD, D])
        n.agg_src = dram("agg_src", [PAD, D])
        n.sorted_dst = dram("sorted_dst", [PAD + 2, 4], I32)
        n.sorted_src = dram("sorted_src", [PAD + 2, 4], I32)
        n.degree = dram("degree", [PAD])
        n.ident = sb("ident", [P, P])
        n.ident_b = sb("ident_b", [P, P], BF16)
        n.ones = sb("ones", [P, LO])
        n.part = sb("part", [P, 2])
        n.relid = sb("relid", [P, N_REL // 2])
        n.cols_dst = sb("cols_dst", [P, NG, 3, G], I32)
        n.cols_src = sb("cols_src", [P, NG, 3, G], I32)
        n.marks_dst = sb("marks_dst", [P, NG, 3, G], BF16)
        n.marks_src = sb("marks_src", [P, NG, 3, G], BF16)
        n.falls = sb("falls", [1, 1], I32)
        n.inv = sb("inv", [P, TILES])
        n.w0 = sb("w0", [P, P])
        n.bias0 = sb("bias0", [P, D])
        n.score_w = sb("score_w", [P, D])
        n.score_b = sb("score_b", [P, D])
        n.edge_w = sb("edge_w", [D + 1, D + 1])
        n.wa = sb("wa", [P, D])
        n.wa_b = sb("wa_b", [P, 1])
        n.rel_w = sb("rel_w", [P, N_REL // 2, D])
        n.node_w = sb("node_w", [P, D])
        n.att_w = sb("att_w", [P, D + 1])
        n.rel_rows = sb("rel_rows", [RH, 2, D])
        n.att_rel = sb("att_rel", [RH, 2, D + 1])
        with ExitStack() as sorting:
            def sb2(name, shape, dt=F32):
                return sorting.enter_context(nc.sbuf_tensor(name, shape, dt))
            n.payload = sb2("payload", [P, TILES, 4], I32)
            n.before = sb2("before", [P, E])
            n.lower = sb2("lower", [P, HH])
            n.iota_lo = sb2("iota_lo", [P, LO], BF16)
            n.digit = sb2("digit", [P, 2, 2, TILES])
            n.lo = sb2("lo", [P, 2, TILES], BF16)
            n.hi256 = sb2("hi256", [P, 2, TILES], BF16)
            n.keyf = sb2("keyf", [P, 2, TILES])
            n.start = sb2("start", [HH, 2, 2, LO])
            load_phase(nc, n, edge_fields)
            histogram_phase(nc, n, x)
            sort_phase(nc, n)
            order_phase(nc, n, DST, n.sorted_dst, n.cols_dst, n.marks_dst, "order_dst")
            weights_phase(nc, n, w)
            edge_phase(nc, n, "sum", n.y, n.agg_dst, "edges0")
        order_phase(nc, n, SRC, n.sorted_src, n.cols_src, n.marks_src, "order_src")
        norm_phase(nc, n, n.base0, n.agg_dst, n.x1, n.inv, PAD, "norm0")
        edge_phase(nc, n, "gat", n.x1, n.agg_dst, "edges1")
        norm_phase(nc, n, n.x1, n.agg_dst, n.x2, None, PAD, "norm1")
        edge_phase(nc, n, "rel", n.x2, n.agg_dst, "edges2")
        norm_phase(nc, n, n.x2, n.agg_dst, n.x3, None, PAD, "norm2")
        edge_phase(nc, n, "att", n.x3, n.agg_src, "edges3")
        norm_phase(nc, n, n.x3, n.agg_src, out, None, N_NODES, "norm3")


EDGE_INS = ["src", "dst", "edge_type_16", "edge_type_200"]
WEIGHT_INS = ["L0_gnn_W", "L0_gnn_b", "L1_gnn_We_k", "L1_gnn_We_b", "L1_gnn_Ws_k", "L1_gnn_Ws_b", "L1_gnn_Wr_k",
              "L1_gnn_Wr_b", "L1_gnn_Wa_k", "L1_gnn_Wa_b", "L2_gnn_weight", "L3_gnn_W_node", "L3_gnn_W_rel",
              "L3_gnn_attvec", "L3_gnn_rel_emb"]


def kernel(**inputs):
    import concourse.bacc as bacc
    from concourse.bass_utils import run_bass_kernel_spmd

    nc = bacc.Bacc("TRN2", target_bir_lowering=False, num_devices=1)
    arrays, aps = {}, {}
    for name in ["x"] + EDGE_INS + WEIGHT_INS:
        a = np.ascontiguousarray(inputs[name])
        arrays[f"in_{name}"] = a
        aps[name] = nc.dram_tensor(f"in_{name}", a.shape, mybir.dt.from_np(a.dtype), kind="ExternalInput").ap()
    out = nc.dram_tensor("out_x", [N_NODES, D], F32, kind="ExternalOutput").ap()
    build(nc, aps["x"], [aps[name] for name in EDGE_INS], {name: aps[name] for name in WEIGHT_INS}, out)
    ran = run_bass_kernel_spmd(nc, [arrays], core_ids=[0])
    return ran.results[0]["out_x"]
```

```python
from contextlib import ExitStack

import numpy as np

import concourse.bass as bass
from concourse import mybir

ALU = mybir.AluOpType
ACT = mybir.ActivationFunctionType
AX_X = mybir.AxisListType.X
F32 = mybir.dt.float32
BF16 = mybir.dt.bfloat16
I32 = mybir.dt.int32

P = 128
D = 64
N_NODES = 50000
N_EDGES = 50000
TILES = 392
PAD = TILES * P
PAD_KEY = PAD - 1
G = 4
NG = TILES // G
PAIRS = NG // 2
E = G * P
LO = 256
HI = PAD // LO
HH = HI // 2
QA = TILES // 4
N_REL = 16
RELS = 200
RH = RELS // 2
NEG = -1.0e30
SKIP = 65536
EPS = 1e-5
SRC, DST, T16, T200 = range(4)
J = 14
NCH = TILES // J

assert PAD == HI * LO and TILES % (2 * G) == 0 and NCH % 2 == 0


class Net:
    pass


def phase(nc, name):
    ctx = ExitStack()
    sems = []

    def clear():
        nc.clear_and_free_semaphores(sems)
        nc.all_engine_barrier()

    ctx.callback(clear)

    def sb(n, shape, dt=F32):
        return ctx.enter_context(nc.sbuf_tensor(f"{name}_{n}", shape, dt))

    def ps(n, shape, dt=F32):
        return ctx.enter_context(nc.psum_tensor(f"{name}_{n}", shape, dt))

    def sem(n):
        sems.append(nc.alloc_semaphore(f"{name}_{n}"))
        return sems[-1]

    return ctx, sb, ps, sem


def linker(eng, sem, base):
    count = [0]

    def link(ins):
        count[0] += 1
        ins.then_inc(sem, 1)
        eng.wait_ge(sem, base + count[0])

    return link


def pipelined(eng, stages, unroll=1):
    def pair(i, begun):
        for s in range(2):
            for stage, lag in stages:
                turn = i + (s - lag) // 2
                if begun or 0 <= turn < PAIRS:
                    stage((s - lag) % 2, turn)

    peeled = 1 - min((0 - lag) // 2 for _, lag in stages)
    for i in range(peeled):
        pair(i, False)
    assert (PAIRS - peeled) % unroll == 0
    with eng.Fori(0, (PAIRS - peeled) // unroll) as i:
        for u in range(unroll):
            pair(i * unroll + peeled + u, True)
    for i in range(PAIRS, PAIRS + peeled - 1):
        pair(i, False)


def again(turn):
    return not (isinstance(turn, int) and turn == 0)


def node_group(table, g):
    return table.rearrange("(p g c) d -> p g (c d)", p=P, c=G)[:, bass.ds(g, 1), :].rearrange("p o f -> p (o f)")


def rows_of(tile):
    return tile.rearrange("p c d -> p (c d)")


def per_node(column, g):
    return column[:, bass.ds(g * G, G)].unsqueeze(2).broadcast_to([P, G, D])


def load_phase(nc, n, edge_fields):
    ctx, sb, ps, sem = phase(nc, "load")
    with ctx:
        iota_i = sb("iota_i", [P, LO], I32)
        part_i = sb("part_i", [P, 1], I32)
        half = sb("half", [P, 1])
        raw = sb("raw", [QA, 4, 4, P], I32)
        rawf = sb("rawf", [QA, 4, 4, P])
        after = sb("after", [QA, 4, P], I32)
        afterf = sb("afterf", [QA, 4, P])
        falls = sb("falls", [QA, 4, P])
        fall = sb("fall", [QA, 1])
        falls_p = ps("falls_p", [1, 1])
        as_given = sb("as_given", [QA, 4, P, 4], I32)
        digit_i = sb("digit_i", [P, 2, 2, TILES], I32)
        turned = ps("turned", [P, 4, 512])

        pads_set = sem("pads_set")
        pool_step = sem("pool_step")
        consts_made = sem("consts_made")
        edges_in = sem("edges_in")
        floats_made = sem("floats_made")
        fields_turned = sem("fields_turned")
        payload_made = sem("payload_made")
        after_in = sem("after_in")
        falls_made = sem("falls_made")
        falls_summed = sem("falls_summed")
        given_made = sem("given_made")
        given_out = sem("given_out")
        dve_step = sem("dve_step")

        block = ctx.enter_context(nc.Block())

        @block.gpsimd
        def _(pool):
            nc.gpsimd.memset(n.ident[:], 0.0).then_inc(pool_step, 1)
            nc.gpsimd.memset(n.before[:], 1.0).then_inc(pool_step, 1)
            nc.gpsimd.memset(n.lower[:], 1.0).then_inc(pool_step, 1)
            nc.gpsimd.memset(n.ones[:], 1.0).then_inc(consts_made, 1)
            pool.wait_ge(pool_step, 3)
            nc.gpsimd.affine_select(out=n.ident[:], in_=n.ident[:], compare_op=ALU.not_equal, fill=1.0,
                                    base=0, pattern=[[-1, P]], channel_multiplier=1).then_inc(consts_made, 1)
            nc.gpsimd.affine_select(out=n.before[:, E - P:E], in_=n.before[:, E - P:E], compare_op=ALU.is_gt,
                                    fill=0.0, base=0, pattern=[[-1, P]], channel_multiplier=1).then_inc(consts_made, 1)
            nc.gpsimd.affine_select(out=n.lower[:], in_=n.lower[:], compare_op=ALU.is_gt,
                                    fill=0.0, base=0, pattern=[[1, HH]], channel_multiplier=-1).then_inc(consts_made, 1)
            nc.gpsimd.iota(iota_i[:], pattern=[[1, LO]], base=0, channel_multiplier=0).then_inc(consts_made, 1)
            nc.gpsimd.iota(part_i[:], pattern=[[1, 1]], base=0, channel_multiplier=1).then_inc(consts_made, 1)
            pool.wait_ge(edges_in, 16 * 12)
            for f in range(4):
                nc.gpsimd.tensor_copy(as_given[:, :, :, f], raw[:, f]).then_inc(given_made, 1)

        @block.sync
        def _(sp):
            sp.wait_ge(pads_set, 3)
            whole = 3 * QA * P
            for f, a in enumerate(edge_fields):
                sp.dma_start(raw[:, f, 0:3, :], a[0:whole].rearrange("(q a c) -> a q c", q=3, c=P)).then_inc(edges_in, 16)
                rows = (N_EDGES - whole) // P
                rest = whole + rows * P
                sp.dma_start(raw[0:rows, f, 3, :], a[whole:rest].rearrange("(a c) -> a c", c=P)).then_inc(edges_in, 16)
                sp.dma_start(raw[rows:rows + 1, f, 3, 0:N_EDGES - rest],
                             a[rest:N_EDGES].rearrange("(a c) -> a c", a=1)).then_inc(edges_in, 16)
            a = edge_fields[DST]
            sp.dma_start(after[:, 0:3, :], a[1:1 + whole].rearrange("(q a c) -> a q c", q=3, c=P)).then_inc(after_in, 16)
            sp.dma_start(after[0:rows, 3, :], a[1 + whole:1 + rest].rearrange("(a c) -> a c", c=P)).then_inc(after_in, 16)
            sp.dma_start(after[rows:rows + 1, 3, 0:N_EDGES - rest - 1],
                         a[rest + 1:N_EDGES].rearrange("(a c) -> a c", a=1)).then_inc(after_in, 16)
            sp.wait_ge(given_made, 4)
            sp.dma_start(n.sorted_dst[1:PAD + 1, :].rearrange("(q a c) f -> a q (c f)", q=4, c=P),
                         as_given[:].rearrange("a q c f -> a q (c f)")).then_inc(given_out, 16)
            sp.wait_ge(given_out, 16)

        @block.tensor
        def _(pe):
            pe.wait_ge(floats_made, 1)
            pe.wait_ge(consts_made, 6)
            for f in range(4):
                for q in range(4):
                    mm = pe.transpose(turned[:, f, q * QA:(q + 1) * QA], rawf[:, f, q, :], n.ident[0:QA, 0:QA])
                mm.then_inc(fields_turned, 1)
            pe.wait_ge(falls_made, 1)
            pe.matmul(falls_p[:], lhsT=fall[:], rhs=n.ones[0:QA, 0:1], start=True, stop=True).then_inc(falls_summed, 1)

        @block.scalar
        def _(act):
            for f in range(4):
                act.wait_ge(fields_turned, f + 1)
                nc.scalar.copy(n.payload[:, :, f], turned[:, f, 0:TILES]).then_inc(payload_made, 1)

        @block.vector
        def _(dve):
            link = linker(dve, dve_step, 0)
            nc.vector.memset(raw[96:QA, SRC:DST + 1, 3, :], PAD_KEY).then_inc(pads_set, 1)
            nc.vector.memset(raw[96:QA, T16:T200 + 1, 3, :], 0).then_inc(pads_set, 1)
            nc.vector.memset(after[96:QA, 3, :], PAD_KEY).then_inc(pads_set, 1)
            dve.wait_ge(edges_in, 16 * 12)
            nc.vector.tensor_copy(rawf[:], raw[:]).then_inc(floats_made, 1)
            dve.wait_ge(consts_made, 6)
            link(nc.vector.tensor_copy(n.ident_b[:], n.ident[:]))
            link(nc.vector.tensor_copy(n.iota_lo[:], iota_i[:]))
            link(nc.vector.tensor_copy(n.part[:, 0:1], part_i[:]))
            link(nc.vector.tensor_scalar(n.part[:, 1:2], n.part[:, 0:1], float(RH), None, ALU.add))
            link(nc.vector.tensor_scalar(half[:], n.part[:, 0:1], float(D), None, ALU.is_ge))
            for j in range(N_REL // 2):
                link(nc.vector.tensor_scalar(n.relid[:, j:j + 1], half[:], float(2 * j), None, ALU.add))
            dve.wait_ge(after_in, 16 * 3)
            link(nc.vector.tensor_copy(afterf[:], after[:]))
            link(nc.vector.tensor_tensor(falls[:], rawf[:, DST], afterf[:], ALU.is_gt))
            nc.vector.tensor_reduce(fall[:], falls[:].rearrange("a q c -> a (q c)"), AX_X, ALU.add).then_inc(falls_made, 1)
            dve.wait_ge(falls_summed, 1)
            link(nc.vector.tensor_copy(n.falls[:], falls_p[:]))
            dve.wait_ge(payload_made, 4)
            for k in (SRC, DST):
                link(nc.vector.tensor_scalar(digit_i[:, k, 0, :], n.payload[:, :, k], 8, None, ALU.logical_shift_right))
                link(nc.vector.tensor_scalar(digit_i[:, k, 1, :], n.payload[:, :, k], LO - 1, None, ALU.bitwise_and))
                for d in range(2):
                    link(nc.vector.tensor_copy(n.digit[:, k, d, :], digit_i[:, k, d, :]))
                link(nc.vector.tensor_scalar(n.hi256[:, k, :], n.digit[:, k, 0, :], float(LO), None, ALU.mult))
                link(nc.vector.tensor_copy(n.lo[:, k, :], n.digit[:, k, 1, :]))
                link(nc.vector.tensor_copy(n.keyf[:, k, :], n.payload[:, :, k]))


def one_hots(eng, n, k, g, hot, digit, tiles=range(G)):
    width = HI if digit == 0 else LO
    for c in tiles:
        last = eng.tensor_scalar(hot[:, c, :], n.iota_lo[:, 0:width], n.digit[:, k, digit, bass.ds(g * G + c, 1)],
                                 None, ALU.is_equal)
    return last


def histogram_parts(nc, n, k, sb, ps, sem):
    r = Net()
    lo_hot = sb("lo_hot", [P, 2, G, LO], BF16)
    hi_hot = sb("hi_hot", [P, 2, G, HI], BF16)
    apart = sb("apart", [P, 2, G // 2, HI], BF16)
    act_tiles = (G // 2, G // 4)
    counts = sb("counts", [HH, 2, LO])
    upto = sb("upto", [HH, 2, LO])
    total = sb("total", [HH, 2])
    excl = sb("excl", [HH, 2, LO])
    hist = ps("hist", [HH, 2, LO])
    offset = ps("offset", [HH, 2])

    hots_made = sem("hots_made")
    apart_made = sem("apart_made")
    act_hots_made = sem("act_hots_made")
    hots_used = sem("hots_used")
    counts_made = sem("counts_made")
    totals_made = sem("totals_made")
    offsets_made = sem("offsets_made")
    prefix_step = sem("prefix_step")

    def vector(dve):
        def hots(s, t):
            g = 2 * t + s
            if again(t):
                dve.wait_ge(hots_used, g - 1)
            one_hots(nc.vector, n, k, g, hi_hot[:, s], 0, range(act_tiles[s], G))
            one_hots(nc.vector, n, k, g, lo_hot[:, s], 1).then_inc(hots_made, 1)

        pipelined(dve, [(hots, 0)], unroll=3)
        dve.wait_ge(hots_used, NG)
        link = linker(dve, prefix_step, 0)
        nc.vector.tensor_copy(counts[:], hist[:]).then_inc(counts_made, 1)
        dve.wait_ge(counts_made, 1)
        for h in range(2):
            link(nc.vector.tensor_tensor_scan(upto[:, h], n.ones[0:HH, 0:LO], counts[:, h], 0.0, ALU.mult, ALU.add))
        nc.vector.tensor_copy(total[:], upto[:, :, LO - 1]).then_inc(totals_made, 1)
        link(nc.vector.tensor_tensor(excl[:], upto[:], counts[:], ALU.subtract))
        dve.wait_ge(offsets_made, 1)
        for h in range(2):
            link(nc.vector.tensor_scalar(n.start[:, k, h], excl[:, h], offset[:, h:h + 1], None, ALU.add))

    def scalar(act):
        def distances(s, t):
            if s == 1:
                return
            if again(t):
                act.wait_ge(act_hots_made, 2 * t)
            for m in range(2):
                for c in range(act_tiles[m]):
                    last = nc.scalar.activation(apart[:, m, c, :], n.iota_lo[:, 0:HI], ACT.Abs, scale=-1.0,
                                                bias=n.digit[:, k, 0, bass.ds((2 * t + m) * G + c, 1)])
            last.then_inc(apart_made, 1)

        def hots(s, t):
            g = 2 * t + s
            if s == 0:
                act.wait_ge(apart_made, t + 1)
            if again(t):
                act.wait_ge(hots_used, g - 1)
            tiles = act_tiles[s]
            nc.scalar.activation(hi_hot[:, s, 0:tiles], apart[:, s, 0:tiles], ACT.Relu, scale=-1.0,
                                 bias=n.ones[:, 0:1]).then_inc(act_hots_made, 1)

        pipelined(act, [(distances, 0), (hots, 0)], unroll=3)

    def tensor(pe):
        def count(s, t):
            g = 2 * t + s
            pe.wait_ge(hots_made, g + 1)
            pe.wait_ge(act_hots_made, g + 1)
            for c in range(G):
                for h in range(2):
                    mm = pe.matmul(hist[:, h, :], lhsT=hi_hot[:, s, c, h * HH:(h + 1) * HH], rhs=lo_hot[:, s, c, :],
                                   start=not again(t) and s == 0 and c == 0 and h == 0, stop=False,
                                   skip_group_check=True)
            mm.then_inc(hots_used, 1)

        pipelined(pe, [(count, 0)], unroll=3)
        pe.wait_ge(totals_made, 1)
        pe.matmul(offset[:, 0:1], lhsT=n.lower[0:HH, :], rhs=total[:, 0:1], start=True, stop=True)
        pe.matmul(offset[:, 1:2], lhsT=n.lower[0:HH, :], rhs=total[:, 1:2], start=True, stop=False)
        pe.matmul(offset[:, 1:2], lhsT=n.ones[0:HH, 0:HH], rhs=total[:, 0:1], start=False,
                  stop=True).then_inc(offsets_made, 1)

    r.vector, r.scalar, r.tensor, r.counts, r.counts_made = vector, scalar, tensor, counts, counts_made
    return r


def fill_phase(nc, n, x):
    ctx, sb, ps, sem = phase(nc, "fill")
    with ctx:
        hist = histogram_parts(nc, n, DST, sb, ps, sem)
        zeros = sb("zeros", [P, TILES // 7 * D])
        minus = sb("minus", [1, 4], I32)

        zeros_set = sem("zeros_set")
        filled = sem("filled")
        stored = sem("stored")

        block = ctx.enter_context(nc.Block())

        @block.vector
        def _(dve):
            hist.vector(dve)

        @block.scalar
        def _(act):
            hist.scalar(act)

        @block.tensor
        def _(pe):
            hist.tensor(pe)

        @block.gpsimd
        def _(pool):
            nc.gpsimd.memset(zeros[:], 0.0).then_inc(zeros_set, 1)
            nc.gpsimd.memset(minus[:], -1).then_inc(zeros_set, 1)

        @block.sync
        def _(sp):
            split = lambda t: t.rearrange("(p r) d -> p (r d)", p=400)
            sp.dma_start(split(n.xpad[0:N_NODES, :]), split(x)).then_inc(filled, 16)
            sp.wait_ge(zeros_set, 2)
            pad_rows = PAD - N_NODES
            sp.dma_start(n.xpad[N_NODES:PAD, :].rearrange("(p r) d -> p (r d)", r=2),
                         zeros[0:pad_rows // 2, 0:2 * D]).then_inc(filled, 16)
            for table in (n.agg_dst, n.agg_src):
                view = table.rearrange("(p c r) d -> c p (r d)", p=P, c=7)
                for c in range(7):
                    sp.dma_start(view[c], zeros[:]).then_inc(filled, 16)
            for table in (n.sorted_dst, n.sorted_src):
                sp.dma_start(table[0:1, :], minus[:]).then_inc(filled, 16)
                sp.dma_start(table[PAD + 1:PAD + 2, :], minus[:]).then_inc(filled, 16)
            sp.wait_ge(hist.counts_made, 1)
            sp.dma_start(n.degree.rearrange("(h p l) -> p h l", h=2, l=LO), hist.counts[:]).then_inc(stored, 16)
            sp.wait_ge(stored, 16)
            sp.wait_ge(filled, 16 * (2 + 14 + 4))


def prepare_phase(nc, n, w):
    SLOTS = 6
    ctx, sb, ps, sem = phase(nc, "prepare")
    with ctx:
        hist = histogram_parts(nc, n, SRC, sb, ps, sem)
        weights = weights_parts(nc, n, w, sb, ps, sem)
        degree = sb("degree_in", [P, TILES])
        y = sb("y", [P, SLOTS, J, D])

        degree_in = sem("degree_in")
        root_made = sem("root_made")
        inv_made = sem("inv_made")
        x_in = [sem(f"x_in{s}") for s in range(SLOTS)]
        y_made = sem("y_made")
        y_out = [sem(f"y_out{s}") for s in range(SLOTS)]

        block = ctx.enter_context(nc.Block())
        by_part = lambda t: t.rearrange("(p g c) d -> p g (c d)", p=P, c=J)

        @block.sync
        def _(sp):
            def load(c):
                s = c % SLOTS
                if c >= SLOTS:
                    sp.wait_ge(y_out[s], 16 * (c // SLOTS))
                sp.dma_start(rows_of(y[:, s]), by_part(n.xpad)[:, c, :]).then_inc(x_in[s], 16)

            def store(c):
                sp.wait_ge(y_made, c + 1)
                sp.dma_start(by_part(n.y)[:, c, :], rows_of(y[:, c % SLOTS])).then_inc(y_out[c % SLOTS], 16)

            sp.dma_start(degree[:], n.degree.rearrange("(p t) -> p t", p=P)).then_inc(degree_in, 16)
            for c in range(3):
                load(c)
            weights.sync(sp)
            for c in range(NCH):
                if c + 3 < NCH:
                    load(c + 3)
                store(c)
            for s in range(SLOTS):
                sp.wait_ge(y_out[s], 16 * len(range(s, NCH, SLOTS)))

        @block.scalar
        def _(act):
            act.wait_ge(degree_in, 16)
            nc.scalar.activation(n.root[:], degree[:], ACT.Sqrt, bias=n.ones[:, 0:1]).then_inc(root_made, 1)
            hist.scalar(act)

        @block.vector
        def _(dve):
            dve.wait_ge(root_made, 1)
            nc.vector.reciprocal(n.inv[:], n.root[:]).then_inc(inv_made, 1)
            dve.wait_ge(inv_made, 1)
            nc.vector.tensor_tensor(n.inv_deg[:], n.inv[:], n.inv[:], ALU.mult)
            hist.vector(dve)
            weights.vector(dve)

        @block.tensor
        def _(pe):
            hist.tensor(pe)
            weights.tensor(pe)

        @block.gpsimd
        def _(pool):
            pool.wait_ge(inv_made, 1)
            for c in range(NCH):
                s = c % SLOTS
                pool.wait_ge(x_in[s], 16 * (c // SLOTS + 1))
                nc.gpsimd.tensor_tensor(y[:, s], y[:, s], n.inv[:, c * J:(c + 1) * J].unsqueeze(2).broadcast_to([P, J, D]),
                                        ALU.mult).then_inc(y_made, 1)


def sort_parts(nc, n, k, table, sb, ps, sem, deep):
    r = Net()
    slots = 2 if deep else 1
    lo_hot = sb("lo_hot", [P, 2, G, LO], BF16)
    hi_hot = sb("hi_hot", [P, 2, G, HI], BF16)
    hi_turned = sb("hi_turned", [HH, 2, 2 * G, P], BF16)
    free_hi = sb("free_hi", [HH, 2, 2, LO], BF16)
    free_lo = sb("free_lo", [HH, 2, 2, LO], BF16)
    picked = sb("picked", [P, G, LO])
    matched = sb("matched", [P, G, E])
    base = sb("base", [P, 2, G])
    rank = sb("rank", [P, 2, G])
    place = sb("place", [P, 2, G], I32)
    moved = sb("moved", [P, 2, G, 4], I32)
    running = ps("running", [HH, 2, LO])
    turned = ps("hi_turns", [HH, 2 * G, P], BF16)
    keys = [ps(f"keys{s}", [P, G, P]) for s in range(slots)]
    found = [ps(f"found{s}", [P, G, LO]) for s in range(slots)]

    hi_hots_made = sem("hi_hots_made")
    lo_hots_made = sem("lo_hots_made")
    turns_made = sem("hi_turns_made")
    turns_copied = sem("hi_turns_copied")
    free_hi_made = sem("free_hi_made")
    free_made = sem("free_made")
    found_made = sem("found_made")
    updated = sem("updated")
    picks_made = sem("picks_made")
    places_made = sem("places_made")
    payload_staged = sem("payload_staged")
    scatter_begun = sem("sort_begun")
    scattered = [sem(f"sort_scattered{s}") for s in range(2)]

    def vector(dve):
        def hi_hots(s, t):
            g = 2 * t + s
            if again(t):
                dve.wait_ge(updated, g)
            one_hots(nc.vector, n, k, g, hi_hot[:, s], 0).then_inc(hi_hots_made, 1)

        def lo_hots(s, t):
            g = 2 * t + s
            if again(t):
                dve.wait_ge(updated, g)
            one_hots(nc.vector, n, k, g, lo_hot[:, s], 1).then_inc(lo_hots_made, 1)

        def split(s, t):
            g = 2 * t + s
            dve.wait_ge(free_hi_made, g + 1)
            if again(t):
                dve.wait_ge(found_made, g - 1)
            nc.vector.tensor_tensor(free_lo[:, s], running[:], free_hi[:, s], ALU.subtract).then_inc(free_made, 1)

        def places(s, t):
            g = 2 * t + s
            dve.wait_ge(found_made, g + 1)
            if again(t):
                dve.wait_ge(scattered[s], 64 * t)
            for c in range(G):
                nc.vector.tensor_tensor_reduce(picked[:, c], found[s % slots][:, c], lo_hot[:, s, c], 1.0, 0.0,
                                               ALU.mult, ALU.add, base[:, s, c:c + 1])
                last = nc.vector.scalar_tensor_tensor(
                    matched[:, c, 0:(c + 1) * P], keys[s % slots][:, 0:c + 1, :].rearrange("p c e -> p (c e)"),
                    n.keyf[:, k, bass.ds(g * G + c, 1)], n.before[:, (G - 1 - c) * P:E],
                    ALU.is_equal, ALU.mult, accum_out=rank[:, s, c:c + 1])
            last.then_inc(picks_made, 1)
            dve.wait_ge(picks_made, g + 1)
            nc.vector.scalar_tensor_tensor(place[:, s], base[:, s], 1.0, rank[:, s],
                                           ALU.add, ALU.add).then_inc(places_made, 1)

        if deep:
            return [(split, 1), (hi_hots, 0), (places, 2), (lo_hots, 0)]
        return [(places, 2), (lo_hots, 0), (split, 1), (hi_hots, 0)]

    def tensor(pe):
        def turns(s, t):
            g = 2 * t + s
            pe.wait_ge(hi_hots_made, g + 1)
            if again(t) or s == 1:
                pe.wait_ge(turns_copied, g)
            for c in range(G):
                for h in range(2):
                    mm = pe.transpose(turned[:, 2 * c + h, :], hi_hot[:, s, c, h * HH:(h + 1) * HH], n.ident_b[:])
            mm.then_inc(turns_made, 1)

        def lookups(s, t):
            g = 2 * t + s
            if deep:
                if again(t):
                    pe.wait_ge(places_made, g - 1)
            elif again(t) or s == 1:
                pe.wait_ge(places_made, g)
            for c in range(G):
                col = bass.ds(g * G + c, 1)
                pe.matmul(keys[s % slots][:, c, :], lhsT=n.hi256[:, k, col].broadcast_to([P, P]), rhs=n.ident_b[:],
                          start=True, stop=False)
                pe.matmul(keys[s % slots][:, c, :], lhsT=n.lo[:, k, col].broadcast_to([P, P]), rhs=n.ident_b[:],
                          start=False, stop=True)
            pe.wait_ge(turns_copied, g + 1)
            pe.wait_ge(free_made, g + 1)
            for c in range(G):
                for h in range(2):
                    for part in (free_hi, free_lo):
                        mm = pe.matmul(found[s % slots][:, c, :], lhsT=hi_turned[:, s, 2 * c + h, :],
                                       rhs=part[:, s, h, :], start=(h == 0 and part is free_hi),
                                       stop=(h == 1 and part is free_lo))
            mm.then_inc(found_made, 1)
            pe.wait_ge(lo_hots_made, g + 1)
            for c in range(G):
                for h in range(2):
                    mm = pe.matmul(running[:, h, :], lhsT=hi_hot[:, s, c, h * HH:(h + 1) * HH],
                                   rhs=lo_hot[:, s, c, :], start=False, stop=False, skip_group_check=True)
            mm.then_inc(updated, 1)

        for h in range(2):
            mm = pe.matmul(running[:, h, :], lhsT=n.ident[0:HH, 0:HH], rhs=n.start[:, k, h, :],
                           start=(h == 0), stop=False, skip_group_check=True)
        mm.then_inc(updated, 1)
        return [(lookups, 1), (turns, 0)]

    def scalar(act):
        def copies(s, t):
            g = 2 * t + s
            act.wait_ge(turns_made, g + 1)
            if again(t):
                act.wait_ge(found_made, g - 1)
            nc.scalar.copy(hi_turned[:, s], turned[:]).then_inc(turns_copied, 1)

        def free(s, t):
            g = 2 * t + s
            act.wait_ge(updated, g + 1)
            nc.scalar.copy(free_hi[:, s], running[:]).then_inc(free_hi_made, 1)

        def stage(s, t):
            g = 2 * t + s
            if again(t):
                act.wait_ge(scattered[s], 64 * t)
            nc.scalar.copy(moved[:, s], n.payload[:, bass.ds(g * G, G), :]).then_inc(payload_staged, 1)

        return [(free, 0), (copies, 0), (stage, 2)]

    def gpsimd(pool, last_row):
        def scatter(s, t):
            g = 2 * t + s
            pool.wait_ge(places_made, g + 1)
            pool.wait_ge(payload_staged, g + 1)
            pool.sem_inc(scatter_begun, 1)
            for c in range(G):
                pool.indirect_dma_start(out=table, out_offset=bass.IndirectOffsetOnAxis(ap=place[:, s, c:c + 1], axis=0),
                                        in_=moved[:, s, c, :], in_offset=None,
                                        bounds_check=last_row, oob_is_err=False).then_inc(scattered[s], 16)

        return [(scatter, 3)]

    def finish(pool):
        for s in range(2):
            pool.wait_ge(scattered[s], 64 * PAIRS)

    r.vector, r.tensor, r.scalar, r.gpsimd, r.finish = vector, tensor, scalar, gpsimd, finish
    return r


def sort_phase(nc, n):
    ctx, sb, ps, sem = phase(nc, "sort")
    with ctx:
        sort = sort_parts(nc, n, DST, n.sorted_dst, sb, ps, sem, True)
        block = ctx.enter_context(nc.Block())

        def if_unsorted(eng, name):
            falls = eng.alloc_register(f"falls_{name}")
            eng.load(falls, n.falls[0:1, 0:1])
            return eng.If_ne(falls, 0)

        @block.vector
        def _(dve):
            with if_unsorted(dve, "dve"):
                pipelined(dve, sort.vector(dve))

        @block.scalar
        def _(act):
            with if_unsorted(act, "act"):
                pipelined(act, sort.scalar(act))

        @block.tensor
        def _(pe):
            with if_unsorted(pe, "pe"):
                pipelined(pe, sort.tensor(pe))

        @block.gpsimd
        def _(pool):
            with if_unsorted(pool, "pool"):
                last_row = pool.to_reg(PAD + 1)
                pipelined(pool, sort.gpsimd(pool, last_row))
                sort.finish(pool)


def edge_phase(nc, n, kind, rows, agg, name):
    A = D + 1
    soft = kind in ("gat", "att")
    ends = 2 if soft else 1
    wide = D if kind == "sum" else P
    order, marks = (n.cols_src, n.marks_src) if kind == "att" else (n.cols_dst, n.marks_dst)
    SRC_COL, KEY_COL = 0, 1
    F = A if soft else D
    LATE = 4 if kind == "rel" else 3

    ctx, sb, ps, sem = phase(nc, name)
    with ctx:
        gcol = sb("gcol", [P, 2, 2, G], I32)
        scol = sb("scol", [P, 2, G], I32)
        mark = sb("mark", [P, 2, 3, G], BF16)
        got = sb("got", [P, 2, G, P if kind in ("sum",) else ends * D])
        feat = sb("feat", [wide, 2, E])
        state = sb("state", [P if kind == "sum" else F, 2, E])
        outs = sb("outs", [P, 2, G, D])
        turned = [ps(f"turned{s}", [P if kind == "sum" else ends * D, G, P]) for s in range(1 if kind == "sum" else 2)]
        turned = turned * (3 - len(turned))
        keep = ps("keep", [F, G, P])
        back = ps("back", [P, G, P if kind == "sum" else A if soft else D])
        if kind == "sum":
            sort = sort_parts(nc, n, SRC, n.sorted_src, sb, ps, sem, False)
            xin = sb("xin", [P, 2, G, D])
            base = sb("own_base", [P, 2, G, D])
            own_in = [sem(f"own_in{s}") for s in range(2)]
            x_in = [sem(f"x_in{s}") for s in range(2)]
            base_step = sem("base_step")
            base_made = sem("base_made")
            base_out = [sem(f"base_out{s}") for s in range(2)]
        if kind != "sum":
            keep_s = sb("keep_s", [F, 2, E])
        if kind in ("rel", "att"):
            types = ps("types", [P, G, P])
            msg = [ps(f"msg{s}", [D, E]) for s in range(2)]
        if kind == "rel":
            masked = sb("masked", [P, 2, N_REL // 2, E])
        if kind == "att":
            hot = sb("hot", [RH, 2, 2, E])
            raw_score = sb("raw_score", [A, E])
            score = sb("score", [A, 2, E])
        if kind == "gat":
            pre = ps("pre", [P, G, D])
            z = sb("z", [P, 2, G, D])
            clamped = sb("clamped", [P, 2, G, D])
            u = sb("u", [P, 2, G, D])
            t2 = sb("t2", [P, G, D])
            den = sb("den", [P, G, D])
            mish = sb("mish", [P, 2, G, D])
            logit = sb("logit", [P, 2, G])
        if soft:
            score_p = ps("score_p", [A, G, P])
            top = sb("top", [A, 2, E + 1])
            drop = sb("drop", [A, 2, E])
            below = sb("below", [A, 2, E])
            decay = sb("decay", [A, 2, E])
            weight = sb("weight", [A, 2, E])
            inv_den = sb("inv_den", [P, 2, G])

        gcol_in = [sem(f"gcol_in{s}") for s in range(2)]
        mark_in = [sem(f"mark_in{s}") for s in range(2)]
        scol_in = [sem(f"scol_in{s}") for s in range(2)]
        gathered = [sem(f"gathered{s}") for s in range(2)]
        scattered = [sem(f"scattered{s}") for s in range(2)]
        pool_begun = sem("pool_begun")
        turns_made = sem("turns_made")
        feat_made = sem("feat_made")
        keep_copied = sem("keep_copied")
        start_set = sem("start_set")
        scanned = sem("scanned")
        back_begun = sem("back_begun")
        back_made = sem("back_made")
        outs_made = sem("outs_made")
        if kind in ("rel", "att"):
            picked = sem("picked")
            msg_made = sem("msg_made")
        if kind == "att":
            score_in = sem("score_in")
            score_made = sem("score_made")
            raw_copied = sem("raw_copied")
        if kind == "gat":
            pre_made = sem("pre_made")
            z_made = sem("z_made")
            clamp_made = sem("clamp_made")
            u_made = sem("u_made")
            mish_step = sem("mish_step")
            logits_made = sem("logits_made")
            score_in = sem("score_in")
        if soft:
            top_step = sem("top_step")
            drop_made = sem("drop_made")
            below_made = sem("below_made")
            decay_made = sem("decay_made")
            weight_made = sem("weight_made")
            weighted = sem("weighted")
            den_made = sem("den_made")

        flat = lambda a: a.rearrange("p c e -> p (c e)")
        block = ctx.enter_context(nc.Block())

        @block.sync
        def _(sp):
            def gather_cols(s, t):
                g = 2 * t + s
                if again(t):
                    sp.wait_ge(gathered[s], 64 * ends * t)
                sp.dma_start(gcol[:, s], order[:, bass.ds(g, 1), 0:2, :].rearrange("p o f c -> p (o f c)")
                             .rearrange("p (f c) -> p f c", f=2)).then_inc(gcol_in[s], 16)
                if again(t):
                    sp.wait_ge(turns_made, g - 1)
                sp.dma_start(mark[:, s], marks[:, bass.ds(g, 1), :, :].rearrange("p o f c -> p (o f c)")
                             .rearrange("p (f c) -> p f c", f=3)).then_inc(mark_in[s], 16)

            def scatter_cols(s, t):
                g = 2 * t + s
                if again(t):
                    sp.wait_ge(scattered[s], 64 * t)
                sp.dma_start(scol[:, s], order[:, bass.ds(g, 1), 2, :].rearrange("p o c -> p (o c)")).then_inc(scol_in[s], 16)

            def own_rows(s, t):
                g = 2 * t + s
                sp.dma_start(got[:, s, :, D:P], n.y.rearrange("(p g c) d -> p g c d", p=P, c=G)[:, bass.ds(g, 1)]
                             .rearrange("p o c d -> p (o c) d")).then_inc(own_in[s], 16)

            def x_rows(s, t):
                g = 2 * t + s
                if again(t):
                    sp.wait_ge(base_made, g - 1)
                sp.dma_start(rows_of(xin[:, s]), node_group(n.xpad, g)).then_inc(x_in[s], 16)

            def base_rows(s, t):
                g = 2 * t + s
                sp.wait_ge(base_made, g + 1)
                sp.dma_start(node_group(n.base0, g), rows_of(base[:, s])).then_inc(base_out[s], 16)

            stages = [(scatter_cols, LATE), (gather_cols, 0)]
            if kind == "sum":
                stages = [(scatter_cols, LATE), (gather_cols, 0), (own_rows, 0), (x_rows, 1), (base_rows, 3)]
            pipelined(sp, stages)
            if kind == "sum":
                for s in range(2):
                    sp.wait_ge(base_out[s], 16 * PAIRS)

        @block.gpsimd
        def _(pool):
            last_row = pool.to_reg(PAD - 1)

            def gather(s, t):
                g = 2 * t + s
                pool.wait_ge(gcol_in[s], 16 * t + 16)
                if again(t):
                    pool.wait_ge(turns_made, g - 1)
                pool.sem_inc(pool_begun, 1)
                for m, col in enumerate((SRC_COL, KEY_COL)[:ends]):
                    for c in range(G):
                        pool.indirect_dma_start(
                            out=got[:, s, c, m * D:(m + 1) * D], out_offset=None, in_=rows,
                            in_offset=bass.IndirectOffsetOnAxis(ap=gcol[:, s, col, c:c + 1], axis=0),
                            bounds_check=last_row, oob_is_err=False).then_inc(gathered[s], 16)

            def scatter(s, t):
                g = 2 * t + s
                pool.wait_ge(scol_in[s], 16 * t + 16)
                pool.wait_ge(outs_made, g + 1)
                pool.sem_inc(pool_begun, 1)
                for c in range(G):
                    pool.indirect_dma_start(
                        out=agg, out_offset=bass.IndirectOffsetOnAxis(ap=scol[:, s, c:c + 1], axis=0),
                        in_=outs[:, s, c, :], in_offset=None,
                        bounds_check=last_row, oob_is_err=False).then_inc(scattered[s], 16)

            if kind == "sum":
                pipelined(pool, [(gather, 0), (scatter, LATE)] + sort.gpsimd(pool, pool.to_reg(PAD + 1)))
                sort.finish(pool)
            else:
                pipelined(pool, [(gather, 0), (scatter, LATE)])
            for s in range(2):
                pool.wait_ge(scattered[s], 64 * PAIRS)

        @block.tensor
        def _(pe):
            def turn(s, t):
                g = 2 * t + s
                pe.wait_ge(gathered[s], 64 * ends * (t + 1))
                pe.wait_ge(mark_in[s], 16 * t + 16)
                if kind == "sum":
                    pe.wait_ge(own_in[s], 16 * (t + 1))
                    if again(t) or s == 1:
                        pe.wait_ge(feat_made, g)
                elif again(t):
                    pe.wait_ge(feat_made, g - 1)
                if again(t) or s == 1:
                    if kind == "sum":
                        pe.wait_ge(scanned, g)
                    else:
                        pe.wait_ge(keep_copied, g)
                m = 1 if soft else 0
                for c in range(G):
                    pe.matmul(keep[:, c, :], lhsT=mark[:, s, m, c:c + 1].broadcast_to([P, F]), rhs=n.ident_b[:],
                              start=True, stop=True)
                if kind in ("rel", "att"):
                    if again(t) or s == 1:
                        pe.wait_ge(picked, g)
                    for c in range(G):
                        pe.matmul(types[:, c, :], lhsT=mark[:, s, 2, c:c + 1].broadcast_to([P, P]),
                                  rhs=n.ident_b[:], start=True, stop=True)
                for c in range(G):
                    mm = pe.transpose(turned[s][:, c, :], got[:, s, c, :], n.ident[:])
                mm.then_inc(turns_made, 1)

            def relate(s, t):
                g = 2 * t + s
                pe.wait_ge(picked, g + 1)
                if again(t):
                    pe.wait_ge(scanned, g - 1)
                for j in range(N_REL // 2):
                    mm = pe.matmul(msg[s][:], lhsT=n.rel_w[:, j, :], rhs=masked[:, s, j, :],
                                   start=(j == 0), stop=(j == N_REL // 2 - 1))
                mm.then_inc(msg_made, 1)

            def attend(s, t):
                g = 2 * t + s
                pe.wait_ge(feat_made, g + 1)
                pe.wait_ge(picked, g + 1)
                if again(t) or s == 1:
                    pe.wait_ge(score_made, g)
                if again(t):
                    pe.wait_ge(weighted, g - 1)
                sp_flat = flat(score_p[:])
                pe.matmul(sp_flat, lhsT=n.att_w[:], rhs=feat[:, s], start=True, stop=False)
                for h in range(2):
                    mm = pe.matmul(sp_flat, lhsT=n.att_rel[:, h, :], rhs=hot[:, s, h, :], start=False, stop=(h == 1))
                mm.then_inc(score_in, 1)
                pe.matmul(msg[s][:], lhsT=n.node_w[:], rhs=feat[:, s], start=True, stop=False)
                for h in range(2):
                    mm = pe.matmul(msg[s][:], lhsT=n.rel_rows[:, h, :], rhs=hot[:, s, h, :], start=False, stop=(h == 1))
                mm.then_inc(msg_made, 1)

            def preact(s, t):
                g = 2 * t + s
                pe.wait_ge(feat_made, g + 1)
                if again(t) or s == 1:
                    pe.wait_ge(clamp_made, g)
                for c in range(G):
                    mm = pe.matmul(pre[:, c, :], lhsT=feat[:, s, c * P:(c + 1) * P], rhs=n.score_w[:],
                                   start=True, stop=True)
                mm.then_inc(pre_made, 1)

            def spread(s, t):
                g = 2 * t + s
                pe.wait_ge(logits_made, g + 1)
                if again(t) or s == 1:
                    pe.wait_ge(below_made, g)
                for c in range(G):
                    mm = pe.matmul(score_p[:, c, :], lhsT=logit[:, s, c:c + 1].broadcast_to([P, A]), rhs=n.ident[:],
                                   start=True, stop=True)
                mm.then_inc(score_in, 1)

            def turn_back(s, t):
                g = 2 * t + s
                pe.wait_ge(scanned, g + 1)
                if again(t) or s == 1:
                    pe.wait_ge(outs_made, g)
                pe.sem_inc(back_begun, 1)
                for c in range(G):
                    part = state[:, s, c * P:(c + 1) * P]
                    if kind in ("sum", "gat"):
                        mm = pe.matmul(back[:, c, :], lhsT=part, rhs=n.w0[:] if kind == "sum" else n.edge_w[:],
                                       start=True, stop=True)
                    else:
                        mm = pe.transpose(back[:, c, :], part, n.ident[0:F, 0:F])
                mm.then_inc(back_made, 1)

            pipelined(pe, {
                "sum": [(turn, 0), (turn_back, 1)] + (sort.tensor(pe) if kind == "sum" else []),
                "gat": [(turn, 0), (spread, 1), (preact, 0), (turn_back, 1)],
                "rel": [(turn, 0), (relate, 1), (turn_back, 2)],
                "att": [(turn, 0), (attend, 0), (turn_back, 1)],
            }[kind])

        @block.scalar
        def _(act):
            def copies(s, t):
                g = 2 * t + s
                act.wait_ge(turns_made, g + 1)
                if again(t):
                    act.wait_ge(scanned if kind == "sum" else picked if kind == "rel" else weighted, g - 1)
                    if kind == "gat":
                        act.wait_ge(pre_made, g - 1)
                    if kind == "att":
                        act.wait_ge(msg_made, g - 1)
                if kind == "sum":
                    if again(t):
                        act.wait_ge(back_made, g - 1)
                    nc.scalar.copy(state[D:P, s], flat(turned[s][D:P]))
                if kind == "rel":
                    nc.scalar.copy(feat[D:P, s], flat(turned[s][:]))
                nc.scalar.copy(feat[0:ends * D, s], flat(turned[s][0:ends * D])).then_inc(feat_made, 1)
                if kind != "sum":
                    if again(t):
                        act.wait_ge(scanned, g - 1)
                    nc.scalar.copy(keep_s[:, s], flat(keep[:])).then_inc(keep_copied, 1)

            def raw_scores(s, t):
                g = 2 * t + s
                act.wait_ge(score_in, g + 1)
                if again(t) or s == 1:
                    act.wait_ge(score_made, g)
                nc.scalar.copy(raw_score[:], flat(score_p[:])).then_inc(raw_copied, 1)

            def exps(s, t):
                g = 2 * t + s
                act.wait_ge(drop_made, g + 1)
                act.wait_ge(below_made, g + 1)
                if again(t):
                    act.wait_ge(scanned, g - 1)
                nc.scalar.activation(weight[:, s], below[:, s], ACT.Exp).then_inc(weight_made, 1)
                nc.scalar.activation(decay[:, s], drop[:, s], ACT.Exp).then_inc(decay_made, 1)

            def exp_z(s, t):
                g = 2 * t + s
                act.wait_ge(clamp_made, g + 1)
                if again(t):
                    act.wait_ge(logits_made, g - 1)
                nc.scalar.activation(u[:, s], clamped[:, s], ACT.Exp).then_inc(u_made, 1)

            if kind == "sum":
                pipelined(act, [(copies, 0)] + sort.scalar(act))
            elif kind == "rel":
                pipelined(act, [(copies, 0)])
            elif kind == "gat":
                pipelined(act, [(copies, 0), (exps, 1), (exp_z, 0)])
            else:
                pipelined(act, [(copies, 0), (exps, 1), (raw_scores, 0)])

        @block.vector
        def _(dve):
            nc.vector.memset(state[0:F, 1, E - 1:E], 0.0).then_inc(start_set, 1)
            if soft:
                nc.vector.memset(top[:, 1, E:E + 1], 0.0).then_inc(start_set, 1)
            dve.wait_ge(start_set, 2 if soft else 1)

            def scan(s, t):
                g = 2 * t + s
                if again(t):
                    dve.wait_ge(back_made, g - 1)
                if again(t) or s == 1:
                    dve.wait_ge(scanned, g)
                first = state[0:F, 1 - s, E - 1:E]
                if kind == "sum":
                    dve.wait_ge(feat_made, g + 1)
                    ins = nc.vector.tensor_tensor_scan(state[0:F, s], flat(keep[:]), feat[:, s], first, ALU.mult, ALU.add)
                elif kind == "rel":
                    dve.wait_ge(keep_copied, g + 1)
                    dve.wait_ge(msg_made, g + 1)
                    ins = nc.vector.tensor_tensor_scan(state[:, s], keep_s[:, s], msg[s][:], first, ALU.mult, ALU.add)
                else:
                    dve.wait_ge(decay_made, g + 1)
                    dve.wait_ge(weighted, g + 1)
                    ins = nc.vector.tensor_tensor_scan(state[:, s], decay[:, s], weight[:, s], first, ALU.mult, ALU.add)
                ins.then_inc(scanned, 1)

            def finish(s, t):
                g = 2 * t + s
                dve.wait_ge(back_made, g + 1)
                if again(t):
                    dve.wait_ge(scattered[s], 64 * t)
                if kind == "sum":
                    link = linker(dve, base_step, 2 * g)
                    dve.wait_ge(x_in[s], 16 * t + 16)
                    if again(t):
                        dve.wait_ge(base_out[s], 16 * t)
                    link(nc.vector.tensor_tensor(base[:, s], xin[:, s], n.bias0[:].unsqueeze(1).broadcast_to([P, G, D]),
                                                 ALU.add))
                    link(nc.vector.tensor_tensor(base[:, s], base[:, s], per_node(n.root, g), ALU.mult))
                    nc.vector.tensor_tensor(base[:, s], base[:, s], back[:, :, D:P], ALU.add).then_inc(base_made, 1)
                if not soft:
                    nc.vector.tensor_copy(outs[:, s], back[:, :, 0:D]).then_inc(outs_made, 1)
                    return
                link = linker(dve, den_made, (2 if kind == "att" else 1) * g)
                if kind == "att":
                    link(nc.vector.tensor_scalar(inv_den[:, s], back[:, :, D], 1e-12, None, ALU.add))
                    link(nc.vector.reciprocal(inv_den[:, s], inv_den[:, s]))
                else:
                    link(nc.vector.reciprocal(inv_den[:, s], back[:, :, D]))
                nc.vector.tensor_tensor(outs[:, s], back[:, :, 0:D], inv_den[:, s].unsqueeze(2).broadcast_to([P, G, D]),
                                        ALU.mult).then_inc(outs_made, 1)

            def mask(s, t):
                g = 2 * t + s
                dve.wait_ge(feat_made, g + 1)
                if again(t):
                    dve.wait_ge(msg_made, g - 1)
                for j in range(N_REL // 2):
                    ins = nc.vector.scalar_tensor_tensor(masked[:, s, j, :], flat(types[:]), n.relid[:, j:j + 1],
                                                         feat[:, s], ALU.is_equal, ALU.mult)
                ins.then_inc(picked, 1)

            def hots(s, t):
                g = 2 * t + s
                dve.wait_ge(turns_made, g + 1)
                if again(t):
                    dve.wait_ge(msg_made, g - 1)
                for h in range(2):
                    ins = nc.vector.tensor_scalar(hot[:, s, h, :], flat(types[0:RH]), n.part[0:RH, h:h + 1], None, ALU.is_equal)
                ins.then_inc(picked, 1)

            def leaky(s, t):
                g = 2 * t + s
                dve.wait_ge(raw_copied, g + 1)
                if again(t):
                    dve.wait_ge(below_made, g - 1)
                nc.vector.scalar_tensor_tensor(score[:, s], flat(score_p[:]), 0.2, raw_score[:], ALU.mult,
                                               ALU.max).then_inc(score_made, 1)

            def tops(s, t):
                g = 2 * t + s
                link = linker(dve, top_step, 3 * g)
                if again(t):
                    dve.wait_ge(decay_made, g - 1)
                if kind == "gat":
                    dve.wait_ge(score_in, g + 1)
                    sc = flat(score_p[:])
                else:
                    dve.wait_ge(score_made, g + 1)
                    sc = score[:, s]
                dve.wait_ge(keep_copied, g + 1)
                link(nc.vector.tensor_copy(top[:, s, 0:1], top[:, 1 - s, E:E + 1]))
                link(nc.vector.tensor_tensor_scan(top[:, s, 1:E + 1], keep_s[:, s], sc, top[:, s, 0:1], ALU.add, ALU.max))
                link(nc.vector.tensor_tensor(drop[:, s], top[:, s, 0:E], keep_s[:, s], ALU.add))
                nc.vector.tensor_tensor(drop[:, s], drop[:, s], top[:, s, 1:E + 1], ALU.subtract).then_inc(drop_made, 1)
                nc.vector.tensor_tensor(below[:, s], sc, top[:, s, 1:E + 1], ALU.subtract).then_inc(below_made, 1)

            def weigh(s, t):
                g = 2 * t + s
                dve.wait_ge(weight_made, g + 1)
                other = feat[0:D, s] if kind == "gat" else msg[s][:]
                nc.vector.tensor_tensor(weight[0:D, s], weight[0:D, s], other, ALU.mult).then_inc(weighted, 1)

            def clamp(s, t):
                g = 2 * t + s
                dve.wait_ge(pre_made, g + 1)
                if again(t):
                    dve.wait_ge(u_made, g - 1)
                nc.vector.tensor_tensor(z[:, s], pre[:], n.score_b[:].unsqueeze(1).broadcast_to([P, G, D]),
                                        ALU.add).then_inc(z_made, 1)
                dve.wait_ge(z_made, g + 1)
                nc.vector.tensor_scalar(clamped[:, s], z[:, s], 20.0, None, ALU.min).then_inc(clamp_made, 1)

            def logits(s, t):
                g = 2 * t + s
                dve.wait_ge(u_made, g + 1)
                if again(t):
                    dve.wait_ge(score_in, g - 1)
                link = linker(dve, mish_step, 7 * g)
                link(nc.vector.scalar_tensor_tensor(t2[:], u[:, s], 2.0, u[:, s], ALU.add, ALU.mult))
                link(nc.vector.tensor_scalar(den[:], t2[:], 2.0, None, ALU.add))
                link(nc.vector.reciprocal(den[:], den[:]))
                link(nc.vector.tensor_tensor(t2[:], t2[:], z[:, s], ALU.mult))
                link(nc.vector.tensor_tensor(mish[:, s], t2[:], den[:], ALU.mult))
                link(nc.vector.tensor_tensor(mish[:, s], mish[:, s], n.wa[:].unsqueeze(1).broadcast_to([P, G, D]), ALU.mult))
                link(nc.vector.tensor_reduce(logit[:, s], mish[:, s], AX_X, ALU.add))
                nc.vector.tensor_scalar(logit[:, s], logit[:, s], n.wa_b[:, 0:1], None, ALU.add).then_inc(logits_made, 1)

            if kind == "sum":
                pipelined(dve, sort.vector(dve) + [(scan, 0), (finish, 1)])
            elif kind == "rel":
                pipelined(dve, [(mask, 0), (scan, 1), (finish, 2)])
            elif kind == "gat":
                pipelined(dve, [(tops, 1), (clamp, 0), (weigh, 1), (scan, 1), (logits, 0), (finish, 1)])
            else:
                pipelined(dve, [(hots, 0), (tops, 1), (weigh, 1), (scan, 1), (leaky, 0), (finish, 1)])


def order_parts(nc, n, k, sb, ps, sem):
    r = Net()
    table, cols, marks = (n.sorted_dst, n.cols_dst, n.marks_dst) if k == DST else (n.sorted_src, n.cols_src, n.marks_src)
    other, kind = (SRC, T16) if k == DST else (DST, T200)
    edges = [sb(f"edges{m}", [QA, 4, P, 4], I32) for m in range(3)]
    f = sb("fields", [QA, 6, 4, P])
    near = sb("near", [QA, 3, 4, P])
    turned = ps("order_turned", [P, 6, 512])

    loaded = sem("order_loaded")
    order_step = sem("order_step")
    fields_made = sem("fields_made")
    turns_made = sem("turns_made")

    def sync(sp):
        for m in range(3):
            view = table[m:m + PAD, :].rearrange("(q a c) f -> a q (c f)", q=4, c=P)
            sp.dma_start(edges[m][:].rearrange("a q c f -> a q (c f)"), view).then_inc(loaded, 16)

    def vector(dve):
        link = linker(dve, order_step, 0)
        dve.wait_ge(loaded, 48)
        for m in range(3):
            link(nc.vector.tensor_copy(near[:, m], edges[m][:, :, :, k]))
        link(nc.vector.tensor_copy(f[:, 0], edges[1][:, :, :, other]))
        link(nc.vector.tensor_copy(f[:, 1], near[:, 1]))
        link(nc.vector.tensor_tensor(f[:, 2], near[:, 1], near[:, 2], ALU.is_equal))
        link(nc.vector.scalar_tensor_tensor(f[:, 2], f[:, 2], float(SKIP), near[:, 1], ALU.mult, ALU.add))
        link(nc.vector.tensor_tensor(f[:, 3], near[:, 1], near[:, 0], ALU.is_equal))
        link(nc.vector.tensor_scalar(f[:, 4], f[:, 3], -NEG, NEG, ALU.mult, ALU.add))
        nc.vector.tensor_copy(f[:, 5], edges[1][:, :, :, kind]).then_inc(fields_made, 1)

    def tensor(pe):
        pe.wait_ge(fields_made, 1)
        for m in range(6):
            for q in range(4):
                mm = pe.transpose(turned[:, m, q * QA:(q + 1) * QA], f[:, m, q, :], n.ident[0:QA, 0:QA])
            mm.then_inc(turns_made, 1)

    def scalar(act):
        for m in range(6):
            act.wait_ge(turns_made, m + 1)
            to = cols[:, :, m, :] if m < 3 else marks[:, :, m - 3, :]
            nc.scalar.copy(to, turned[:, m, 0:TILES].rearrange("p (g c) -> p g c", c=G))

    r.sync, r.vector, r.tensor, r.scalar = sync, vector, tensor, scalar
    return r


def order_phase(nc, n, k, name):
    ctx, sb, ps, sem = phase(nc, name)
    with ctx:
        order = order_parts(nc, n, k, sb, ps, sem)
        block = ctx.enter_context(nc.Block())

        @block.sync
        def _(sp):
            order.sync(sp)

        @block.vector
        def _(dve):
            order.vector(dve)

        @block.tensor
        def _(pe):
            order.tensor(pe)

        @block.scalar
        def _(act):
            order.scalar(act)


def weights_parts(nc, n, w, sb, ps, sem):
    r = Net()
    A = D + 1
    raw = sb("raw", [D, 8, D])
    row = sb("row", [1, 2, D])
    col = sb("col", [D, 4])
    emb = sb("emb", [RH, 2, D])
    turned_s = sb("turned_s", [D, 4, D])
    emb_t = sb("emb_t", [D, 2, RH])
    v3 = sb("v3", [D, 1])
    vcat = sb("vcat", [P, 1])
    ra = sb("ra", [RH, 2])
    turned = ps("turned", [D, 4, D])
    emb_p = ps("emb_p", [D, 2, RH])
    prod = ps("prod", [P, D])
    bias = ps("bias", [P, D])
    rel = ps("rel", [RH, 2, D])
    vec = ps("vec", [P, 8])

    loaded = sem("loaded")
    weights_step = sem("weights_step")
    turns_made = sem("turns_made")
    turns_copied = sem("turns_copied")
    products_made = sem("products_made")
    v3_made = sem("v3_made")
    v3_copied = sem("v3_copied")
    last_made = sem("last_made")

    loads = [
        (raw[:, 0, :], w["L0_gnn_W"]), (raw[:, 1, :], w["L1_gnn_We_k"].rearrange("f h d -> f (h d)")),
        (raw[:, 2, :], w["L1_gnn_Ws_k"]), (raw[:, 3, :], w["L3_gnn_W_node"]),
        (raw[:, 4, :], w["L3_gnn_W_node"]), (raw[:, 5, :], w["L3_gnn_W_rel"]),
        (row[:, 0, :], w["L1_gnn_Ws_b"].unsqueeze(0)), (row[:, 1, :], w["L1_gnn_Wr_b"]),
        (emb[:], w["L3_gnn_rel_emb"].rearrange("(h p) d -> p h d", h=2)),
        (col[:, 0:1], w["L1_gnn_We_b"].rearrange("h d -> d h")),
        (n.score_w[D:P, :], w["L1_gnn_Wr_k"].rearrange("f h d -> f (h d)")),
        (n.edge_w[0:D, 0:D], w["L1_gnn_We_k"].rearrange("f h d -> f (h d)")),
        (n.edge_w[D:A, 0:D], w["L1_gnn_We_b"]),
        (n.wa[:], w["L1_gnn_Wa_k"].rearrange("d o -> o d").broadcast_to([P, D])),
        (n.wa_b[:], w["L1_gnn_Wa_b"].unsqueeze(0).broadcast_to([P, 1])),
        (n.bias0[:], w["L0_gnn_b"].unsqueeze(0).broadcast_to([P, D])),
    ]
    loads += [(col[:, 1 + c:2 + c], w["L3_gnn_attvec"][:, c * D:(c + 1) * D].rearrange("o d -> d o")) for c in range(3)]
    loads += [(n.rel_w[h * D:(h + 1) * D], w["L2_gnn_weight"].rearrange("(j h) k n -> h k j n", h=2)[h])
              for h in range(2)]

    def sync(sp):
        with nc.allow_non_contiguous_dma(reason="a few short vectors"):
            for to, of in loads:
                sp.dma_start(to, of).then_inc(loaded, 16)
        sp.wait_ge(loaded, 16 * len(loads))

    def tensor(pe):
        pe.wait_ge(loaded, 16 * len(loads))
        for m, r in enumerate((0, 1, 3, 5)):
            pe.transpose(turned[:, m, :], raw[:, r, :], n.ident[0:D, 0:D])
        for h in range(2):
            mm = pe.transpose(emb_p[:, h, :], emb[:, h, :], n.ident[0:RH, 0:RH])
        mm.then_inc(turns_made, 1)
        pe.matmul(vec[0:D, 0:1], lhsT=raw[:, 5, :], rhs=col[:, 3:4], start=True, stop=True).then_inc(v3_made, 1)
        pe.wait_ge(turns_copied, 1)
        pe.matmul(prod[0:D, :], lhsT=turned_s[:, 1, :], rhs=raw[:, 2, :], start=True, stop=True)
        pe.matmul(bias[:], lhsT=col[:, 0:1].broadcast_to([D, P]), rhs=raw[:, 2, :], start=True, stop=False)
        for r in range(2):
            pe.matmul(bias[:], lhsT=n.ones[0:1, 0:P], rhs=row[:, r, :], start=False, stop=(r == 1))
        for h in range(2):
            mm = pe.matmul(rel[:, h, :], lhsT=emb_t[:, h, :], rhs=turned_s[:, 3, :], start=True, stop=True)
        mm.then_inc(products_made, 1)
        pe.wait_ge(v3_copied, 1)
        pe.matmul(vec[:, 1:2], lhsT=raw[:, 3:5, :].rearrange("o c i -> o (c i)"), rhs=col[:, 2:3], start=True, stop=True)
        pe.matmul(vec[:, 2:3], lhsT=raw[:, 3:5, :].rearrange("o c i -> o (c i)"), rhs=col[:, 1:2], start=True, stop=True)
        for h in range(2):
            mm = pe.matmul(vec[0:RH, 3 + h:4 + h], lhsT=emb_t[:, h, :], rhs=v3[:], start=True, stop=True)
        mm.then_inc(last_made, 1)

    def vector(dve):
        link = linker(dve, weights_step, 0)
        dve.wait_ge(loaded, 16 * len(loads))
        link(nc.vector.memset(n.edge_w[:, D:A], 0.0))
        link(nc.vector.memset(n.edge_w[D:A, D:A], 1.0))
        link(nc.vector.memset(n.node_w[:], 0.0))
        link(nc.vector.memset(n.w0[:], 0.0))
        dve.wait_ge(turns_made, 1)
        link(nc.vector.tensor_copy(emb_t[:], emb_p[:]))
        link(nc.vector.tensor_copy(n.w0[0:D, 0:D], turned[:, 0, :]))
        link(nc.vector.tensor_copy(n.w0[D:P, D:P], turned[:, 0, :]))
        link(nc.vector.tensor_copy(n.node_w[0:D, :], turned[:, 2, :]))
        nc.vector.tensor_copy(turned_s[:], turned[:]).then_inc(turns_copied, 1)
        dve.wait_ge(v3_made, 1)
        nc.vector.tensor_copy(v3[:], vec[0:D, 0:1]).then_inc(v3_copied, 1)
        dve.wait_ge(products_made, 1)
        link(nc.vector.tensor_copy(n.score_w[0:D, :], prod[0:D, :]))
        link(nc.vector.tensor_copy(n.score_b[:], bias[:]))
        link(nc.vector.tensor_copy(n.rel_rows[:], rel[:]))
        dve.wait_ge(last_made, 1)
        link(nc.vector.tensor_copy(vcat[0:D, :], vec[0:D, 1:2]))
        link(nc.vector.tensor_copy(vcat[D:P, :], vec[D:P, 2:3]))
        link(nc.vector.tensor_copy(ra[:], vec[0:RH, 3:5]))
        link(nc.vector.tensor_copy(n.att_w[:], vcat[:].broadcast_to([P, A])))
        link(nc.vector.tensor_copy(n.att_rel[:], ra[:].unsqueeze(2).broadcast_to([RH, 2, A])))

    r.sync, r.tensor, r.vector = sync, tensor, vector
    return r


def norm_phase(nc, n, base, sums, to, scale, rows, name):
    SLOTS = 7
    ctx, sb, ps, sem = phase(nc, name)
    with ctx:
        order = order_parts(nc, n, SRC, sb, ps, sem) if scale is not None else None
        a = sb("a", [P, SLOTS, J, D])
        b = sb("b", [P, SLOTS, J, D])
        sq = sb("sq", [P, SLOTS, J, D])
        o = sb("o", [P, SLOTS, J, D])
        total = sb("total", [P, SLOTS, J])
        mean = sb("mean", [P, SLOTS, J])
        var = sb("var", [P, SLOTS, J])
        dev = sb("dev", [P, SLOTS, J])
        inv = sb("inv", [P, SLOTS, J])
        eps = sb("eps", [P, 1])

        rows_in = [sem(f"rows_in{s}") for s in range(SLOTS)]
        eps_set = sem("eps_set")
        added = sem("added")
        var_step = sem("var_step")
        inv_step = sem("inv_step")
        dve_step = sem("dve_step")
        centred = sem("centred")
        squared = sem("squared")
        var_made = sem("var_made")
        dev_made = sem("dev_made")
        inv_made = sem("inv_made")
        rows_made = sem("rows_made")
        rows_out = [sem(f"rows_out{s}") for s in range(SLOTS)]

        block = ctx.enter_context(nc.Block())
        by_part = lambda t: t.rearrange("(p g c) d -> p g (c d)", p=P, c=J)
        flat = lambda t: t.rearrange("p c d -> p (c d)")
        spread = lambda t: t.unsqueeze(2).broadcast_to([P, J, D])
        full = (N_NODES - (P - 1) * TILES) // J
        part = N_NODES - (P - 1) * TILES - full * J

        def chunks(stages):
            for step in range(NCH + max(lag for _, lag in stages)):
                for stage, lag in stages:
                    if 0 <= step - lag < NCH:
                        stage(step - lag, (step - lag) % SLOTS)

        def stores(c):
            each = [1 if rows == PAD or d > full or (d == full and not part) else 2 for d in range(c % SLOTS, c, SLOTS)]
            return sum(each)

        @block.sync
        def _(sp):
            def load(c, s):
                if c >= SLOTS:
                    sp.wait_ge(rows_made, c - SLOTS + 1)
                sp.dma_start(flat(a[:, s]), by_part(base)[:, c, :]).then_inc(rows_in[s], 16)
                sp.dma_start(flat(b[:, s]), by_part(sums)[:, c, :]).then_inc(rows_in[s], 16)

            chunks([(load, 0)])
            if order:
                order.sync(sp)

        @block.vector
        def _(dve):
            nc.vector.memset(eps[:], EPS).then_inc(eps_set, 1)

            def centre(c, s):
                dve.wait_ge(added, c + 1)
                if c >= SLOTS:
                    dve.wait_ge(var_made, c - SLOTS + 1)
                link = linker(dve, dve_step, 2 * c)
                link(nc.vector.tensor_reduce(total[:, s], a[:, s], AX_X, ALU.add))
                link(nc.vector.tensor_scalar(mean[:, s], total[:, s], 1.0 / D, None, ALU.mult))
                nc.vector.tensor_tensor(a[:, s], a[:, s], spread(mean[:, s]), ALU.subtract).then_inc(centred, 1)

            def variance(c, s):
                dve.wait_ge(squared, c + 1)
                if c >= SLOTS:
                    dve.wait_ge(dev_made, c - SLOTS + 1)
                ins = nc.vector.tensor_reduce(var[:, s], sq[:, s], AX_X, ALU.add)
                if scale is not None:
                    linker(dve, var_step, c)(ins)
                    ins = nc.vector.tensor_tensor(var[:, s], var[:, s], n.inv_deg[:, c * J:(c + 1) * J], ALU.mult)
                ins.then_inc(var_made, 1)

            def invert(c, s):
                dve.wait_ge(dev_made, c + 1)
                if c >= SLOTS:
                    dve.wait_ge(rows_made, c - SLOTS + 1)
                ins = nc.vector.reciprocal(inv[:, s], dev[:, s])
                if scale is not None:
                    linker(dve, inv_step, c)(ins)
                    ins = nc.vector.tensor_tensor(inv[:, s], inv[:, s], scale[:, c * J:(c + 1) * J], ALU.mult)
                ins.then_inc(inv_made, 1)

            chunks([(centre, 1), (variance, 2), (invert, 3)])
            if order:
                order.vector(dve)

        if order:
            @block.tensor
            def _(pe):
                order.tensor(pe)

        @block.scalar
        def _(act):
            act.wait_ge(eps_set, 1)

            def square(c, s):
                act.wait_ge(centred, c + 1)
                if c >= SLOTS:
                    act.wait_ge(var_made, c - SLOTS + 1)
                nc.scalar.activation(sq[:, s], a[:, s], ACT.Square).then_inc(squared, 1)

            def root(c, s):
                act.wait_ge(var_made, c + 1)
                if c >= SLOTS:
                    act.wait_ge(inv_made, c - SLOTS + 1)
                nc.scalar.activation(dev[:, s], var[:, s], ACT.Sqrt, bias=eps[:, 0:1], scale=1.0 / D).then_inc(dev_made, 1)

            def store(c, s):
                act.wait_ge(rows_made, c + 1)
                if rows == PAD:
                    act.dma_start(by_part(to)[:, c, :], flat(o[:, s])).then_inc(rows_out[s], 16)
                    return
                view = to[0:(P - 1) * TILES, :].rearrange("(p g c) d -> p g (c d)", p=P - 1, c=J)
                act.dma_start(view[:, c, :], flat(o[0:P - 1, s])).then_inc(rows_out[s], 16)
                left = J if c < full else part if c == full else 0
                if left:
                    first = (P - 1) * TILES + c * J
                    act.dma_start(to[first:first + left, :].rearrange("(o r) d -> o (r d)", o=1),
                                  flat(o[P - 1:P, s, 0:left])).then_inc(rows_out[s], 16)

            chunks([(square, 1), (root, 2), (store, 5)])
            if order:
                order.scalar(act)
            for c in range(NCH, NCH + SLOTS):
                act.wait_ge(rows_out[c % SLOTS], 16 * stores(c))

        @block.gpsimd
        def _(pool):
            def add(c, s):
                pool.wait_ge(rows_in[s], 32 * (c // SLOTS + 1))
                nc.gpsimd.tensor_tensor(a[:, s], a[:, s], b[:, s], ALU.add).then_inc(added, 1)

            def normalise(c, s):
                pool.wait_ge(inv_made, c + 1)
                if c >= SLOTS:
                    pool.wait_ge(rows_out[s], 16 * stores(c))
                nc.gpsimd.tensor_tensor(o[:, s], a[:, s], spread(inv[:, s]), ALU.mult).then_inc(rows_made, 1)

            chunks([(add, 0), (normalise, 4)])


def build(nc, x, edge_fields, w, out):
    n = Net()
    ctx = ExitStack()

    def dram(name, shape, dt=F32):
        return nc.dram_tensor(name, shape, dt, kind="Internal").ap()

    def sb(name, shape, dt=F32):
        return ctx.enter_context(nc.sbuf_tensor(name, shape, dt))

    with ctx:
        n.xpad = dram("xpad", [PAD, D])
        n.y = dram("y", [PAD, D])
        n.base0 = dram("base0", [PAD, D])
        n.x1 = dram("x1", [PAD, D])
        n.x2 = dram("x2", [PAD, D])
        n.x3 = dram("x3", [PAD, D])
        n.agg_dst = dram("agg_dst", [PAD, D])
        n.agg_src = dram("agg_src", [PAD, D])
        n.sorted_dst = dram("sorted_dst", [PAD + 2, 4], I32)
        n.sorted_src = dram("sorted_src", [PAD + 2, 4], I32)
        n.degree = dram("degree", [PAD])
        n.ident = sb("ident", [P, P])
        n.ident_b = sb("ident_b", [P, P], BF16)
        n.ones = sb("ones", [P, LO])
        n.part = sb("part", [P, 2])
        n.relid = sb("relid", [P, N_REL // 2])
        n.cols_dst = sb("cols_dst", [P, NG, 3, G], I32)
        n.cols_src = sb("cols_src", [P, NG, 3, G], I32)
        n.marks_dst = sb("marks_dst", [P, NG, 3, G], BF16)
        n.marks_src = sb("marks_src", [P, NG, 3, G], BF16)
        n.falls = sb("falls", [1, 1], I32)
        n.inv = sb("inv", [P, TILES])
        n.root = sb("root", [P, TILES])
        n.inv_deg = sb("inv_deg", [P, TILES])
        n.w0 = sb("w0", [P, P])
        n.bias0 = sb("bias0", [P, D])
        n.score_w = sb("score_w", [P, D])
        n.score_b = sb("score_b", [P, D])
        n.edge_w = sb("edge_w", [D + 1, D + 1])
        n.wa = sb("wa", [P, D])
        n.wa_b = sb("wa_b", [P, 1])
        n.rel_w = sb("rel_w", [P, N_REL // 2, D])
        n.node_w = sb("node_w", [P, D])
        n.att_w = sb("att_w", [P, D + 1])
        n.rel_rows = sb("rel_rows", [RH, 2, D])
        n.att_rel = sb("att_rel", [RH, 2, D + 1])
        with ExitStack() as sorting:
            def sb2(name, shape, dt=F32):
                return sorting.enter_context(nc.sbuf_tensor(name, shape, dt))
            n.payload = sb2("payload", [P, TILES, 4], I32)
            n.before = sb2("before", [P, E])
            n.lower = sb2("lower", [P, HH])
            n.iota_lo = sb2("iota_lo", [P, LO], BF16)
            n.digit = sb2("digit", [P, 2, 2, TILES])
            n.lo = sb2("lo", [P, 2, TILES], BF16)
            n.hi256 = sb2("hi256", [P, 2, TILES], BF16)
            n.keyf = sb2("keyf", [P, 2, TILES])
            n.start = sb2("start", [HH, 2, 2, LO])
            load_phase(nc, n, edge_fields)
            fill_phase(nc, n, x)
            prepare_phase(nc, n, w)
            sort_phase(nc, n)
            order_phase(nc, n, DST, "order_dst")
            edge_phase(nc, n, "sum", n.y, n.agg_dst, "edges0")
        norm_phase(nc, n, n.base0, n.agg_dst, n.x1, n.inv, PAD, "norm0")
        edge_phase(nc, n, "gat", n.x1, n.agg_dst, "edges1")
        norm_phase(nc, n, n.x1, n.agg_dst, n.x2, None, PAD, "norm1")
        edge_phase(nc, n, "rel", n.x2, n.agg_dst, "edges2")
        norm_phase(nc, n, n.x2, n.agg_dst, n.x3, None, PAD, "norm2")
        edge_phase(nc, n, "att", n.x3, n.agg_src, "edges3")
        norm_phase(nc, n, n.x3, n.agg_src, out, None, N_NODES, "norm3")


EDGE_INS = ["src", "dst", "edge_type_16", "edge_type_200"]
WEIGHT_INS = ["L0_gnn_W", "L0_gnn_b", "L1_gnn_We_k", "L1_gnn_We_b", "L1_gnn_Ws_k", "L1_gnn_Ws_b", "L1_gnn_Wr_k",
              "L1_gnn_Wr_b", "L1_gnn_Wa_k", "L1_gnn_Wa_b", "L2_gnn_weight", "L3_gnn_W_node", "L3_gnn_W_rel",
              "L3_gnn_attvec", "L3_gnn_rel_emb"]


def kernel(**inputs):
    import concourse.bacc as bacc
    from concourse.bass_utils import run_bass_kernel_spmd

    nc = bacc.Bacc("TRN2", target_bir_lowering=False, num_devices=1)
    arrays, aps = {}, {}
    for name in ["x"] + EDGE_INS + WEIGHT_INS:
        a = np.ascontiguousarray(inputs[name])
        arrays[f"in_{name}"] = a
        aps[name] = nc.dram_tensor(f"in_{name}", a.shape, mybir.dt.from_np(a.dtype), kind="ExternalInput").ap()
    out = nc.dram_tensor("out_x", [N_NODES, D], F32, kind="ExternalOutput").ap()
    build(nc, aps["x"], [aps[name] for name in EDGE_INS], {name: aps[name] for name in WEIGHT_INS}, out)
    ran = run_bass_kernel_spmd(nc, [arrays], core_ids=[0])
    return ran.results[0]["out_x"]
```
